# Optimizing a Trainium2 kernel written in Bass

```python
import numpy as np
import jax
import jax.numpy as jnp

def _softmax(x, axis=-1):
    return jax.nn.softmax(x, axis=axis)

def _gelu(x):
    return jax.nn.gelu(x, approximate=True)

def _silu(x):
    return jax.nn.silu(x)

def _sigmoid(x):
    return jax.nn.sigmoid(x)

def _layernorm(x, axis=-1, eps=1e-05):
    m = jnp.mean(x, axis=axis, keepdims=True)
    v = jnp.var(x, axis=axis, keepdims=True)
    return (x - m) / jnp.sqrt(v + eps)

def _scatter_add(tgt, idx, src, axis=0):
    return tgt.at[idx].add(src)

def _segment_sum(src, seg, n):
    return jax.ops.segment_sum(src, seg, n)
kernel_name = 'mk_seq_preln_d2_jaxref_r4_8171c0'

def setup_inputs(seed: int=0):
    np.random.seed(seed)
    _w = jnp.asarray

    def _L0_attn_setup():
        import jax, jax.numpy as jnp
        import numpy as np
        B, S, D, H = (2, 512, 256, 16)
        HD = D // H
        key = jax.random.key(seed)
        k0, k1, k2 = jax.random.split(key, 3)
        return {'x': jax.random.normal(k0, (B, S, D), jnp.float32), 'qkv_w': jax.random.normal(k1, (D, 3 * D), jnp.float32) / np.sqrt(D).astype(np.float32), 'qkv_b': jnp.zeros((3 * D,), jnp.float32), 'out_w': jax.random.normal(k2, (D, D), jnp.float32) / np.sqrt(D).astype(np.float32), 'out_b': jnp.zeros((D,), jnp.float32)}
    _L0_attn_in = _L0_attn_setup()

    def _L0_ffn_setup():
        import jax, jax.numpy as jnp
        import numpy as np
        EPS = 1e-08

        def _ternary_linear(x, w):
            alpha = jnp.mean(jnp.abs(w))
            w_t = jnp.sign(w) * (jnp.abs(w) > 0.5 * alpha).astype(w.dtype)
            w_q = w + jax.lax.stop_gradient(w_t - w)
            d = x.shape[-1]
            rms = jnp.sqrt(jnp.sum(x * x, axis=-1, keepdims=True)) / jnp.sqrt(jnp.asarray(d, x.dtype))
            x_norm = x / (rms + EPS)
            return jnp.einsum('bsd,fd->bsf', x_norm, w_q)
        key = jax.random.key(seed)
        k1, k2, k3 = jax.random.split(key, 3)
        d_model, d_ff = (256, 1024)
        B, S = (4, 1024)
        x = jax.random.normal(k1, (B, S, d_model), dtype=jnp.float32)
        w_up = jax.random.normal(k2, (d_ff, d_model), dtype=jnp.float32) * 0.02
        w_down = jax.random.normal(k3, (d_model, d_ff), dtype=jnp.float32) * 0.02
        return {'x': x, 'w_up': w_up, 'w_down': w_down}
    _L0_ffn_in = _L0_ffn_setup()

    def _L1_attn_setup():
        import jax, jax.numpy as jnp
        import numpy as np
        D_MODEL = 256
        D_STATE = 16
        BATCH = 2
        SEQ = 512
        key = jax.random.key(seed)
        k1, k2, k3, k4, k5 = jax.random.split(key, 5)
        x = jax.random.normal(k1, (BATCH, SEQ, D_MODEL), dtype=jnp.float32)
        log_A_diag = jax.random.normal(k2, (D_MODEL, D_STATE), dtype=jnp.float32)
        B_w = jax.random.normal(k3, (D_STATE, D_MODEL), dtype=jnp.float32) / np.sqrt(D_MODEL)
        C_w = jax.random.normal(k4, (D_MODEL, D_STATE), dtype=jnp.float32) / np.sqrt(D_STATE)
        D_vec = jax.random.normal(k5, (D_MODEL,), dtype=jnp.float32)
        return {'x': x, 'log_A_diag': log_A_diag, 'B_w': B_w, 'C_w': C_w, 'D_vec': D_vec}
    _L1_attn_in = _L1_attn_setup()

    def _L1_ffn_setup():
        import jax, jax.numpy as jnp
        import numpy as np
        B, S, D = (4, 512, 256)
        E = 8
        TOPK = 2
        I = 938

        def _swiglu(x, gate_up, down):
            h = jnp.einsum('bsd,fd->bsf', x, gate_up)
            g, u = jnp.split(h, 2, axis=-1)
            return jnp.einsum('bsi,di->bsd', jax.nn.silu(g) * u, down)
        key = jax.random.key(seed)
        ks = jax.random.split(key, 6)
        scale = 1.0 / np.sqrt(D)
        return {'hidden_states': jax.random.normal(ks[0], (B, S, D), dtype=jnp.float32), 'gate_weight': jax.random.normal(ks[1], (E, D), dtype=jnp.float32) * scale, 'shared_gate_up': jax.random.normal(ks[2], (2 * I, D), dtype=jnp.float32) * scale, 'shared_down': jax.random.normal(ks[3], (D, I), dtype=jnp.float32) * (1.0 / np.sqrt(I)), 'experts_gate_up': jax.random.normal(ks[4], (E, 2 * I, D), dtype=jnp.float32) * scale, 'experts_down': jax.random.normal(ks[5], (E, D, I), dtype=jnp.float32) * (1.0 / np.sqrt(I))}
    _L1_ffn_in = _L1_ffn_setup()
    _d = {'L0_attn_x': _L0_attn_in['x'], 'L0_attn_qkv_w': _L0_attn_in['qkv_w'], 'L0_attn_qkv_b': _L0_attn_in['qkv_b'], 'L0_attn_out_w': _L0_attn_in['out_w'], 'L0_attn_out_b': _L0_attn_in['out_b'], 'L0_ffn_w_up': _L0_ffn_in['w_up'], 'L0_ffn_w_down': _L0_ffn_in['w_down'], 'L1_attn_log_A_diag': _L1_attn_in['log_A_diag'], 'L1_attn_B_w': _L1_attn_in['B_w'], 'L1_attn_C_w': _L1_attn_in['C_w'], 'L1_attn_D_vec': _L1_attn_in['D_vec'], 'L1_ffn_gate_weight': _L1_ffn_in['gate_weight'], 'L1_ffn_shared_gate_up': _L1_ffn_in['shared_gate_up'], 'L1_ffn_shared_down': _L1_ffn_in['shared_down'], 'L1_ffn_experts_gate_up': _L1_ffn_in['experts_gate_up'], 'L1_ffn_experts_down': _L1_ffn_in['experts_down']}
    _x0 = _d['L0_attn_x']
    _d['L0_attn_x'] = jax.random.normal(jax.random.fold_in(jax.random.key(seed), 1), (2, 2048, 256), dtype=_x0.dtype)
    del _x0
    return _d

def reference(L0_attn_x, L0_attn_qkv_w, L0_attn_qkv_b, L0_attn_out_w, L0_attn_out_b, L0_ffn_w_up, L0_ffn_w_down, L1_attn_log_A_diag, L1_attn_B_w, L1_attn_C_w, L1_attn_D_vec, L1_ffn_gate_weight, L1_ffn_shared_gate_up, L1_ffn_shared_down, L1_ffn_experts_gate_up, L1_ffn_experts_down):

    def _L0_attn_ref(x, qkv_w, qkv_b, out_w, out_b):
        import jax, jax.numpy as jnp
        import numpy as np
        B, S, D, H = (2, 512, 256, 16)
        HD = D // H
        b, s, d = x.shape
        h, hd = (H, d // H)
        scale = 1.0 / np.sqrt(hd).astype(np.float32)
        qkv = (x @ qkv_w + qkv_b).reshape(b, s, 3, h, hd)
        q, k, v = (qkv[:, :, 0], qkv[:, :, 1], qkv[:, :, 2])
        logits = jnp.einsum('bqhd,bkhd->bhqk', q, k)
        causal_mask = jnp.triu(jnp.ones((s, s), bool), 1)
        logits = jnp.where(causal_mask, -jnp.inf, logits) * scale
        att = jax.nn.softmax(logits, axis=-1)
        out = jnp.einsum('bhqk,bkhd->bqhd', att, v).reshape(b, s, d)
        return out @ out_w + out_b

    def _L0_ffn_ref(x, w_up, w_down):
        import jax, jax.numpy as jnp
        import numpy as np
        EPS = 1e-08

        def _ternary_linear(x, w):
            alpha = jnp.mean(jnp.abs(w))
            w_t = jnp.sign(w) * (jnp.abs(w) > 0.5 * alpha).astype(w.dtype)
            w_q = w + jax.lax.stop_gradient(w_t - w)
            d = x.shape[-1]
            rms = jnp.sqrt(jnp.sum(x * x, axis=-1, keepdims=True)) / jnp.sqrt(jnp.asarray(d, x.dtype))
            x_norm = x / (rms + EPS)
            return jnp.einsum('bsd,fd->bsf', x_norm, w_q)
        h = jax.nn.gelu(_ternary_linear(x, w_up), approximate=False)
        return _ternary_linear(h, w_down)

    def _L1_attn_ref(x, log_A_diag, B_w, C_w, D_vec):
        import jax, jax.numpy as jnp
        import numpy as np
        D_MODEL = 256
        D_STATE = 16
        BATCH = 2
        SEQ = 512
        B, L, D = x.shape
        pad = 2 * L
        A_bar = jnp.exp(-jnp.exp(log_A_diag))
        B_t = jnp.einsum('bld,sd->bls', x, B_w)
        k_idx = jnp.arange(L, dtype=x.dtype)
        kernel = A_bar[..., None] ** k_idx
        kernel_fft = jnp.fft.rfft(kernel, n=pad, axis=-1)
        B_fft = jnp.fft.rfft(B_t.transpose(0, 2, 1), n=pad, axis=-1)
        conv_fft = kernel_fft[None] * B_fft[:, None]
        conv = jnp.fft.irfft(conv_fft, n=pad, axis=-1)[..., :L]
        y = jnp.einsum('bdsl,ds->bld', conv, C_w)
        y = y + D_vec[None, None, :] * x
        return y

    def _L1_ffn_ref(hidden_states, gate_weight, shared_gate_up, shared_down, experts_gate_up, experts_down):
        import jax, jax.numpy as jnp
        import numpy as np
        B, S, D = (4, 512, 256)
        E = 8
        TOPK = 2
        I = 938

        def _swiglu(x, gate_up, down):
            h = jnp.einsum('bsd,fd->bsf', x, gate_up)
            g, u = jnp.split(h, 2, axis=-1)
            return jnp.einsum('bsi,di->bsd', jax.nn.silu(g) * u, down)
        x = hidden_states
        out = _swiglu(x, shared_gate_up, shared_down)
        logits = jnp.einsum('bsd,ed->bse', x, gate_weight)
        probs = jax.nn.softmax(logits.astype(jnp.float32), axis=-1)
        top_p, sel = jax.lax.top_k(probs, TOPK)
        top_p = top_p / (jnp.sum(top_p, axis=-1, keepdims=True) + 1e-08)
        cw = jnp.sum(top_p[..., None] * jax.nn.one_hot(sel, E, dtype=top_p.dtype), axis=2)
        for e in range(E):
            y = _swiglu(x, experts_gate_up[e], experts_down[e])
            out = out + cw[..., e:e + 1] * y
        return out
    x = L0_attn_x
    x = x + _L0_attn_ref(_layernorm(x, axis=-1), L0_attn_qkv_w, L0_attn_qkv_b, L0_attn_out_w, L0_attn_out_b)
    x = x + _L0_ffn_ref(_layernorm(x, axis=-1), L0_ffn_w_up, L0_ffn_w_down)
    x = x + _L1_attn_ref(_layernorm(x, axis=-1), L1_attn_log_A_diag, L1_attn_B_w, L1_attn_C_w, L1_attn_D_vec)
    x = x + _L1_ffn_ref(_layernorm(x, axis=-1), L1_ffn_gate_weight, L1_ffn_shared_gate_up, L1_ffn_shared_down, L1_ffn_experts_gate_up, L1_ffn_experts_down)
    return x

_drawn_inputs = setup_inputs


def setup_inputs(seed=0):
    import zlib

    import numpy as np

    out = dict(_drawn_inputs(seed))
    spreads = {'L0_attn_qkv_b': (0.0, 0.1), 'L0_attn_out_b': (0.0, 0.1)}
    factors = {'L1_ffn_gate_weight': 4.057,
     'L1_ffn_experts_gate_up': 3.41,
     'L1_ffn_experts_down': 3.393,
     'L1_ffn_shared_gate_up': 3.324,
     'L1_ffn_shared_down': 3.327}
    for name, (base, spread) in spreads.items():
        noise = np.random.default_rng([zlib.crc32(name.encode()), seed]).standard_normal(out[name].shape)
        drawn = base * np.exp(spread * noise) if base else spread * noise
        out[name] = jnp.asarray(drawn.astype(out[name].dtype))
    for name, factor in factors.items():
        out[name] = (out[name] * factor).astype(out[name].dtype)
    return out
```

```python
from contextlib import ExitStack

import numpy as np

import concourse.bass as bass
from concourse import mybir

F32 = mybir.dt.float32
FR = mybir.dt.float32r
BF16 = mybir.dt.bfloat16
ALU = mybir.AluOpType
ACT = mybir.ActivationFunctionType
AX = mybir.AxisListType

P = 128
BATCH, SEQ, D = 2, 2048, 256
TOK = BATCH * SEQ
TILES = TOK // P
CT = 512
TPC = CT // P
CHUNKS = TOK // CT
KD = D // P
H, HD = 16, 16
EPS = 1e-5
MASKED = -1e30

C_IDENT = 0
C_MASK_QK = 128
C_MASK_KQ = 256
C_SEL = 512
SELW = 18
C_NEG_TAU = 536
C_TAU_MASK = 540
C_STEP = 572
C_SAME_S = 604
C_SAME_G = 620
C_UPPER = 628
C_LEFT = 756
C_LIMITS = 764
C_TILE = 772
C_END = 804


def host_constants():
    c = np.zeros((P, C_END), np.float32)
    i = np.arange(P)
    c[:, C_IDENT:C_IDENT + P] = np.eye(P)
    c[:, C_MASK_QK:C_MASK_QK + P] = np.where(i[None, :] > i[:, None], MASKED, 0)
    c[:, C_MASK_KQ:C_MASK_KQ + P] = MASKED
    c[:, C_MASK_KQ + P:C_MASK_KQ + 2 * P] = np.where(i[:, None] > i[None, :], MASKED, 0)
    for j in range(HD + 1):
        c[i % 32 == j, C_SEL + j] = 1
    tau, s = i // NSTATE, i % NSTATE
    m, r = np.arange(MT), np.arange(T)
    c[:, C_NEG_TAU:C_NEG_TAU + MT] = -(TAUS * m[None, :] + tau[:, None])
    c[:, C_TAU_MASK:C_TAU_MASK + T] = r[None, :] >= tau[:, None]
    c[:, C_STEP:C_STEP + T] = -(r[None, :] + 1)
    c[:, C_SAME_S:C_SAME_S + NSTATE] = s[:, None] == np.arange(NSTATE)[None, :]
    c[:, C_SAME_G:C_SAME_G + TAUS] = tau[:, None] == np.arange(TAUS)[None, :]
    c[:, C_UPPER:C_UPPER + P] = i[:, None] < i[None, :]
    c[:, C_LEFT:C_LEFT + E] = E - np.arange(E)
    c[:, C_LIMITS:C_LIMITS + CHUNKS] = np.arange(CHUNKS) * CT
    c[:, C_TILE:C_TILE + ROUTED] = np.arange(ROUTED)
    return c


E, TOPK = 8, 2
ROUTED = (TOPK * TOK + E * (CT - 1)) // CT
NSTATE = 16
TAUS = P // NSTATE
T = 32
MT = T // TAUS
BLOCKS = TOK // T
DB = D // TAUS


START = 1


class Semaphores:

    def __init__(self, nc, ctx):
        self.nc, self.ctx, self.new = nc, ctx, []

    def __call__(self, name):
        self.new.append(self.ctx.enter_context(self.nc.semaphore(name)))
        return self.new[-1]

    def from_zero(self, name):
        return self.ctx.enter_context(self.nc.semaphore(name))

    def start(self):
        new, self.new = self.new, []
        with self.nc.Block() as block:
            @block.sync
            def _(sp):
                for s in new:
                    sp.sem_inc(s, START)


class Steps:

    def __init__(self, eng, sem, base=0):
        self.eng, self.sem, self.base, self.n = eng, sem, base, 0

    def add(self, instruction):
        instruction.then_inc(self.sem, 1)
        self.n += 1

    def last(self):
        self.eng.wait_ge(self.sem, self.base + self.n + START)


def on_its_own(eng, g):
    eng.sem_inc(g.passed, 1)


def product3(pe, out, wh, wl, xh, xl, start, stop):
    pe.matmul(out, wh, xh, start=start, stop=False)
    pe.matmul(out, wh, xl, start=False, stop=False)
    return pe.matmul(out, wl, xh, start=False, stop=stop)


def ds(start, size):
    return bass.ds(start, size)


def phase_qkv(nc, top, g):
    with ExitStack() as ctx:
        sb = lambda name, shape, dt=F32: ctx.enter_context(nc.sbuf_tensor(name, shape, dt))
        pb = lambda name, shape, dt=F32: ctx.enter_context(nc.psum_tensor(name, shape, dt))
        sem = Semaphores(nc, ctx)
        NW = 3 * D
        w32 = sb("qkv_w32", [P, KD, NW])
        wh = sb("qkv_wh", [P, KD, NW], FR)
        wl = sb("qkv_wl", [P, KD, NW], FR)
        qk_bias = sb("qk_bias", [P, 4])
        v_bias = sb("v_bias", [P, D])
        stats = sb("qkv_stats", [P, TPC, 6])
        mv = sb("qkv_mv", [P, TPC, 2])
        sd = sb("qkv_sd", [P, TPC])
        rstd = sb("qkv_rstd", [P, TPC])
        xn = sb("qkv_xn", [P, TPC, D])
        xth = sb("qkv_xth", [P, KD, CT], FR)
        xtl = sb("qkv_xtl", [P, KD, CT], FR)
        qk32 = sb("qk32", [P, 4, CT])
        qkh = sb("qkh", [P, 4, CT], FR)
        qkl = sb("qkl", [P, 4, CT], FR)
        ps_t = pb("qkv_ps_t", [P, KD, CT])
        ps_qk = pb("ps_qk", [P, 2, CT])
        ps_v = pb("ps_v", [P, 2, CT])

        const_in = sem("const_in")
        w_in = sem("qkv_w_in")
        x_in = sem("x_in")
        w_hi = sem("qkv_w_hi")
        w_lo = sem("qkv_w_lo")
        const_bf = sem("const_bf")
        own = sem("qkv_dve_own")
        var_ready = sem("qkv_var_ready")
        sd_ready = sem("qkv_sd_ready")
        xn_ready = sem("qkv_xn_ready")
        xt_ready = sem("qkv_xt_ready")
        xt_hi = sem("qkv_xt_hi")
        xt_lo = sem("qkv_xt_lo")
        qk_ps = sem("qk_ps")
        qk_f32 = sem("qk_f32")
        qk_hi = sem("qk_hi")
        qk_lo = sem("qk_lo")
        v_ps = sem("v_ps")
        v_ready = sem("v_ready")
        qk_out = sem("qk_out")

        sem.start()
        with nc.Block() as block:
            @block.sync
            def _(sp):
                sp.dma_start(g.const[:, :], g.constants).then_inc(const_in, 16)
                sp.dma_start(w32[:, :, :], g.qkv_w.rearrange("(k p) n -> p k n", p=P)).then_inc(w_in, 16)
                sp.dma_start(qk_bias[:, :], g.qk_bias).then_inc(w_in, 16)
                sp.dma_start(v_bias[:, :], g.v_bias.rearrange("(o n) -> o n", o=1)
                             .broadcast_to([P, D])).then_inc(w_in, 16)
                with sp.Fori(0, CHUNKS) as it:
                    sp.wait_ge(x_in, it * 16 + START)
                    sp.dma_start(g.x[:, ds(it * TPC, TPC), :],
                                 g.x_in[ds(it * CT, CT), :].rearrange("(t p) n -> p t n", p=P)).then_inc(x_in, 16)
                with sp.Fori(0, CHUNKS) as it:
                    sp.wait_ge(qk_out, it * 32 + START)
                    sp.wait_ge(qk_hi, it * 4 + 4 + START)
                    sp.wait_ge(qk_lo, it * 4 + 4 + START)
                    sp.dma_start(g.q_k_hi[:, ds(it * CT, CT)].rearrange("(m p) t -> p m t", p=P),
                                 qkh[:, :, :].bitcast(F32)).then_inc(qk_out, 16)
                    sp.dma_start(g.q_k_lo[:, ds(it * CT, CT)].rearrange("(m p) t -> p m t", p=P),
                                 qkl[:, :, :].bitcast(F32)).then_inc(qk_out, 16)
                sp.wait_ge(qk_out, CHUNKS * 32 + START)

            @block.gpsimd
            def _(pool):
                pool.wait_ge(w_in, 48 + START)
                on_its_own(pool, g)
                pool.tensor_copy(wh[:, :, :], w32[:, :, :]).then_inc(w_hi, 1)
                with pool.Fori(0, CHUNKS) as it:
                    pool.wait_ge(qk_out, it * 32 + START)
                    for m in range(4):
                        pool.wait_ge(qk_f32, it * 4 + m + 1 + START)
                        on_its_own(pool, g)
                        pool.tensor_copy(qkh[:, m, :], qk32[:, m, :]).then_inc(qk_hi, 1)

            @block.vector
            def _(dve):
                dve.memset(g.eps[:, :], EPS).then_inc(g.started, 1)
                dve.wait_ge(const_in, 16 + START)
                dve.tensor_copy(g.ident_bf[:, :], g.const[:, C_IDENT:C_IDENT + P]).then_inc(const_bf, 1)
                dve.tensor_copy(g.mask_bf[:, :], g.const[:, C_MASK_QK:C_MASK_QK + 3 * P]).then_inc(const_bf, 1)
                dve.wait_ge(w_hi, 1 + START)
                dve.tensor_tensor(wl[:, :, :], w32[:, :, :], wh[:, :, :].bitcast(F32), ALU.subtract).then_inc(w_lo, 1)
                K = TPC + 1
                with dve.Fori(0, CHUNKS) as it:
                    dve.wait_ge(x_in, it * 16 + 16 + START)
                    steps = Steps(dve, own, it * K)
                    on_its_own(dve, g)
                    for j in range(TPC):
                        steps.add(dve.bn_stats(stats[:, j, :], g.x[:, ds(it * TPC + j, 1), :]))
                    steps.last()
                    on_its_own(dve, g)
                    for j in range(TPC):
                        last = dve.bn_aggr(mv[:, j, :], stats[:, j, :])
                    last.then_inc(var_ready, 1)
                    dve.wait_ge(sd_ready, it + 1 + START)
                    steps.add(dve.reciprocal(rstd[:, :], sd[:, :]))
                    steps.last()
                    dve.wait_ge(xt_ready, it + START)
                    for j in range(TPC):
                        last = dve.tensor_scalar(xn[:, j, :], g.x[:, ds(it * TPC + j, 1), :], mv[:, j, 0:1],
                                                 rstd[:, j:j + 1], ALU.subtract, ALU.mult)
                    last.then_inc(xn_ready, 1)
                    assert steps.n == K
                    dve.wait_ge(xt_hi, it + 1 + START)
                    dve.tensor_tensor(xtl[:, :, :], ps_t[:, :, :], xth[:, :, :].bitcast(F32), ALU.subtract)\
                       .then_inc(xt_lo, 1)
                    dve.wait_ge(qk_out, it * 32 + START)
                    for m in range(4):
                        dve.wait_ge(qk_hi, it * 4 + m + 1 + START)
                        dve.tensor_tensor(qkl[:, m, :], qk32[:, m, :], qkh[:, m, :].bitcast(F32), ALU.subtract)\
                           .then_inc(qk_lo, 1)
                    for j in range(TPC):
                        dve.wait_ge(v_ps, it * TPC + j + 1 + START)
                        dve.tensor_tensor(g.v[:, ds(it * TPC + j, 1), :], ps_v[:, j % 2, 0:D], v_bias[:, :], ALU.add)\
                           .then_inc(v_ready, 1)

            @block.scalar
            def _(act):
                act.wait_ge(g.started, 1)
                act.wait_ge(w_in, 48 + START)
                with act.Fori(0, CHUNKS) as it:
                    act.wait_ge(var_ready, it + 1 + START)
                    act.activation(sd[:, :], mv[:, :, 1], ACT.Sqrt, bias=g.eps[:, 0:1]).then_inc(sd_ready, 1)
                    act.wait_ge(xt_ready, it + 1 + START)
                    act.wait_ge(v_ps, it * TPC + START)
                    act.activation(xth[:, :, :], ps_t[:, :, :], ACT.Copy).then_inc(xt_hi, 1)
                    for m in range(4):
                        act.wait_ge(qk_ps, it * 4 + m + 1 + START)
                        act.wait_ge(qk_lo, it * 4 + START)
                        act.activation(qk32[:, m, :], ps_qk[:, m % 2, :], ACT.Identity, bias=qk_bias[:, m:m + 1])\
                           .then_inc(qk_f32, 1)

            @block.tensor
            def _(pe):
                pe.wait_ge(const_bf, 2 + START)
                pe.wait_ge(w_lo, 1 + START)
                with pe.Fori(0, CHUNKS) as it:
                    pe.wait_ge(xn_ready, it + 1 + START)
                    pe.wait_ge(xt_lo, it + START)
                    for k in range(KD):
                        for j in range(TPC):
                            last = pe.transpose(ps_t[:, k, j * P:(j + 1) * P], xn[:, j, k * P:(k + 1) * P],
                                                g.const[:, C_IDENT:C_IDENT + P])
                    last.then_inc(xt_ready, 1)
                    pe.wait_ge(xt_lo, it + 1 + START)
                    for m in range(4):
                        pe.wait_ge(qk_f32, it * 4 + max(m - 1, 0) + START)
                        for k in range(KD):
                            w = slice(m * P, (m + 1) * P)
                            last = product3(pe, ps_qk[:, m % 2, :], wh[:, k, w], wl[:, k, w], xth[:, k, :],
                                            xtl[:, k, :], k == 0, k == KD - 1)
                        last.then_inc(qk_ps, 1)
                    for j in range(TPC):
                        pe.wait_ge(v_ready, it * TPC + max(j - 1, 0) + START)
                        for k in range(KD):
                            t = slice(j * P, (j + 1) * P)
                            last = product3(pe, ps_v[:, j % 2, 0:D], xth[:, k, t], xtl[:, k, t],
                                            wh[:, k, 2 * D:], wl[:, k, 2 * D:], k == 0, k == KD - 1)
                        last.then_inc(v_ps, 1)


TILES_OF = [(c, kt, 0 if kt < c * TPC + 2 else CT // 2) for c in range(4) for kt in range((c + 1) * TPC)]
MAXES = [(i, c, min(CT, (i + 1) * P - c * CT)) for i in range(SEQ // P) for c in range(i // TPC + 1)]
NT = len(TILES_OF)
assert NT == len(MAXES) and NT % TPC == 0
GROUPS = NT // TPC
CHUNK_END = [(c + 1) * (c + 2) // 2 - 1 for c in range(4)]
CHUNK_MAX_AT = {CHUNK_END[c] + 1: c for c in range(4)}
TURN_AT = {3: 0, 4: 1, 7: 2, GROUPS: 3}
O_AT = {CHUNK_END[c] + 1: c for c in range(4)}
SUMS_AT = {5: 0, 6: 1, 8: 2, GROUPS + 1: 3}
NORMALISE_AT = 2
PER_MAX = 2
HEADS = BATCH * H
STACK = 3 * HD
MROW = 96
SCALE = HD ** -0.5


def batch_head(n):
    return n // H, n % H


def phase_attention(nc, top, g):
    with ExitStack() as ctx:
        sb = lambda name, shape, dt=F32: ctx.enter_context(nc.sbuf_tensor(name, shape, dt))
        pb = lambda name, shape, dt=F32: ctx.enter_context(nc.psum_tensor(name, shape, dt))
        sem = Semaphores(nc, ctx)
        q_st = [sb(f"q_stack{u}", [P, SEQ], FR) for u in range(3)]
        k_st = [sb(f"k_stack{u}", [P, SEQ], FR) for u in range(3)]
        v_st = [sb(f"v_stack{u}", [P, SEQ // P, 32]) for u in range(3)]
        probs = sb("probs", [P, 2 * TPC, CT])
        maxes = sb("maxes", [P, SEQ // P, 4])
        mx = sb("mx", [P, SEQ // P])
        mh = sb("mh", [TPC, 4, P], FR)
        ml = sb("ml", [TPC, 4, P], FR)
        o_sb = sb("o_sb", [P, 2, CT])
        rden = sb("rden", [P, SEQ // P, 1])
        ones = sb("att_ones", [1, SEQ])
        onesr = sb("att_onesr", [1, SEQ], FR)
        zeros = sb("att_zeros", [P, CT])
        ps_m = pb("ps_m", [P, 3, CT])
        ps_s = pb("ps_s", [P, 3, CT])
        ps_o = pb("ps_o", [P, CT])
        ps_f = pb("ps_f", [P, CT])
        fin = ps_f[:, 0:SEQ // P * SELW].rearrange("p (t w) -> p t w", w=SELW)
        turned = ps_f[0:TPC, 384:512]

        init = sem("att_init")
        ones_r = sem("att_ones_r")
        ones_in = sem("att_ones_in")
        stack_in = [sem(f"stack_in{u}") for u in range(3)]
        v_in = sem("att_v_in")
        mrow_in = [sem(f"mrow_in{c}") for c in range(4)]
        zeroed = sem("att_zeroed")
        zero_rows = sem("att_zero_rows")
        max_ps = sem("max_ps")
        max_used = sem("max_used")
        chunk_max = sem("chunk_max")
        own = sem("att_dve_own")
        m_turned = sem("m_turned")
        m_hi = sem("m_hi")
        m_lo = sem("m_lo")
        s_ps = sem("s_ps")
        p_ready = sem("p_ready")
        pv_done = sem("pv_done")
        o_copied = sem("o_copied")
        fin_ps = sem("fin_ps")
        fin_used = sem("fin_used")

        def upto(n, per, k):
            return max(n * per + k, 0) if isinstance(n, int) else n * per + k

        def load_stacks(sp, n, u, done):
            sp.wait_ge(s_ps, done * NT + START)
            b, h = batch_head(n)
            rows_q, rows_k = ds(h * HD, HD), ds(h * HD + D, HD)
            t = ds(b * SEQ, SEQ)
            for dst, src in ((q_st[u][0:HD, :], g.q_k_hi[rows_q, t]), (q_st[u][HD:2 * HD, :], g.q_k_hi[rows_q, t]),
                             (q_st[u][2 * HD:STACK, :], g.q_k_lo[rows_q, t]), (k_st[u][0:HD, :], g.q_k_hi[rows_k, t]),
                             (k_st[u][HD:2 * HD, :], g.q_k_lo[rows_k, t]), (k_st[u][2 * HD:STACK, :], g.q_k_hi[rows_k, t])):
                sp.dma_start(dst.bitcast(F32), src).then_inc(stack_in[u], 16)

        def load_mrow(sp, n, u, c):
            sp.wait_ge(m_lo, n * 4 + c + 1 + START)
            for r, part in ((MROW, mh), (MROW + 1, ml)):
                sp.dma_start(q_st[u][r:r + 1, c * CT:(c + 1) * CT].bitcast(F32).rearrange("o (t p) -> o t p", p=P),
                             part[:, c, :].bitcast(F32)).then_inc(mrow_in[c], 16)

        LOADS = 6 * 16
        TRIPLES = (HEADS - 2) // 3
        sem.start()
        with nc.Block() as block:
            @block.sync
            def _(sp):
                sp.wait_ge(zeroed, 6 + START)
                sp.wait_ge(ones_r, 1 + START)
                for u in range(3):
                    for r in (MROW, MROW + 1):
                        sp.dma_start(k_st[u][r:r + 1, :].bitcast(F32), onesr[0:1, :].bitcast(F32)).then_inc(ones_in, 16)
                load_stacks(sp, 0, 0, 0)
                load_stacks(sp, 1, 1, 0)

                def step(n, u, last=None, next_up=None, done=None):
                    if last is not None:
                        load_mrow(sp, last, (u + 2) % 3, 3)
                    if next_up is not None:
                        load_stacks(sp, next_up, (u + 1) % 3, done)
                    for c in range(3):
                        load_mrow(sp, n, u, c)
                step(0, 0)
                step(1, 1, 0, 2, 0)
                with sp.Fori(0, TRIPLES - 1) as i:
                    for v in range(3):
                        step(3 * i + v + 2, (v + 2) % 3, 3 * i + v + 1, 3 * i + v + 3, 3 * i + v + 1)
                for n in range(HEADS - 3, HEADS):
                    step(n, n % 3, n - 1, n + 1 if n + 1 < HEADS else None, n - 1)
                load_mrow(sp, HEADS - 1, (HEADS - 1) % 3, 3)
                for c in range(4):
                    sp.wait_ge(mrow_in[c], HEADS * 32 + START)

            @block.gpsimd
            def _(pool):
                for u in range(3):
                    pool.memset(v_st[u][:, :, :], 0.0).then_inc(init, 1)
                pool.wait_ge(init, 3 + START)
                for u in range(3):
                    pool.memset(v_st[u][:, :, HD:HD + 1], 1.0).then_inc(init, 1)

                def stage_v(n, u, done):
                    pool.wait_ge(pv_done, done * GROUPS + START)
                    on_its_own(pool, g)
                    b, h = batch_head(n)
                    pool.tensor_copy(v_st[u][:, :, 0:HD], g.v[:, ds(b * (SEQ // P), SEQ // P), ds(h * HD, HD)])\
                        .then_inc(v_in, 1)
                stage_v(0, 0, 0)
                stage_v(1, 1, 0)
                with pool.Fori(0, TRIPLES) as i:
                    for v in range(3):
                        stage_v(3 * i + v + 2, (v + 2) % 3, 3 * i + v)

            @block.vector
            def _(dve):
                dve.memset(zeros[:, :], 0.0).then_inc(zero_rows, 1)
                dve.memset(ones[:, :], 1.0).then_inc(own, 1)
                dve.memset(maxes[:, :, :], -3e38).then_inc(own, 1)
                dve.memset(ps_o[:, :], 0.0).then_inc(own, 1)
                dve.wait_ge(own, 3 + START)
                dve.tensor_copy(onesr[:, :], ones[:, :]).then_inc(ones_r, 1)
                dve.wait_ge(zero_rows, 1 + START)
                for st in (*q_st, *k_st):
                    dve.tensor_copy(st[:, :].rearrange("p (c t) -> p c t", t=CT),
                                    zeros[:, :].rearrange("p (o t) -> p o t", o=1).broadcast_to([P, SEQ // CT, CT]))\
                       .then_inc(zeroed, 1)

                def maximum(n, u, x):
                    i, c, w = MAXES[x]
                    dve.wait_ge(max_ps, n * NT + x + 1 + START)
                    dve.reduce_max(maxes[:, i, c:c + 1], ps_m[:, (u + x) % 3, 0:w], AX.X).then_inc(max_used, PER_MAX)

                def chunk(n, c):
                    dve.wait_ge(max_used, (n * NT + (CHUNK_END[c] + 1) * TPC) * PER_MAX + START)
                    dve.wait_ge(m_turned, upto(n, 4, c - 3) + START)
                    dve.reduce_max(mx[:, c * TPC:(c + 1) * TPC], maxes[:, c * TPC:(c + 1) * TPC, :], AX.X)\
                       .then_inc(chunk_max, 1)

                def low(n, c):
                    dve.wait_ge(m_hi, n * 4 + c + 1 + START)
                    dve.scalar_tensor_tensor(out=ml[:, c, :], in0=turned, scalar=-1.0, in1=mh[:, c, :].bitcast(F32),
                                             op0=ALU.mult, op1=ALU.subtract).then_inc(m_lo, 1)

                def reciprocals(n):
                    dve.wait_ge(fin_ps, n * 4 + 4 + START)
                    dve.reciprocal(rden[:, :, :], fin[:, :, HD:HD + 1]).then_inc(own, 1)

                def normalise(n):
                    dve.wait_ge(own, n + 4 + START)
                    b, h = batch_head(n)
                    dve.tensor_tensor(g.att[:, ds(b * (SEQ // P), SEQ // P), ds(h * HD, HD)], fin[:, :, 0:HD],
                                      rden[:, :, :].broadcast_to([P, SEQ // P, HD]), ALU.mult).then_inc(fin_used, 1)

                def step(n, u, last=None, before_last=None):
                    for q in range(GROUPS):
                        for r in range(TPC):
                            if n is not None:
                                maximum(n, u, q * TPC + r)
                            if r == 0 and q == 0 and last is not None:
                                chunk(last, 3)
                            if r == 0 and q in CHUNK_MAX_AT and n is not None:
                                chunk(n, CHUNK_MAX_AT[q])
                            if r == 1 and q == NORMALISE_AT and before_last is not None:
                                reciprocals(before_last)
                        if q == NORMALISE_AT and before_last is not None:
                            normalise(before_last)
                        if q == 0 and last is not None:
                            low(last, 3)
                        if q in TURN_AT and n is not None:
                            low(n, TURN_AT[q])
                step(0, 0)
                step(1, 1, 0)
                with dve.Fori(0, TRIPLES) as i:
                    for v in range(3):
                        step(3 * i + v + 2, (v + 2) % 3, 3 * i + v + 1, 3 * i + v)
                step(None, HEADS % 3, HEADS - 1, HEADS - 2)
                reciprocals(HEADS - 1)
                normalise(HEADS - 1)

            @block.scalar
            def _(act):
                def high(n, c):
                    act.wait_ge(m_turned, n * 4 + c + 1 + START)
                    act.wait_ge(mrow_in[c], n * 32 + START)
                    act.activation(mh[:, c, :], turned, ACT.Copy, scale=-1.0).then_inc(m_hi, 1)

                def exp(n, u, t):
                    c, kt, q0 = TILES_OF[t]
                    act.wait_ge(s_ps, n * NT + t + 1 + START)
                    act.wait_ge(pv_done, upto(n, GROUPS, t // TPC - 1) + START)
                    act.activation(probs[:, t % (2 * TPC), q0:], ps_s[:, (u + t) % 3, q0:], ACT.Exp, scale=SCALE)\
                       .then_inc(p_ready, 1)

                def copy_o(n, c):
                    act.wait_ge(pv_done, n * GROUPS + CHUNK_END[c] + 1 + START)
                    act.wait_ge(fin_ps, upto(n, 4, c - 1) + START)
                    act.activation(o_sb[:, c % 2, :], ps_o[:, :], ACT.Copy).then_inc(o_copied, 1)

                def step(n, u, last, before_last=None):
                    for q in range(GROUPS):
                        if last is not None:
                            for t in range(q * TPC, (q + 1) * TPC):
                                exp(last, (u + 2) % 3, t)
                        if q == 0 and before_last is not None:
                            copy_o(before_last, 3)
                        if q in O_AT and last is not None:
                            copy_o(last, O_AT[q])
                        if q == 0 and last is not None:
                            high(last, 3)
                        if q in TURN_AT and n is not None:
                            high(n, TURN_AT[q])
                act.wait_ge(init, 6 + START)
                step(0, 0, None)
                step(1, 1, 0)
                with act.Fori(0, TRIPLES) as i:
                    for v in range(3):
                        step(3 * i + v + 2, (v + 2) % 3, 3 * i + v + 1, 3 * i + v)
                step(None, HEADS % 3, HEADS - 1, HEADS - 2)
                copy_o(HEADS - 1, 3)

            @block.tensor
            def _(pe):
                pe.wait_ge(ones_in, 6 * 16 + START)
                pe.wait_ge(init, 6 + START)
                pe.wait_ge(own, 3 + START)
                pe.wait_ge(zeroed, 6 + START)

                def scores_for_max(n, u, x):
                    i, c, w = MAXES[x]
                    diagonal = (i + 1) * P == c * CT + w
                    pe.wait_ge(max_used, upto(n, NT * PER_MAX, (x - 2) * PER_MAX) + START)
                    mm = pe.matmul(ps_m[:, (u + x) % 3, 0:w], q_st[u][0:MROW, i * P:(i + 1) * P],
                                   k_st[u][0:MROW, c * CT:c * CT + w], start=True, stop=not diagonal)
                    if diagonal:
                        mm = pe.matmul(ps_m[:, (u + x) % 3, w - P:w], g.ident_bf[:, :], g.mask_bf[:, 0:P],
                                       start=False, stop=True)
                    mm.then_inc(max_ps, 1)

                def turn(n, c, normalised):
                    pe.wait_ge(chunk_max, n * 4 + c + 1 + START)
                    pe.wait_ge(m_lo, n * 4 + c + START)
                    pe.wait_ge(fin_used, normalised + START)
                    pe.transpose(turned, mx[:, c * TPC:(c + 1) * TPC], g.const[:, C_IDENT:C_IDENT + P])\
                      .then_inc(m_turned, 1)

                def scores(n, u, t):
                    c, kt, q0 = TILES_OF[t]
                    out, diag = ps_s[:, (u + t) % 3], kt - c * TPC
                    pe.wait_ge(mrow_in[c], n * 32 + 32 + START)
                    pe.wait_ge(p_ready, upto(n, NT, t - 2) + START)
                    mm = pe.matmul(out[:, q0:], k_st[u][:, kt * P:(kt + 1) * P], q_st[u][:, c * CT + q0:(c + 1) * CT],
                                   start=True, stop=diag < 0)
                    if diag >= 0:
                        w = P * (1 + diag % 2)
                        mm = pe.matmul(out[:, q0:q0 + w], g.ident_bf[:, :], g.mask_bf[:, 3 * P - w:3 * P],
                                       start=False, stop=True)
                    mm.then_inc(s_ps, 1)

                def times_v(n, u, q):
                    pe.wait_ge(p_ready, n * NT + (q + 1) * TPC + START)
                    if TILES_OF[q * TPC][1] == 0:
                        pe.wait_ge(o_copied, n * 4 + TILES_OF[q * TPC][0] + START)
                    for t in range(q * TPC, (q + 1) * TPC):
                        c, kt, q0 = TILES_OF[t]
                        r = 32 * (kt % TPC)
                        mm = pe.matmul(ps_o[r:r + 32, q0:], v_st[u][:, kt, :], probs[:, t % (2 * TPC), q0:],
                                       start=kt < TPC, stop=kt >= c * TPC, tile_position=(0, r))
                    mm.then_inc(pv_done, 1)

                def sums(n, c, turned_read):
                    pe.wait_ge(o_copied, n * 4 + c + 1 + START)
                    pe.wait_ge(m_lo, turned_read + START)
                    if c == 0:
                        pe.wait_ge(fin_used, n + START)
                    for j in range(TPC):
                        rows = P // 2 if c == 0 and j < 2 else P
                        mm = pe.matmul(fin[:, c * TPC + j, :], o_sb[0:rows, c % 2, j * P:(j + 1) * P],
                                       g.const[0:rows, C_SEL:C_SEL + SELW], start=True, stop=True)
                    mm.then_inc(fin_ps, 1)

                def step(n, u, last, before_last=None, nth=0):
                    if n is not None:
                        pe.wait_ge(stack_in[u], (nth + 1) * LOADS + START)
                    if last is not None:
                        pe.wait_ge(v_in, last + 1 + START)
                    for q in range(GROUPS):
                        for r in range(TPC):
                            if r == TPC - 1 and q and last is not None:
                                times_v(last, (u + 2) % 3, q - 1)
                            if r == TPC - 1 and q == 0 and before_last is not None:
                                times_v(before_last, (u + 1) % 3, GROUPS - 1)
                            if last is not None:
                                scores(last, (u + 2) % 3, q * TPC + r)
                            if n is not None:
                                scores_for_max(n, u, q * TPC + r)
                        if q == 0 and last is not None:
                            turn(last, 3, 0 if before_last is None else before_last)
                        if q in TURN_AT and n is not None:
                            turn(n, TURN_AT[q], 0 if before_last is None else before_last + 1)
                        new = sum(at <= q for at in TURN_AT)
                        read = (lambda k: k * 4 + new) if n is not None else (lambda k: HEADS * 4)
                        if q + GROUPS in SUMS_AT and before_last is not None:
                            sums(before_last, SUMS_AT[q + GROUPS], read(n))
                        if q in SUMS_AT and last is not None:
                            sums(last, SUMS_AT[q], read(n))
                step(0, 0, None)
                step(1, 1, 0)
                with pe.Fori(0, TRIPLES) as i:
                    for v in range(3):
                        step(3 * i + v + 2, (v + 2) % 3, 3 * i + v + 1, 3 * i + v, i + (v + 2) // 3)
                step(None, HEADS % 3, HEADS - 1, HEADS - 2)
                times_v(HEADS - 1, (HEADS - 1) % 3, GROUPS - 1)
                sums(HEADS - 1, 3, HEADS * 4)


FF = 1024
KF = FF // P


def phase_ffn(nc, top, g):
    with ExitStack() as ctx:
        sb = lambda name, shape, dt=F32: ctx.enter_context(nc.sbuf_tensor(name, shape, dt))
        pb = lambda name, shape, dt=F32: ctx.enter_context(nc.psum_tensor(name, shape, dt))
        sem = Semaphores(nc, ctx)
        ow32 = sb("ow32", [P, KD, D])
        owh = sb("owh", [P, KD, D], FR)
        owl = sb("owl", [P, KD, D], FR)
        ob = sb("ob", [P, D])
        hf = sb("ffn_h", [P, KF, CT])
        raw = hf[:, :, :].rearrange("p k n -> p (k n)")
        up32 = raw[:, 0:KD * FF].rearrange("p (k n) -> p k n", n=FF)
        dn32 = raw[:, KD * FF:KD * FF + KF * D].rearrange("p (k n) -> p k n", n=D)
        up = sb("up_ternary", [P, KD, FF], FR)
        dn = sb("dn_ternary", [P, KF, D], FR)
        absum = sb("absum", [P, 2])
        alpha = sb("alpha", [P, 2])
        alpha_neg = sb("alpha_neg", [P, 2])
        below = sb("below", [P, KD * FF])
        att_st = sb("att_st", [P, TPC, D])
        ones = sb("ffn_ones", [P, P])
        stats = sb("ffn_stats", [P, TPC, 6])
        mv = sb("ffn_mv", [P, TPC, 2])
        sd = sb("ffn_sd", [P, TPC])
        rstd = sb("ffn_rstd", [P, TPC])
        xn = sb("ffn_xn", [P, TPC, D])
        sq = sb("ffn_sq", [P, D])
        ss = sb("ffn_ss", [P, TPC])
        rms = sb("ffn_rms", [P, TPC])
        rr = sb("ffn_rr", [P, TPC])
        hrms = sb("ffn_hrms", [P, TPC])
        hrr = sb("ffn_hrr", [P, TPC])
        th = sb("ffn_th", [P, KD, CT], FR)
        tl = sb("ffn_tl", [P, KD, CT], FR)
        hh = sb("ffn_hh", [P, KF, CT], FR)
        hl = sb("ffn_hl", [P, KF, CT], FR)
        ps_t = pb("ffn_ps_t", [P, KD, CT])
        ps_y = pb("ffn_ps_y", [P, TPC, D])
        ps_u = pb("ffn_ps_u", [P, 2, CT])
        ps_r = pb("ffn_ps_r", [P, CT])

        w_in = sem("ffn_w_in")
        setup = sem("ffn_setup")
        w_hi = sem("ffn_w_hi")
        al_ps = sem("alpha_ps")
        own = sem("ffn_dve_own")
        att_staged = sem("att_staged")
        at_ready = sem("at_transposed")
        at_hi = sem("at_hi")
        at_lo = sem("at_lo")
        y_ps = sem("proj_ps")
        var_ready = sem("ffn_var_ready")
        sd_ready = sem("ffn_sd_ready")
        sq_ready = sem("ffn_sq_ready")
        ln_ready = sem("ffn_ln_ready")
        rms_ready = sem("ffn_rms_ready")
        xn_ready = sem("ffn_xn_ready")
        xt_ready = sem("ffn_xt_ready")
        xt_hi = sem("ffn_xt_hi")
        xt_lo = sem("ffn_xt_lo")
        u_ps = sem("up_ps")
        h_ready = sem("h_ready")
        h_hi = sem("h_hi")
        h_lo = sem("h_lo")
        h_sq = sem("h_sq")
        r_ps = sem("h_sumsq_ps")
        hrms_ready = sem("hrms_ready")
        dn_ps = sem("dn_ps")
        x_done = sem("ffn_x_done")

        sem.start()
        with nc.Block() as block:
            @block.sync
            def _(sp):
                sp.dma_start(ow32[:, :, :], g.out_w.rearrange("(k p) n -> p k n", p=P)).then_inc(w_in, 16)
                sp.dma_start(up32[:, :, :], g.up_t.rearrange("(k p) n -> p k n", p=P)).then_inc(w_in, 16)
                sp.dma_start(dn32[:, :, :], g.down_t.rearrange("(k p) n -> p k n", p=P)).then_inc(w_in, 16)
                sp.dma_start(ob[:, :], g.out_b.rearrange("(o n) -> o n", o=1).broadcast_to([P, D])).then_inc(w_in, 16)

            @block.gpsimd
            def _(pool):
                pool.memset(ones[:, :], 1.0).then_inc(w_hi, 1)
                pool.wait_ge(w_in, 64 + START)
                on_its_own(pool, g)
                pool.tensor_copy(owh[:, :, :], ow32[:, :, :]).then_inc(w_hi, 1)
                with pool.Fori(0, CHUNKS) as it:
                    pool.wait_ge(at_ready, it + START)
                    on_its_own(pool, g)
                    pool.tensor_copy(att_st[:, :, :], g.att[:, ds(it * TPC, TPC), :]).then_inc(att_staged, 1)
                    for m in range(KF):
                        pool.wait_ge(h_ready, it * KF + m + 1 + START)
                        pool.wait_ge(dn_ps, it * TPC + START)
                        on_its_own(pool, g)
                        pool.tensor_copy(hh[:, m, :], hf[:, m, :]).then_inc(h_hi, 1)
                        pool.wait_ge(h_lo, it * KF + m + 1 + START)
                        pool.tensor_tensor(hf[:, m, :], hf[:, m, :], hf[:, m, :], ALU.mult).then_inc(h_sq, 1)

            @block.vector
            def _(dve):
                dve.wait_ge(w_in, 64 + START)
                s = Steps(dve, setup)
                s.add(dve.tensor_reduce(absum[:, 0:1], up32[:, :, :], AX.XY, ALU.add, apply_absolute_value=True))
                s.add(dve.tensor_reduce(absum[:, 1:2], dn32[:, :, :], AX.XY, ALU.add, apply_absolute_value=True))
                dve.wait_ge(al_ps, 1 + START)
                s.add(dve.tensor_scalar(alpha[:, :], ps_r[:, 0:2], 1.0 / (D * FF), 0.5, ALU.mult, ALU.mult))
                s.last()
                s.add(dve.tensor_scalar(alpha_neg[:, :], alpha[:, :], -1.0, None, ALU.mult))
                s.last()
                for i, (src, dst) in enumerate(((up32, up), (dn32, dn))):
                    t = below[:, :].rearrange("p (k n) -> p k n", n=src.shape[2])
                    s.add(dve.tensor_scalar(t, src[:, :, :], alpha_neg[:, i:i + 1], None, ALU.is_lt))
                    s.last()
                    s.add(dve.scalar_tensor_tensor(out=dst[:, :, :], in0=src[:, :, :], scalar=alpha[:, i:i + 1],
                                                   in1=t, op0=ALU.is_gt, op1=ALU.subtract))
                    s.last()
                dve.wait_ge(w_hi, 2 + START)
                s.add(dve.tensor_tensor(owl[:, :, :], ow32[:, :, :], owh[:, :, :].bitcast(F32), ALU.subtract))
                assert s.n == FFN_SETUP
                K = 2 + TPC + 1 + 2 + 2
                with dve.Fori(0, CHUNKS) as it:
                    st = Steps(dve, own, it * K)
                    xs = g.x[:, ds(it * TPC, TPC), :]
                    dve.wait_ge(at_hi, it + 1 + START)
                    dve.tensor_tensor(tl[:, :, :], ps_t[:, :, :], th[:, :, :].bitcast(F32), ALU.subtract)\
                       .then_inc(at_lo, 1)
                    dve.wait_ge(y_ps, it + 1 + START)
                    st.add(dve.tensor_tensor(xs, xs, ps_y[:, :, :], ALU.add))
                    st.last()
                    st.add(dve.tensor_tensor(xs, xs, ob[:, :].rearrange("p (o n) -> p o n", o=1)
                                             .broadcast_to([P, TPC, D]), ALU.add))
                    st.last()
                    on_its_own(dve, g)
                    for j in range(TPC):
                        st.add(dve.bn_stats(stats[:, j, :], g.x[:, ds(it * TPC + j, 1), :]))
                    st.last()
                    on_its_own(dve, g)
                    for j in range(TPC):
                        last = dve.bn_aggr(mv[:, j, :], stats[:, j, :])
                    last.then_inc(var_ready, 1)
                    dve.wait_ge(sd_ready, it + 1 + START)
                    st.add(dve.reciprocal(rstd[:, :], sd[:, :]))
                    st.last()
                    for j in range(TPC):
                        last = dve.tensor_scalar(xn[:, j, :], g.x[:, ds(it * TPC + j, 1), :], mv[:, j, 0:1],
                                                 rstd[:, j:j + 1], ALU.subtract, ALU.mult)
                    last.then_inc(ln_ready, 1)
                    dve.wait_ge(rms_ready, it + 1 + START)
                    st.add(dve.tensor_scalar(rr[:, :], rms[:, :], 1e-8, None, ALU.add))
                    st.last()
                    st.add(dve.reciprocal(rr[:, :], rr[:, :]))
                    st.last()
                    for j in range(TPC):
                        last = dve.tensor_scalar(xn[:, j, :], xn[:, j, :], rr[:, j:j + 1], None, ALU.mult)
                    last.then_inc(xn_ready, 1)
                    dve.wait_ge(xt_hi, it + 1 + START)
                    dve.tensor_tensor(tl[:, :, :], ps_t[:, :, :], th[:, :, :].bitcast(F32), ALU.subtract)\
                       .then_inc(xt_lo, 1)
                    dve.wait_ge(dn_ps, it * TPC + START)
                    for m in range(KF):
                        dve.wait_ge(h_hi, it * KF + m + 1 + START)
                        dve.tensor_tensor(hl[:, m, :], hf[:, m, :], hh[:, m, :].bitcast(F32), ALU.subtract)\
                           .then_inc(h_lo, 1)
                    dve.wait_ge(hrms_ready, it + 1 + START)
                    st.add(dve.tensor_scalar(hrr[:, :], hrms[:, :], 1e-8, None, ALU.add))
                    st.last()
                    st.add(dve.reciprocal(hrr[:, :], hrr[:, :]))
                    st.last()
                    for j in range(TPC):
                        xj = g.x[:, ds(it * TPC + j, 1), :]
                        dve.wait_ge(dn_ps, it * TPC + j // 2 * 2 + 2 + START)
                        dve.scalar_tensor_tensor(out=xj, in0=ps_y[:, j:j + 1, :], scalar=hrr[:, j:j + 1], in1=xj,
                                                 op0=ALU.mult, op1=ALU.add).then_inc(x_done, 1)
                    assert st.n == K

            @block.scalar
            def _(act):
                act.wait_ge(w_hi, 1 + START)
                with act.Fori(0, CHUNKS) as it:
                    act.wait_ge(at_ready, it + 1 + START)
                    act.wait_ge(u_ps, it * KF + START)
                    act.activation(th[:, :, :], ps_t[:, :, :], ACT.Copy).then_inc(at_hi, 1)
                    act.wait_ge(var_ready, it + 1 + START)
                    act.activation(sd[:, :], mv[:, :, 1], ACT.Sqrt, bias=g.eps[:, 0:1]).then_inc(sd_ready, 1)
                    act.wait_ge(ln_ready, it + 1 + START)
                    for j in range(TPC):
                        if j:
                            act.wait_ge(sq_ready, it * TPC + j + START)
                        else:
                            act.wait_ge(sq_ready, it * TPC + START)
                        act.activation(sq[:, :], xn[:, j, :], ACT.Square, accum_out=ss[:, j:j + 1]).then_inc(sq_ready, 1)
                    act.wait_ge(sq_ready, it * TPC + TPC + START)
                    act.activation(rms[:, :], ss[:, :], ACT.Sqrt, scale=1.0 / D).then_inc(rms_ready, 1)
                    act.wait_ge(xt_ready, it + 1 + START)
                    act.wait_ge(y_ps, it + 1 + START)
                    act.activation(th[:, :, :], ps_t[:, :, :], ACT.Copy).then_inc(xt_hi, 1)
                    for m in range(KF):
                        act.wait_ge(u_ps, it * KF + m + 1 + START)
                        act.wait_ge(r_ps, it + START)
                        act.activation(hf[:, m, :], ps_u[:, m % 2, :], ACT.Gelu).then_inc(h_ready, 1)
                    act.wait_ge(r_ps, it + 1 + START)
                    act.activation(hrms[:, :], ps_r[:, 0:TPC], ACT.Sqrt, scale=1.0 / FF).then_inc(hrms_ready, 1)

            @block.tensor
            def _(pe):
                pe.wait_ge(w_hi, 1 + START)
                pe.wait_ge(setup, 2 + START)
                pe.matmul(ps_r[:, 0:2], ones[:, :], absum[:, :], start=True, stop=True).then_inc(al_ps, 1)
                pe.wait_ge(setup, FFN_SETUP + START)
                ident = g.const[:, C_IDENT:C_IDENT + P]
                with pe.Fori(0, CHUNKS) as it:
                    pe.wait_ge(att_staged, it + 1 + START)
                    pe.wait_ge(xt_lo, it + START)
                    for k in range(KD):
                        for j in range(TPC):
                            last = pe.transpose(ps_t[:, k, j * P:(j + 1) * P], att_st[:, j, k * P:(k + 1) * P], ident)
                    last.then_inc(at_ready, 1)
                    pe.wait_ge(at_lo, it + 1 + START)
                    pe.wait_ge(x_done, it * TPC + START)
                    for j in range(TPC):
                        for k in range(KD):
                            t = slice(j * P, (j + 1) * P)
                            last = product3(pe, ps_y[:, j, :], th[:, k, t], tl[:, k, t], owh[:, k, :], owl[:, k, :],
                                            k == 0, k == KD - 1)
                    last.then_inc(y_ps, 1)
                    pe.wait_ge(xn_ready, it + 1 + START)
                    for k in range(KD):
                        for j in range(TPC):
                            last = pe.transpose(ps_t[:, k, j * P:(j + 1) * P], xn[:, j, k * P:(k + 1) * P], ident)
                    last.then_inc(xt_ready, 1)
                    pe.wait_ge(xt_lo, it + 1 + START)
                    for m in range(KF):
                        pe.wait_ge(h_ready, it * KF + max(m - 1, 0) + START)
                        w = slice(m * P, (m + 1) * P)
                        for k in range(KD):
                            pe.matmul(ps_u[:, m % 2, :], up[:, k, w], th[:, k, :], start=k == 0, stop=False)
                            last = pe.matmul(ps_u[:, m % 2, :], up[:, k, w], tl[:, k, :], start=False, stop=k == KD - 1)
                        last.then_inc(u_ps, 1)
                    pe.wait_ge(h_lo, it * KF + KF + START)
                    for j in range(TPC):
                        t = slice(j * P, (j + 1) * P)
                        for m in range(KF):
                            pe.matmul(ps_y[:, j, :], hh[:, m, t], dn[:, m, :], start=m == 0, stop=False)
                            last = pe.matmul(ps_y[:, j, :], hl[:, m, t], dn[:, m, :], start=False, stop=m == KF - 1)
                        last.then_inc(dn_ps, 1)
                    pe.wait_ge(h_sq, it * KF + KF + START)
                    pe.wait_ge(hrms_ready, it + START)
                    for j in range(TPC):
                        for m in range(KF):
                            last = pe.matmul(ps_r[:, j:j + 1], hf[:, m, j * P:(j + 1) * P], ones[:, 0:1],
                                             start=m == 0, stop=m == KF - 1)
                    last.then_inc(r_ps, 1)


FFN_SETUP = 9


def phase_ssm(nc, top, g):
    with ExitStack() as ctx:
        sb = lambda name, shape, dt=F32: ctx.enter_context(nc.sbuf_tensor(name, shape, dt))
        pb = lambda name, shape, dt=F32: ctx.enter_context(nc.psum_tensor(name, shape, dt))
        sem = Semaphores(nc, ctx)
        rate8 = sb("rate8", [P, D])
        c8 = sb("c8", [P, D])
        rate_b = sb("rate_b", [P, DB])
        c_b = sb("c_b", [P, DB])
        b_raw = sb("b_raw", [P, KD, NSTATE])
        b8 = sb("b8", [P, KD, TAUS, NSTATE])
        dvec = sb("dvec", [P, D])
        powers = sb("powers", [P, MT, D])
        taps = sb("taps", [P, MT, D])
        carry = sb("carry", [P, DB, T])
        decay = sb("decay", [P, DB])
        NBB = BLOCKS // BATCH
        SLOTS = NBB + 1
        scan_a = sb("scan_a", [P, DB, BATCH, SLOTS])
        states = sb("states", [P, DB, BATCH, SLOTS])
        inputs = scan_a[:, :, :, :].rearrange("p a b c -> p (a b c)")[:, 0:TOK]
        shifted = sb("shifted", [P, TOK])
        stats = sb("ssm_stats", [P, TPC, 6])
        mv = sb("ssm_mv", [P, TPC, 2])
        sd = sb("ssm_sd", [P, TPC])
        rstd = sb("ssm_rstd", [P, TPC])
        xn = sb("ssm_xn", [P, TPC, D])
        xt = sb("ssm_xt", [P, KD, CT])
        ident = g.const[:, C_IDENT:C_IDENT + P]
        ps_t = pb("ssm_ps_t", [P, KD, CT])
        ps_b = pb("ssm_ps_b", [P, 2, CT])
        ps_f = pb("ssm_ps_f", [P, TPC, CT])

        w_in = sem("ssm_w_in")
        rates = sem("ssm_rates")
        b_ready = sem("ssm_b_ready")
        own = sem("ssm_dve_own")
        var_ready = sem("ssm_var_ready")
        sd_ready = sem("ssm_sd_ready")
        xn_ready = sem("ssm_xn_ready")
        xn_kept = sem("ssm_xn_kept")
        xt_ps = sem("ssm_xt_ps")
        xt_ready = sem("ssm_xt_ready")
        in_ps = sem("ssm_in_ps")
        in_ready = sem("ssm_in_ready")
        shift_in = sem("ssm_shift_in")

        sem.start()
        with nc.Block() as block:
            @block.sync
            def _(sp):
                for t in range(TAUS):
                    rows = slice(t * NSTATE, (t + 1) * NSTATE)
                    sp.dma_start(rate8[rows, :], g.log_a_t).then_inc(w_in, 16)
                    sp.dma_start(c8[rows, :], g.c_t).then_inc(w_in, 16)
                sp.dma_start(rate_b[:, :], g.log_a_blocks).then_inc(w_in, 16)
                sp.dma_start(c_b[:, :], g.c_blocks).then_inc(w_in, 16)
                sp.dma_start(b_raw[:, :, :], g.b_t.rearrange("(k p) s -> p k s", p=P)).then_inc(w_in, 16)
                sp.dma_start(dvec[:, :], g.d_vec.rearrange("(o n) -> o n", o=1).broadcast_to([P, D])).then_inc(w_in, 16)
                sp.wait_ge(in_ready, CHUNKS + START)
                sp.wait_ge(b_ready, 3 + START)
                for t in range(TAUS):
                    rows = slice(t * NSTATE, (t + 1) * NSTATE)
                    sp.dma_start(shifted[rows, t:TOK], inputs[rows, 0:TOK - t]).then_inc(shift_in, 16)
                sp.wait_ge(shift_in, TAUS * 16 + START)

            @block.vector
            def _(dve):
                dve.memset(shifted[:, 0:TAUS], 0.0).then_inc(b_ready, 1)
                dve.wait_ge(w_in, 16 * (2 * TAUS + 4) + START)
                for k in range(KD):
                    dve.tensor_copy(b8[:, k, :, :], b_raw[:, k:k + 1, :].broadcast_to([P, TAUS, NSTATE])).then_inc(b_ready, 1)
                dve.wait_ge(rates, 3 + START)
                dve.tensor_tensor(carry[:, :, :], rate_b[:, :].rearrange("p (b o) -> p b o", o=1).broadcast_to([P, DB, T]),
                                  g.const[:, C_STEP:C_STEP + T].rearrange("p (o r) -> p o r", o=1)
                                  .broadcast_to([P, DB, T]), ALU.mult).then_inc(rates, 1)
                K = TPC + 1
                with dve.Fori(0, CHUNKS) as it:
                    st = Steps(dve, own, it * K)
                    on_its_own(dve, g)
                    for j in range(TPC):
                        st.add(dve.bn_stats(stats[:, j, :], g.x[:, ds(it * TPC + j, 1), :]))
                    st.last()
                    on_its_own(dve, g)
                    for j in range(TPC):
                        last = dve.bn_aggr(mv[:, j, :], stats[:, j, :])
                    last.then_inc(var_ready, 1)
                    dve.wait_ge(sd_ready, it + 1 + START)
                    st.add(dve.reciprocal(rstd[:, :], sd[:, :]))
                    st.last()
                    dve.wait_ge(xt_ps, it + START)
                    dve.wait_ge(xn_kept, it + START)
                    for j in range(TPC):
                        last = dve.tensor_scalar(xn[:, j, :], g.x[:, ds(it * TPC + j, 1), :], mv[:, j, 0:1],
                                                 rstd[:, j:j + 1], ALU.subtract, ALU.mult)
                    last.then_inc(xn_ready, 1)
                    assert st.n == K
                    dve.wait_ge(in_ps, it + 1 + START)
                    dve.tensor_copy(inputs[:, ds(it * CT, CT)], ps_b[:, 0, :]).then_inc(in_ready, 1)

            @block.gpsimd
            def _(pool):
                with pool.Fori(0, CHUNKS) as it:
                    pool.wait_ge(xn_ready, it + 1 + START)
                    on_its_own(pool, g)
                    pool.tensor_copy(g.v[:, ds(it * TPC, TPC), :], xn[:, :, :]).then_inc(xn_kept, 1)

            @block.scalar
            def _(act):
                act.wait_ge(w_in, 16 * (2 * TAUS + 4) + START)
                act.activation(rate8[:, :], rate8[:, :], ACT.Exp).then_inc(rates, 1)
                act.activation(rate_b[:, :], rate_b[:, :], ACT.Exp).then_inc(rates, 1)
                act.wait_ge(rates, 2 + START)
                act.activation(decay[:, :], rate_b[:, :], ACT.Exp, scale=-float(T)).then_inc(rates, 1)
                for m in range(MT):
                    act.activation(powers[:, m, :], rate8[:, :], ACT.Exp,
                                   scale=g.const[:, C_NEG_TAU + m:C_NEG_TAU + m + 1])
                act.wait_ge(rates, 4 + START)
                act.activation(carry[:, :, :], carry[:, :, :], ACT.Exp).then_inc(rates, 1)
                with act.Fori(0, CHUNKS) as it:
                    act.wait_ge(var_ready, it + 1 + START)
                    act.activation(sd[:, :], mv[:, :, 1], ACT.Sqrt, bias=g.eps[:, 0:1]).then_inc(sd_ready, 1)
                    act.wait_ge(xt_ps, it + 1 + START)
                    act.wait_ge(in_ps, it + START)
                    act.activation(xt[:, :, :], ps_t[:, :, :], ACT.Copy).then_inc(xt_ready, 1)

            @block.tensor
            def _(pe):
                pe.wait_ge(b_ready, 3 + START)
                with pe.Fori(0, CHUNKS) as it:
                    pe.wait_ge(xn_ready, it + 1 + START)
                    pe.wait_ge(xt_ready, it + START)
                    for k in range(KD):
                        for j in range(TPC):
                            last = pe.transpose(ps_t[:, k, j * P:(j + 1) * P], xn[:, j, k * P:(k + 1) * P], ident)
                    last.then_inc(xt_ps, 1)
                    pe.wait_ge(xt_ready, it + 1 + START)
                    pe.wait_ge(in_ready, it + START)
                    for k in range(KD):
                        last = pe.matmul(ps_b[:, 0, :], b8[:, k, :, :], xt[:, k, :], start=k == 0, stop=k == KD - 1)
                    last.then_inc(in_ps, 1)

        powers_s = [sb(f"powers_s{u}", [P, MT, TAUS, NSTATE]) for u in range(2)]
        tables = sem("ssm_tables")
        ps_ready = sem("powers_s_ready")
        end_ps = sem("end_ps")
        end_ready = sem("end_ready")
        scanned = sem("scanned")
        same_s = g.const[:, C_SAME_S:C_SAME_S + NSTATE].rearrange("p (a b s) -> p a b s", a=1, b=1)\
            .broadcast_to([P, MT, TAUS, NSTATE])
        sem.start()
        with nc.Block() as block:
            @block.gpsimd
            def _(pool):
                pool.tensor_copy(scan_a[:, :, :, :].rearrange("p a b c -> p a (b c)"),
                                 decay[:, :].rearrange("p (a o) -> p a o", o=1).broadcast_to([P, DB, BATCH * SLOTS]))\
                    .then_inc(tables, 1)
                pool.memset(states[:, :, :, 0:1], 0.0).then_inc(tables, 1)
                pool.wait_ge(tables, 1 + START)
                pool.memset(scan_a[:, :, :, 0:1], 0.0).then_inc(tables, 1)
                pool.tensor_tensor(taps[:, :, :], powers[:, :, :], c8[:, :].rearrange("p (o d) -> p o d", o=1)
                                   .broadcast_to([P, MT, D]), ALU.mult).then_inc(tables, 1)

            @block.vector
            def _(dve):
                with dve.Fori(0, DB // 2) as i:
                    for u in range(2):
                        dve.wait_ge(end_ps, 2 * i + START)
                        pw = powers[:, :, ds((2 * i + u) * TAUS, TAUS)].rearrange("p m (g o) -> p m g o", o=1)
                        dve.tensor_tensor(powers_s[u][:, :, :, :], pw.broadcast_to([P, MT, TAUS, NSTATE]), same_s,
                                          ALU.mult).then_inc(ps_ready, 1)
                dve.wait_ge(end_ready, DB + START)
                dve.wait_ge(tables, 4 + START)
                flat = lambda x: x[:, :, :, :].rearrange("p a b c -> p (a b c)")
                dve.tensor_tensor_scan(flat(states), flat(scan_a), flat(states), 0.0, ALU.mult, ALU.add)\
                    .then_inc(scanned, 1)

            @block.scalar
            def _(act):
                with act.Fori(0, DB // 2) as i:
                    for u in range(2):
                        act.wait_ge(end_ps, 2 * i + u + 1 + START)
                        act.activation(states[:, ds(2 * i + u, 1), :, 1:],
                                       ps_b[:, u, 0:BLOCKS].rearrange("p (o b c) -> p o b c", o=1, b=BATCH), ACT.Copy)\
                            .then_inc(end_ready, 1)

            @block.tensor
            def _(pe):
                ends = shifted[:, :].rearrange("p (c t) -> p c t", t=T)
                with pe.Fori(0, DB // 2) as i:
                    for u in range(2):
                        pe.wait_ge(ps_ready, 2 * i + u + 1 + START)
                        pe.wait_ge(end_ready, 2 * i + START)
                        for m in range(MT):
                            last = pe.matmul(ps_b[:, u, 0:BLOCKS], powers_s[u][:, m, :, :], ends[:, :, T - 1 - TAUS * m],
                                             start=m == 0, stop=m == MT - 1)
                        last.then_inc(end_ps, 1)

        diag = [sb(f"state_diag{u}", [P, TAUS, BATCH, NBB]) for u in range(2)]
        carry_c = [sb(f"carry_c{u}", [P, T]) for u in range(2)]
        diag_ready = sem("diag_ready")
        carry_ready = sem("carry_ready")
        inj_ps = sem("inj_ps")
        inj_ready = sem("inj_ready")
        QG = P // T
        sem.start()
        with nc.Block() as block:
            def diagonal(eng, d, u, w):
                st = states[:, ds(d, 1), :, 0:NBB]
                for b in range(BATCH):
                    last = eng.tensor_tensor(
                        diag[u][:, :, b, :], states[:, ds(d, 1), b, 0:NBB].broadcast_to([P, TAUS, NBB]),
                        g.const[:, C_SAME_G:C_SAME_G + TAUS].rearrange("p (g o) -> p g o", o=1)
                        .broadcast_to([P, TAUS, NBB]), ALU.mult)
                    last.then_inc(diag_ready, 1)

            @block.gpsimd
            def _(pool):
                with pool.Fori(0, DB // 2) as i:
                    for u in range(2):
                        pool.wait_ge(inj_ps, 2 * i + START)
                        pool.tensor_tensor(carry_c[u][:, :], carry[:, ds(2 * i + u, 1), :],
                                           c_b[:, ds(2 * i + u, 1)].broadcast_to([P, T]), ALU.mult)\
                            .then_inc(carry_ready, 1)

            @block.vector
            def _(dve):
                with dve.Fori(0, DB // 2) as i:
                    for u in range(2):
                        dve.wait_ge(inj_ps, 2 * i + START)
                        diagonal(dve, 2 * i + u, u, 0)

            @block.scalar
            def _(act):
                with act.Fori(0, DB // 2) as i:
                    for u in range(2):
                        act.wait_ge(inj_ps, 2 * i + u + 1 + START)
                        act.activation(g.att[:, :, ds((2 * i + u) * TAUS, TAUS)],
                                       ps_b[:, u, 0:D].rearrange("p (g t) -> p t g", g=TAUS), ACT.Copy)\
                            .then_inc(inj_ready, 1)

            @block.tensor
            def _(pe):
                with pe.Fori(0, DB // 2) as i:
                    for u in range(2):
                        pe.wait_ge(diag_ready, (2 * i + u + 1) * BATCH + START)
                        pe.wait_ge(carry_ready, 2 * i + u + 1 + START)
                        pe.wait_ge(inj_ready, 2 * i + START)
                        for q in range(QG):
                            rhs = diag[u][:, :, :, :].rearrange("p g b (t q) -> p (g b) t q", q=QG)[:, :, :, q]
                            last = pe.matmul(ps_b[q * T:(q + 1) * T, u, 0:D], carry_c[u][:, :], rhs, start=True,
                                             stop=True, tile_position=(0, q * T))
                        last.then_inc(inj_ps, 1)

        BPC = CT // T
        delayed = sb("delayed", [P, MT, BPC, T])
        total = sb("ssm_total", [P, TPC, D])
        pad_zero = sem("pad_zero")
        pad_ready = sem("pad_ready")
        fir_ps = sem("fir_ps")
        total_own = sem("total_own")
        total_ready = sem("total_ready")
        x_own = sem("ssm_x_own")
        x_ready = sem("ssm_x_ready")
        sem.start()
        with nc.Block() as block:
            @block.gpsimd
            def _(pool):
                pool.memset(delayed[:, :, :, :], 0.0).then_inc(pad_zero, 1)
                pool.wait_ge(pad_zero, 1 + START)
                with pool.Fori(0, CHUNKS) as it:
                    pool.wait_ge(fir_ps, it + START)
                    for m in range(MT):
                        n = T - TAUS * m
                        b = shifted[:, ds(it * CT, CT)].rearrange("p (c t) -> p c t", t=T)
                        pool.tensor_tensor(delayed[:, m, :, TAUS * m:], b[:, :, 0:n],
                                           g.const[:, C_TAU_MASK:C_TAU_MASK + n].rearrange("p (o t) -> p o t", o=1)
                                           .broadcast_to([P, BPC, n]), ALU.mult).then_inc(pad_ready, 1)
                    pool.wait_ge(x_own, it + 1 + START)
                    pool.wait_ge(total_own, it + START)
                    pool.tensor_tensor(total[:, :, :], g.v[:, ds(it * TPC, TPC), :],
                                       dvec[:, :].rearrange("p (o d) -> p o d", o=1).broadcast_to([P, TPC, D]),
                                       ALU.mult).then_inc(total_ready, 1)

            @block.vector
            def _(dve):
                with dve.Fori(0, CHUNKS) as it:
                    xs = g.x[:, ds(it * TPC, TPC), :]
                    dve.tensor_tensor(xs, xs, g.att[:, ds(it * TPC, TPC), :], ALU.add).then_inc(x_own, 1)
                    dve.wait_ge(x_own, it + 1 + START)
                    dve.wait_ge(total_ready, it + 1 + START)
                    dve.tensor_tensor(xs, xs, total[:, :, :], ALU.add).then_inc(total_own, 1)
                    dve.wait_ge(total_own, it + 1 + START)
                    dve.wait_ge(fir_ps, it + 1 + START)
                    dve.tensor_tensor(xs, xs, ps_f[:, :, 0:D], ALU.add).then_inc(x_ready, 1)

            @block.tensor
            def _(pe):
                with pe.Fori(0, CHUNKS) as it:
                    pe.wait_ge(pad_ready, (it + 1) * MT + START)
                    pe.wait_ge(x_ready, it + START)
                    for j in range(TPC):
                        for m in range(MT):
                            w = delayed[:, m, j * QG:(j + 1) * QG, :]
                            last = pe.matmul(ps_f[:, j, 0:D], w, taps[:, m, :], start=m == 0, stop=m == MT - 1)
                    last.then_inc(fir_ps, 1)


FI = 938
KI = -(-FI // P)
FLAST = FI - (KI - 1) * P
RUNS = CHUNKS + ROUTED
SHARED = E
MOE_ROWS = RUNS * CT


def fw(m):
    return P if m < KI - 1 else FLAST


def phase_moe(nc, top, g):
    slots_in = nc.dram_tensor("slots_in", (MOE_ROWS, D), F32, kind="Internal").ap()
    slots_out = nc.dram_tensor("slots_out", (MOE_ROWS, D), F32, kind="Internal").ap()
    with ExitStack() as ctx:
        sem = Semaphores(nc, ctx)
        keep = lambda name, shape, dt=F32: ctx.enter_context(nc.sbuf_tensor(name, shape, dt))
        slot = keep("slot", [P, TOPK, TILES], mybir.dt.int32)
        weight = keep("weight", [P, TOPK, TILES])
        experts = keep("experts", [P, RUNS], mybir.dt.int32)
        logits = keep("logits", [P, TILES, E])
        moe_norm(nc, g, sem, slots_in, logits)
        moe_route(nc, g, sem, slots_in, logits, slot, weight, experts)
        moe_experts(nc, g, sem, slots_in, slots_out, experts)
        moe_combine(nc, g, sem, slots_out, slot, weight)


def moe_norm(nc, g, sem, slots_in, logits):
    with ExitStack() as ctx:
        sb = lambda name, shape, dt=F32: ctx.enter_context(nc.sbuf_tensor(name, shape, dt))
        pb = lambda name, shape, dt=F32: ctx.enter_context(nc.psum_tensor(name, shape, dt))
        gate = sb("gate", [P, KD, E])
        zero = sb("moe_zero", [P, TPC, D])
        stats = sb("moe_stats", [P, TPC, 6])
        mv = sb("moe_mv", [P, TPC, 2])
        sd = sb("moe_sd", [P, TPC])
        rstd = sb("moe_rstd", [P, TPC])
        xn = sb("moe_xn", [P, TPC, D])
        xt = sb("moe_xt", [P, KD, CT])
        ident = g.const[:, C_IDENT:C_IDENT + P]
        ps_t = pb("moe_ps_t", [P, KD, CT])
        ps_l = pb("moe_ps_l", [P, TPC, E])
        gate_in = sem("gate_in")
        zero_ready = sem("moe_zero_ready")
        zero_out = sem("moe_zero_out")
        own = sem("moe_dve_own")
        var_ready = sem("moe_var_ready")
        sd_ready = sem("moe_sd_ready")
        xn_ready = sem("moe_xn_ready")
        xn_kept = sem("moe_xn_kept")
        xn_out = sem("moe_xn_out")
        xt_ps = sem("moe_xt_ps")
        xt_ready = sem("moe_xt_ready")
        lg_ps = sem("logits_ps")
        lg_ready = sem("logits_ready")
        sem.start()
        with nc.Block() as block:
            @block.sync
            def _(sp):
                sp.dma_start(gate[:, :, :], g.gate_t.rearrange("(k p) e -> p k e", p=P)).then_inc(gate_in, 16)
                sp.wait_ge(zero_ready, 1 + START)
                with sp.Fori(0, ROUTED) as i:
                    sp.dma_start(slots_in[ds(TOK + i * CT, CT), :].rearrange("(p t) n -> p t n", p=P),
                                 zero[:, :, :]).then_inc(zero_out, 16)
                with sp.Fori(0, CHUNKS) as it:
                    sp.wait_ge(xn_ready, it + 1 + START)
                    sp.dma_start(slots_in[ds(it * CT, CT), :].rearrange("(t p) n -> p t n", p=P),
                                 xn[:, :, :]).then_inc(xn_out, 16)
                sp.wait_ge(xn_out, CHUNKS * 16 + START)
                sp.wait_ge(zero_out, ROUTED * 16 + START)

            @block.gpsimd
            def _(pool):
                with pool.Fori(0, CHUNKS) as it:
                    pool.wait_ge(xn_ready, it + 1 + START)
                    on_its_own(pool, g)
                    pool.tensor_copy(g.v[:, ds(it * TPC, TPC), :], xn[:, :, :]).then_inc(xn_kept, 1)

            @block.vector
            def _(dve):
                dve.memset(zero[:, :, :], 0.0).then_inc(zero_ready, 1)
                K = TPC + 1
                with dve.Fori(0, CHUNKS) as it:
                    st = Steps(dve, own, it * K)
                    on_its_own(dve, g)
                    for j in range(TPC):
                        st.add(dve.bn_stats(stats[:, j, :], g.x[:, ds(it * TPC + j, 1), :]))
                    st.last()
                    on_its_own(dve, g)
                    for j in range(TPC):
                        last = dve.bn_aggr(mv[:, j, :], stats[:, j, :])
                    last.then_inc(var_ready, 1)
                    dve.wait_ge(sd_ready, it + 1 + START)
                    st.add(dve.reciprocal(rstd[:, :], sd[:, :]))
                    st.last()
                    dve.wait_ge(xt_ps, it + START)
                    dve.wait_ge(xn_kept, it + START)
                    dve.wait_ge(xn_out, it * 16 + START)
                    for j in range(TPC):
                        last = dve.tensor_scalar(xn[:, j, :], g.x[:, ds(it * TPC + j, 1), :], mv[:, j, 0:1],
                                                 rstd[:, j:j + 1], ALU.subtract, ALU.mult)
                    last.then_inc(xn_ready, 1)
                    assert st.n == K
                    dve.wait_ge(lg_ps, it + 1 + START)
                    dve.tensor_copy(logits[:, ds(it * TPC, TPC), :], ps_l[:, :, :]).then_inc(lg_ready, 1)

            @block.scalar
            def _(act):
                with act.Fori(0, CHUNKS) as it:
                    act.wait_ge(var_ready, it + 1 + START)
                    act.activation(sd[:, :], mv[:, :, 1], ACT.Sqrt, bias=g.eps[:, 0:1]).then_inc(sd_ready, 1)
                    act.wait_ge(xt_ps, it + 1 + START)
                    act.wait_ge(lg_ps, it + START)
                    act.activation(xt[:, :, :], ps_t[:, :, :], ACT.Copy).then_inc(xt_ready, 1)

            @block.tensor
            def _(pe):
                pe.wait_ge(gate_in, 16 + START)
                with pe.Fori(0, CHUNKS) as it:
                    pe.wait_ge(xn_ready, it + 1 + START)
                    pe.wait_ge(xt_ready, it + START)
                    for k in range(KD):
                        for j in range(TPC):
                            last = pe.transpose(ps_t[:, k, j * P:(j + 1) * P], xn[:, j, k * P:(k + 1) * P], ident)
                    last.then_inc(xt_ps, 1)
                    pe.wait_ge(xt_ready, it + 1 + START)
                    pe.wait_ge(lg_ready, it + START)
                    for j in range(TPC):
                        for k in range(KD):
                            last = pe.matmul(ps_l[:, j, :], xt[:, k, j * P:(j + 1) * P], gate[:, k, :],
                                             start=k == 0, stop=k == KD - 1)
                    last.then_inc(lg_ps, 1)


def moe_route(nc, g, sem, slots_in, logits, slot, weight, experts):
    with ExitStack() as ctx:
        sb = lambda name, shape, dt=F32: ctx.enter_context(nc.sbuf_tensor(name, shape, dt))
        pb = lambda name, shape, dt=F32: ctx.enter_context(nc.psum_tensor(name, shape, dt))
        ones = sb("rt_ones", [P, P])
        top_l = sb("top_logit", [P, TILES, 1])
        probs = sb("rt_probs", [P, TILES, E])
        psum_e = sb("rt_sum", [P, TILES, 1])
        score = sb("rt_score", [P, TILES, E])
        best = sb("rt_best", [P, TOPK, TILES, 1])
        place = sb("rt_place", [P, TILES, 1])
        chosen = sb("rt_chosen", [P, TOPK, TILES, E])
        member = sb("rt_member", [P, E, TILES])
        counts = sb("rt_counts", [P, E, TILES])
        keep_s = sb("rt_keep", [P, E, TILES])
        running = sb("rt_running", [P, E, TILES])
        where = sb("rt_where", [P, E, TILES])
        over = sb("rt_over", [P, E, CHUNKS])
        tiles = sb("rt_tiles", [P, E])
        tiles_upto = sb("rt_tiles_upto", [P, E])
        base = sb("rt_base", [P, E])
        past = sb("rt_past", [P, ROUTED, E])
        ex_f = sb("rt_experts", [P, RUNS])
        slot_f = sb("rt_slot", [P, TOPK, TILES])
        denom = sb("rt_denom", [P, TILES])
        ps_rank = pb("ps_rank", [P, E, TILES])
        ps_count = pb("ps_count", [P, E, TILES])
        own = sem("rt_own")
        less_max = sem("rt_less_max")
        exp_done = sem("rt_exp_done")
        members = sem("rt_members")
        rank_ps = sem("rank_ps")
        slots = sem("rt_slots")
        sent = sem.from_zero("rt_sent")
        sem.start()
        with nc.Block() as block:
            col = lambda a, w, n: g.const[:, a:a + w].rearrange("p (o e) -> p o e", o=1).broadcast_to([P, n, w])

            @block.vector
            def _(dve):
                st = Steps(dve, own)

                def do(instruction):
                    st.add(instruction)
                    st.last()
                each = lambda x: x.broadcast_to([P, TILES, E])
                do(dve.memset(ones[:, :], 1.0))
                do(dve.reduce_max(top_l[:, :, :], logits[:, :, :], AX.X))
                dve.tensor_tensor(probs[:, :, :], logits[:, :, :], each(top_l[:, :, :]), ALU.subtract).then_inc(less_max, 1)
                dve.wait_ge(exp_done, 1 + START)
                do(dve.reduce_sum(psum_e[:, :, :], probs[:, :, :], AX.X))
                do(dve.reciprocal(psum_e[:, :, :], psum_e[:, :, :]))
                do(dve.tensor_tensor(probs[:, :, :], probs[:, :, :], each(psum_e[:, :, :]), ALU.mult))
                for n in range(TOPK):
                    do(dve.reduce_max(best[:, n, :, :], probs[:, :, :], AX.X))
                    do(dve.tensor_tensor(score[:, :, :], probs[:, :, :], each(best[:, n, :, :]), ALU.is_equal))
                    do(dve.tensor_tensor(score[:, :, :], score[:, :, :], col(C_LEFT, E, TILES), ALU.mult))
                    do(dve.reduce_max(place[:, :, :], score[:, :, :], AX.X))
                    do(dve.tensor_tensor(chosen[:, n, :, :], each(place[:, :, :]), col(C_LEFT, E, TILES), ALU.is_equal))
                    if n == 0:
                        do(dve.scalar_tensor_tensor(out=probs[:, :, :], in0=chosen[:, 0, :, :], scalar=-2.0,
                                                    in1=probs[:, :, :], op0=ALU.mult, op1=ALU.add))
                do(dve.tensor_tensor(denom[:, :], best[:, 0, :, 0], best[:, 1, :, 0], ALU.add))
                do(dve.tensor_scalar(denom[:, :], denom[:, :], 1e-8, None, ALU.add))
                do(dve.reciprocal(denom[:, :], denom[:, :]))
                for n in range(TOPK):
                    do(dve.tensor_tensor(weight[:, n, :], best[:, n, :, 0], denom[:, :], ALU.mult))
                dve.tensor_tensor(member[:, :, :].rearrange("p e t -> p t e"), chosen[:, 0, :, :], chosen[:, 1, :, :],
                                  ALU.add).then_inc(members, 1)
                do(dve.memset(keep_s[:, :, :], 1.0))
                do(dve.memset(keep_s[:, :, 0:1], 0.0))
                dve.wait_ge(rank_ps, 1 + START)
                flat = lambda x: x[:, :, :].rearrange("p e t -> p (e t)")
                do(dve.tensor_copy(counts[:, :, :], ps_count[:, :, :]))
                do(dve.tensor_tensor_scan(flat(running), flat(keep_s), flat(counts), 0.0, ALU.mult, ALU.add))
                do(dve.tensor_tensor(over[:, :, :], running[:, :, TILES - 1:TILES].broadcast_to([P, E, CHUNKS]),
                                     col(C_LIMITS, CHUNKS, E), ALU.is_gt))
                do(dve.reduce_sum(tiles[:, :].rearrange("p (e o) -> p e o", o=1), over[:, :, :], AX.X))
                do(dve.tensor_tensor_scan(tiles_upto[:, :], ones[:, 0:E], tiles[:, :], 0.0, ALU.mult, ALU.add))
                do(dve.tensor_tensor(base[:, :], tiles_upto[:, :], tiles[:, :], ALU.subtract))
                do(dve.tensor_scalar(base[:, :], base[:, :], float(CT), float(TOK), ALU.mult, ALU.add))
                do(dve.tensor_tensor(where[:, :, :], running[:, :, :], counts[:, :, :], ALU.subtract))
                do(dve.tensor_tensor(where[:, :, :], where[:, :, :], ps_rank[:, :, :], ALU.add))
                do(dve.tensor_tensor(where[:, :, :], where[:, :, :], base[:, :].rearrange("p (e o) -> p e o", o=1)
                                     .broadcast_to([P, E, TILES]), ALU.add))
                for n in range(TOPK):
                    do(dve.tensor_tensor(chosen[:, n, :, :], chosen[:, n, :, :], where[:, :, :].rearrange("p e t -> p t e"),
                                         ALU.mult))
                    do(dve.reduce_sum(slot_f[:, n, :].rearrange("p (t o) -> p t o", o=1), chosen[:, n, :, :], AX.X))
                dve.tensor_copy(slot[:, :, :], slot_f[:, :, :]).then_inc(slots, 1)
                do(dve.tensor_tensor(past[:, :, :], tiles_upto[:, :].rearrange("p (o e) -> p o e", o=1)
                                     .broadcast_to([P, ROUTED, E]),
                                     g.const[:, C_TILE:C_TILE + ROUTED].rearrange("p (n o) -> p n o", o=1)
                                     .broadcast_to([P, ROUTED, E]), ALU.is_le))
                do(dve.memset(ex_f[:, 0:CHUNKS], float(SHARED)))
                do(dve.reduce_sum(ex_f[:, CHUNKS:].rearrange("p (n o) -> p n o", o=1), past[:, :, :], AX.X))
                do(dve.tensor_scalar(ex_f[:, CHUNKS:], ex_f[:, CHUNKS:], float(E - 1), None, ALU.min))
                dve.tensor_copy(experts[:, :], ex_f[:, :]).then_inc(slots, 1)

            @block.scalar
            def _(act):
                act.wait_ge(less_max, 1 + START)
                act.activation(probs[:, :, :], probs[:, :, :], ACT.Exp).then_inc(exp_done, 1)

            @block.tensor
            def _(pe):
                pe.wait_ge(members, 1 + START)
                pe.matmul(ps_rank[:, :, :], g.const[:, C_UPPER:C_UPPER + P], member[:, :, :], start=True, stop=True)
                pe.matmul(ps_count[:, :, :], ones[:, :], member[:, :, :], start=True, stop=True).then_inc(rank_ps, 1)

            @block.gpsimd
            def _(pool):
                pool.wait_ge(slots, 2 + START)
                for t in range(TILES):
                    for n in range(TOPK):
                        pool.indirect_dma_start(out=slots_in, out_offset=bass.IndirectOffsetOnAxis(
                            ap=slot[:, n, t:t + 1], axis=0), in_=g.v[:, t, :], in_offset=None).then_inc(sent, 16)
                pool.wait_ge(sent, TILES * TOPK * 16)


def moe_experts(nc, g, sem, slots_in, slots_out, experts):
    with ExitStack() as ctx:
        sb = lambda name, shape, dt=F32: ctx.enter_context(nc.sbuf_tensor(name, shape, dt))
        pb = lambda name, shape, dt=F32: ctx.enter_context(nc.psum_tensor(name, shape, dt))
        up32 = sb("moe_up32", [P, KD, 2 * FI])
        uph = sb("moe_uph", [P, KD, 2 * FI], FR)
        upl = sb("moe_upl", [P, KD, 2 * FI], FR)
        dn32 = sb("moe_dn32", [P, KI, D])
        dnh = sb("moe_dnh", [P, KI, D], FR)
        dnl = sb("moe_dnl", [P, KI, D], FR)
        rows = sb("moe_rows", [P, TPC, D])
        xth = sb("moe_xth", [P, KD, CT], FR)
        xtl = sb("moe_xtl", [P, KD, CT], FR)
        silu = sb("moe_silu", [P, 2, CT])
        h32 = sb("moe_h32", [P, 2, CT])
        hh = sb("moe_hh", [P, KI, CT], FR)
        hl = sb("moe_hl", [P, KI, CT], FR)
        y = sb("moe_y", [P, TPC, D])
        ident = g.const[:, C_IDENT:C_IDENT + P]
        ps_t = pb("ex_ps_t", [P, KD, CT])
        ps_g = pb("ex_ps_g", [P, 2, CT])
        ps_u = pb("ex_ps_u", [P, 2, CT])
        ps_y = pb("ex_ps_y", [P, 2, CT])
        up_in = sem("ex_up_in")
        rows_in = sem("ex_rows_in")
        dn_in = sem("ex_dn_in")
        up_hi = sem("ex_up_hi")
        up_lo = sem("ex_up_lo")
        dn_hi = sem("ex_dn_hi")
        dn_lo = sem("ex_dn_lo")
        xt_ps = sem("ex_xt_ps")
        xt_hi = sem("ex_xt_hi")
        xt_lo = sem("ex_xt_lo")
        gu_ps = sem("ex_gu_ps")
        silu_ready = sem("ex_silu")
        h_ready = sem("ex_h")
        h_hi = sem("ex_h_hi")
        h_lo = sem("ex_h_lo")
        y_ps = sem("ex_y_ps")
        y_ready = sem("ex_y_ready")
        y_out = sem("ex_y_out")
        sem.start()
        with nc.Block() as block:
            @block.sync
            def _(sp):
                with sp.Fori(0, RUNS) as i:
                    expert = sp.value_load(experts[0:1, ds(i, 1)], min_val=0, max_val=SHARED)
                    sp.wait_ge(up_lo, i * KD + START)
                    sp.dma_start(up32[:, :, :], g.w_up[ds(expert * D, D), :].rearrange("(k p) n -> p k n", p=P))\
                      .then_inc(up_in, 16)
                    sp.wait_ge(xt_ps, i + START)
                    sp.dma_start(rows[:, :, :], slots_in[ds(i * CT, CT), :].rearrange("(t p) n -> p t n", p=P))\
                      .then_inc(rows_in, 16)
                    sp.wait_ge(dn_lo, i + START)
                    sp.dma_start(dn32[:, 0:KI - 1, :], g.w_down[ds(expert * FI, (KI - 1) * P), :]
                                 .rearrange("(m p) n -> p m n", p=P)).then_inc(dn_in, 16)
                    sp.dma_start(dn32[0:FLAST, KI - 1, :], g.w_down[ds(expert * FI + (KI - 1) * P, FLAST), :])\
                      .then_inc(dn_in, 16)

            @block.gpsimd
            def _(pool):
                with pool.Fori(0, RUNS) as i:
                    pool.wait_ge(up_in, (i + 1) * 16 + START)
                    pool.wait_ge(gu_ps, i * KI + START)
                    on_its_own(pool, g)
                    for k in range(KD):
                        pool.tensor_copy(uph[:, k, :], up32[:, k, :]).then_inc(up_hi, 1)
                    pool.wait_ge(dn_in, (i + 1) * 32 + START)
                    pool.wait_ge(y_ps, i * TPC + START)
                    on_its_own(pool, g)
                    pool.tensor_copy(dnh[:, 0:KI - 1, :], dn32[:, 0:KI - 1, :]).then_inc(dn_hi, 1)
                    pool.tensor_copy(dnh[0:FLAST, KI - 1, :], dn32[0:FLAST, KI - 1, :]).then_inc(dn_hi, 1)
                    for m in range(KI):
                        pool.wait_ge(h_ready, i * KI + m + 1 + START)
                        on_its_own(pool, g)
                        pool.tensor_copy(hh[0:fw(m), m, :], h32[0:fw(m), m % 2, :]).then_inc(h_hi, 1)

            @block.vector
            def _(dve):
                with dve.Fori(0, RUNS) as i:
                    dve.wait_ge(xt_hi, i + 1 + START)
                    dve.tensor_tensor(xtl[:, :, :], ps_t[:, :, :], xth[:, :, :].bitcast(F32), ALU.subtract)\
                       .then_inc(xt_lo, 1)
                    for k in range(KD):
                        dve.wait_ge(up_hi, i * KD + k + 1 + START)
                        dve.tensor_tensor(upl[:, k, :], up32[:, k, :], uph[:, k, :].bitcast(F32), ALU.subtract)\
                           .then_inc(up_lo, 1)
                    dve.wait_ge(dn_hi, (i + 1) * 2 + START)
                    dve.tensor_tensor(dnl[:, 0:KI - 1, :], dn32[:, 0:KI - 1, :], dnh[:, 0:KI - 1, :].bitcast(F32),
                                      ALU.subtract)
                    dve.tensor_tensor(dnl[0:FLAST, KI - 1, :], dn32[0:FLAST, KI - 1, :],
                                      dnh[0:FLAST, KI - 1, :].bitcast(F32), ALU.subtract).then_inc(dn_lo, 1)

                    def low(m):
                        dve.wait_ge(h_hi, i * KI + m + 1 + START)
                        dve.tensor_tensor(hl[0:fw(m), m, :], h32[0:fw(m), m % 2, :],
                                          hh[0:fw(m), m, :].bitcast(F32), ALU.subtract).then_inc(h_lo, 1)
                    for m in range(KI):
                        dve.wait_ge(silu_ready, i * KI + m + 1 + START)
                        dve.wait_ge(h_lo, i * KI + max(m - 1, 0) + START)
                        dve.tensor_tensor(h32[0:fw(m), m % 2, :], silu[0:fw(m), m % 2, :], ps_u[0:fw(m), m % 2, :],
                                          ALU.mult).then_inc(h_ready, 1)
                        if m:
                            low(m - 1)
                    low(KI - 1)

            @block.scalar
            def _(act):
                def outputs(i):
                    act.wait_ge(y_out, i * 16 + START)
                    for j in range(TPC):
                        act.wait_ge(y_ps, i * TPC + j + 1 + START)
                        act.activation(y[:, j, :], ps_y[:, j % 2, 0:D], ACT.Copy).then_inc(y_ready, 1)
                    act.wait_ge(y_ready, (i + 1) * TPC + START)
                    act.dma_start(slots_out[ds(i * CT, CT), :].rearrange("(t p) n -> p t n", p=P), y[:, :, :])\
                       .then_inc(y_out, 16)

                def step(i, before):
                    act.wait_ge(xt_ps, i + 1 + START)
                    act.wait_ge(gu_ps, i * KI + START)
                    act.activation(xth[:, :, :], ps_t[:, :, :], ACT.Copy).then_inc(xt_hi, 1)
                    if before is not None:
                        outputs(before)
                    for m in range(KI):
                        act.wait_ge(gu_ps, i * KI + m + 1 + START)
                        act.wait_ge(h_ready, i * KI + max(m - 1, 0) + START)
                        act.activation(silu[0:fw(m), m % 2, :], ps_g[0:fw(m), m % 2, :], ACT.Silu).then_inc(silu_ready, 1)
                step(0, None)
                with act.Fori(1, RUNS) as i:
                    step(i, i - 1)
                outputs(RUNS - 1)
                act.wait_ge(y_out, RUNS * 16 + START)

            @block.tensor
            def _(pe):
                def turn(i):
                    pe.wait_ge(rows_in, (i + 1) * 16 + START)
                    pe.wait_ge(xt_lo, i + START)
                    for k in range(KD):
                        for j in range(TPC):
                            last = pe.transpose(ps_t[:, k, j * P:(j + 1) * P], rows[:, j, k * P:(k + 1) * P], ident)
                    last.then_inc(xt_ps, 1)

                def up(i):
                    pe.wait_ge(xt_lo, i + 1 + START)
                    pe.wait_ge(up_lo, (i + 1) * KD + START)
                    for m in range(KI):
                        pe.wait_ge(h_ready, i * KI + max(m - 1, 0) + START)
                        for ps, first in ((ps_g, 0), (ps_u, FI)):
                            w = slice(first + m * P, first + m * P + fw(m))
                            for k in range(KD):
                                last = product3(pe, ps[0:fw(m), m % 2, :], uph[:, k, w], upl[:, k, w], xth[:, k, :],
                                                xtl[:, k, :], k == 0, k == KD - 1)
                        last.then_inc(gu_ps, 1)

                def down(i):
                    pe.wait_ge(h_lo, (i + 1) * KI + START)
                    pe.wait_ge(dn_lo, i + 1 + START)
                    for j in range(TPC):
                        pe.wait_ge(y_ready, i * TPC + max(j - 1, 0) + START)
                        t = slice(j * P, (j + 1) * P)
                        for m in range(KI):
                            last = product3(pe, ps_y[:, j % 2, 0:D], hh[0:fw(m), m, t], hl[0:fw(m), m, t],
                                            dnh[0:fw(m), m, :], dnl[0:fw(m), m, :], m == 0, m == KI - 1)
                        last.then_inc(y_ps, 1)
                turn(0)
                up(0)
                with pe.Fori(1, RUNS) as i:
                    turn(i)
                    down(i - 1)
                    up(i)
                down(RUNS - 1)


def moe_combine(nc, g, sem, slots_out, slot, weight):
    with ExitStack() as ctx:
        N = 4
        sb = lambda name, shape, dt=F32: ctx.enter_context(nc.sbuf_tensor(name, shape, dt))
        own_row = sb("own_row", [P, N, D])
        picked = sb("picked", [P, N, TOPK, D])
        shared_in = [sem(f"cb_shared_in{u}") for u in range(N)]
        picked_in = [sem.from_zero(f"cb_picked_in{u}") for u in range(N)]
        own = sem("cb_own")
        out_ready = sem("cb_ready")
        stored = sem("cb_stored")
        sem.start()
        with nc.Block() as block:
            @block.sync
            def _(sp):
                for t in range(TILES):
                    if t >= N:
                        sp.wait_ge(out_ready, t - N + 1 + START)
                    sp.dma_start(own_row[:, t % N, :], slots_out[t * P:(t + 1) * P, :]).then_inc(shared_in[t % N], 16)

            @block.gpsimd
            def _(pool):
                for t in range(TILES):
                    if t >= N:
                        pool.wait_ge(out_ready, t - N + 1 + START)
                    for n in range(TOPK):
                        pool.indirect_dma_start(out=picked[:, t % N, n, :], out_offset=None, in_=slots_out,
                                                in_offset=bass.IndirectOffsetOnAxis(ap=slot[:, n, t:t + 1], axis=0))\
                            .then_inc(picked_in[t % N], 16)

            @block.vector
            def _(dve):
                st = Steps(dve, own)
                for t in range(TILES):
                    x = g.x[:, t, :]
                    dve.wait_ge(shared_in[t % N], 16 * (t // N + 1) + START)
                    st.add(dve.tensor_tensor(x, x, own_row[:, t % N, :], ALU.add))
                    dve.wait_ge(picked_in[t % N], 16 * TOPK * (t // N + 1))
                    for n in range(TOPK):
                        st.last()
                        last = dve.scalar_tensor_tensor(out=x, in0=picked[:, t % N, n, :], scalar=weight[:, n, t:t + 1],
                                                        in1=x, op0=ALU.mult, op1=ALU.add)
                        if n < TOPK - 1:
                            st.add(last)
                    last.then_inc(out_ready, 1)

            @block.scalar
            def _(act):
                for t in range(TILES):
                    act.wait_ge(out_ready, t + 1 + START)
                    act.dma_start(g.out[t * P:(t + 1) * P, :], g.x[:, t, :]).then_inc(stored, 16)
                act.wait_ge(stored, TILES * 16 + START)


class Shared:
    pass


def program(nc, names):
    g = Shared()
    g.constants = names["constants"]
    g.x_in = names["x_in"]
    g.qkv_w = names["qkv_w"]
    g.qk_bias = names["qk_bias"]
    g.v_bias = names["v_bias"]
    g.out_w = names["out_w"]
    g.out_b = names["out_b"]
    g.up_t = names["up_t"]
    g.down_t = names["down_t"]
    g.log_a_t = names["log_a_t"]
    g.c_t = names["c_t"]
    g.log_a_blocks = names["log_a_blocks"]
    g.c_blocks = names["c_blocks"]
    g.b_t = names["b_t"]
    g.d_vec = names["d_vec"]
    g.gate_t = names["gate_t"]
    g.w_up = names["w_up"]
    g.w_down = names["w_down"]
    g.out = names["out"]
    with ExitStack() as ctx:
        sb = lambda name, shape, dt=F32: ctx.enter_context(nc.sbuf_tensor(name, shape, dt))
        g.const = sb("const", [P, C_END])
        g.ident_bf = sb("ident_bf", [P, P], BF16)
        g.mask_bf = sb("mask_bf", [P, 3 * P], BF16)
        g.eps = sb("eps", [P, 1])
        g.started = ctx.enter_context(nc.semaphore("started"))
        g.passed = ctx.enter_context(nc.semaphore("passed"))
        g.x = sb("x", [P, TILES, D])
        g.v = sb("v", [P, TILES, D])
        g.q_k_hi = nc.dram_tensor("q_k_hi", (2 * D, TOK), F32, kind="Internal").ap()
        g.q_k_lo = nc.dram_tensor("q_k_lo", (2 * D, TOK), F32, kind="Internal").ap()
        phase_qkv(nc, ctx, g)
        with nc.sbuf_tensor("att", [P, TILES, D], F32) as att:
            g.att = att
            phase_attention(nc, ctx, g)
            phase_ffn(nc, ctx, g)
            phase_ssm(nc, ctx, g)
        phase_moe(nc, ctx, g)


def kernel(**inputs):
    import concourse.bacc as bacc
    from concourse.bass_utils import run_bass_kernel_spmd

    a = {k: np.asarray(v) for k, v in inputs.items()}
    lay = np.ascontiguousarray
    up = np.concatenate([a["L1_ffn_experts_gate_up"], a["L1_ffn_shared_gate_up"][None]])
    down = np.concatenate([a["L1_ffn_experts_down"], a["L1_ffn_shared_down"][None]])
    log_a, c = a["L1_attn_log_A_diag"], a["L1_attn_C_w"]
    arrays = {
        "constants": host_constants(),
        "x_in": a["L0_attn_x"].reshape(TOK, D),
        "qkv_w": a["L0_attn_qkv_w"],
        "qk_bias": lay(a["L0_attn_qkv_b"][:2 * D].reshape(-1, P).T),
        "v_bias": lay(a["L0_attn_qkv_b"][2 * D:]),
        "out_w": a["L0_attn_out_w"],
        "out_b": a["L0_attn_out_b"],
        "up_t": lay(a["L0_ffn_w_up"].T),
        "down_t": lay(a["L0_ffn_w_down"].T),
        "log_a_t": lay(log_a.T),
        "c_t": lay(c.T),
        "log_a_blocks": lay(log_a.reshape(-1, P).T),
        "c_blocks": lay(c.reshape(-1, P).T),
        "b_t": lay(a["L1_attn_B_w"].T),
        "d_vec": a["L1_attn_D_vec"],
        "gate_t": lay(a["L1_ffn_gate_weight"].T),
        "w_up": lay(up.transpose(0, 2, 1)).reshape(-1, up.shape[1]),
        "w_down": lay(down.transpose(0, 2, 1)).reshape(-1, D),
    }
    nc = bacc.Bacc("TRN2", target_bir_lowering=False, num_devices=1)
    names = {n: nc.dram_tensor(f"in_{n}", v.shape, mybir.dt.from_np(v.dtype), kind="ExternalInput").ap()
             for n, v in arrays.items()}
    names["out"] = nc.dram_tensor("out", (TOK, D), F32, kind="ExternalOutput").ap()
    program(nc, names)
    result = run_bass_kernel_spmd(nc, [{f"in_{n}": v for n, v in arrays.items()}], core_ids=[0])
    return result.results[0]["out"].reshape(BATCH, SEQ, D)
```

```python
from contextlib import ExitStack

import numpy as np

import concourse.bass as bass
from concourse import mybir

F32 = mybir.dt.float32
FR = mybir.dt.float32r
BF16 = mybir.dt.bfloat16
ALU = mybir.AluOpType
ACT = mybir.ActivationFunctionType
AX = mybir.AxisListType

P = 128
BATCH, SEQ, D = 2, 2048, 256
TOK = BATCH * SEQ
TILES = TOK // P
CT = 512
TPC = CT // P
CHUNKS = TOK // CT
KD = D // P
H, HD = 16, 16
EPS = 1e-5
MASKED = -1e30

C_IDENT = 0
C_MASK_QK = 128
C_MASK_KQ = 256
C_SEL = 512
SELW = 18
C_NEG_TAU = 536
C_TAU_MASK = 540
C_STEP = 572
C_SAME_S = 604
C_SAME_G = 620
C_UPPER = 628
C_LEFT = 756
C_LIMITS = 764
C_TILE = 772
C_END = 804


def host_constants():
    c = np.zeros((P, C_END), np.float32)
    i = np.arange(P)
    c[:, C_IDENT:C_IDENT + P] = np.eye(P)
    c[:, C_MASK_QK:C_MASK_QK + P] = np.where(i[None, :] > i[:, None], MASKED, 0)
    c[:, C_MASK_KQ:C_MASK_KQ + P] = MASKED
    c[:, C_MASK_KQ + P:C_MASK_KQ + 2 * P] = np.where(i[:, None] > i[None, :], MASKED, 0)
    for j in range(HD + 1):
        c[i % 32 == j, C_SEL + j] = 1
    tau, s = i // NSTATE, i % NSTATE
    m, r = np.arange(MT), np.arange(T)
    c[:, C_NEG_TAU:C_NEG_TAU + MT] = -(TAUS * m[None, :] + tau[:, None])
    c[:, C_TAU_MASK:C_TAU_MASK + T] = r[None, :] >= tau[:, None]
    c[:, C_STEP:C_STEP + T] = -(r[None, :] + 1)
    c[:, C_SAME_S:C_SAME_S + NSTATE] = s[:, None] == np.arange(NSTATE)[None, :]
    c[:, C_SAME_G:C_SAME_G + TAUS] = tau[:, None] == np.arange(TAUS)[None, :]
    c[:, C_UPPER:C_UPPER + P] = i[:, None] < i[None, :]
    c[:, C_LEFT:C_LEFT + E] = E - np.arange(E)
    c[:, C_LIMITS:C_LIMITS + CHUNKS] = np.arange(CHUNKS) * CT
    c[:, C_TILE:C_TILE + ROUTED] = np.arange(ROUTED)
    return c


E, TOPK = 8, 2
ROUTED = (TOPK * TOK + E * (CT - 1)) // CT
NSTATE = 16
TAUS = P // NSTATE
T = 32
MT = T // TAUS
BLOCKS = TOK // T
DB = D // TAUS


START = 2


class Semaphores:

    def __init__(self, nc, ctx):
        self.nc, self.ctx, self.new = nc, ctx, []

    def __call__(self, name):
        self.new.append(self.ctx.enter_context(self.nc.semaphore(name)))
        return self.new[-1]

    def from_zero(self, name):
        return self.ctx.enter_context(self.nc.semaphore(name))

    def start(self):
        new, self.new = self.new, []
        with self.nc.Block() as block:
            @block.sync
            def _(sp):
                for s in new:
                    sp.sem_inc(s, START)


class Steps:

    def __init__(self, eng, sem, base=0):
        self.eng, self.sem, self.base, self.n = eng, sem, base, 0

    def add(self, instruction):
        instruction.then_inc(self.sem, 1)
        self.n += 1

    def last(self):
        self.eng.wait_ge(self.sem, self.base + self.n + START)


def on_its_own(eng, g):
    eng.sem_inc(g.passed, 1)


def product3(pe, out, wh, wl, xh, xl, start, stop):
    pe.matmul(out, wh, xh, start=start, stop=False)
    pe.matmul(out, wh, xl, start=False, stop=False)
    return pe.matmul(out, wl, xh, start=False, stop=stop)


def ds(start, size):
    return bass.ds(start, size)


class LayerNorm:

    def __init__(self, g, sb, sem, name):
        self.g = g
        self.stats = sb(name + "_stats", [P, TPC, 6])
        self.mv = sb(name + "_mv", [P, TPC, 2])
        self.sd = sb(name + "_sd", [P, TPC])
        self.rstd = sb(name + "_rstd", [P, TPC])
        self.spread_ready = sem(name + "_spread_ready")
        self.var_ready = sem(name + "_var_ready")
        self.sd_ready = sem(name + "_sd_ready")
        self.rstd_ready = sem(name + "_rstd_ready")
        self.ready = sem(name + "_ready")

    def spread(self, dve, c):
        on_its_own(dve, self.g)
        for j in range(TPC):
            dve.bn_stats(self.stats[:, j, :], self.g.x[:, ds(c * TPC + j, 1), :]).then_inc(self.spread_ready, 1)

    def variance(self, dve, c):
        dve.wait_ge(self.spread_ready, (c + 1) * TPC + START)
        dve.wait_ge(self.ready, c + START)
        on_its_own(dve, self.g)
        for j in range(TPC):
            last = dve.bn_aggr(self.mv[:, j, :], self.stats[:, j, :])
        last.then_inc(self.var_ready, 1)

    def deviation(self, act, c):
        act.wait_ge(self.var_ready, c + 1 + START)
        act.activation(self.sd[:, :], self.mv[:, :, 1], ACT.Sqrt, bias=self.g.eps[:, 0:1]).then_inc(self.sd_ready, 1)

    def invert(self, dve, c):
        dve.wait_ge(self.sd_ready, c + 1 + START)
        dve.reciprocal(self.rstd[:, :], self.sd[:, :]).then_inc(self.rstd_ready, 1)

    def normal(self, dve, c, out):
        dve.wait_ge(self.rstd_ready, c + 1 + START)
        for j in range(TPC):
            last = dve.tensor_scalar(out[:, j, :], self.g.x[:, ds(c * TPC + j, 1), :], self.mv[:, j, 0:1],
                                     self.rstd[:, j:j + 1], ALU.subtract, ALU.mult)
        last.then_inc(self.ready, 1)


def in_pairs(eng, first):
    with eng.Fori(0, CHUNKS // 2 - 1) as i:
        first(2 * i, 0)
        first(2 * i + 1, 1)
    first(CHUNKS - 2, 0)
    first(CHUNKS - 1, 1)


def there(c):
    return not isinstance(c, int) or c < CHUNKS


def phase_qkv(nc, top, g):
    with ExitStack() as ctx:
        sb = lambda name, shape, dt=F32: ctx.enter_context(nc.sbuf_tensor(name, shape, dt))
        pb = lambda name, shape, dt=F32: ctx.enter_context(nc.psum_tensor(name, shape, dt))
        sem = Semaphores(nc, ctx)
        NW = 3 * D
        w32 = sb("qkv_w32", [P, KD, NW])
        wh = sb("qkv_wh", [P, KD, NW], FR)
        wl = sb("qkv_wl", [P, KD, NW], FR)
        qk_bias = sb("qk_bias", [P, 4])
        v_bias = sb("v_bias", [P, D])
        ln = LayerNorm(g, sb, sem, "qkv_ln")
        xn = sb("qkv_xn", [P, TPC, D])
        xth = [sb(f"qkv_xth{u}", [P, KD, CT], FR) for u in range(2)]
        xtl = [sb(f"qkv_xtl{u}", [P, KD, CT], FR) for u in range(2)]
        qk32 = sb("qk32", [P, 2, CT])
        qkh = [sb(f"qkh{u}", [P, 4, CT], FR) for u in range(2)]
        qkl = [sb(f"qkl{u}", [P, 4, CT], FR) for u in range(2)]
        ps_t = pb("qkv_ps_t", [P, KD, CT])
        ps_qk = pb("ps_qk", [P, 2, CT])
        ps_v = pb("ps_v", [P, 2, CT])

        const_in = sem("const_in")
        w_in = sem("qkv_w_in")
        x_in = [sem(f"x_in{u}") for u in range(2)]
        w_hi = sem("qkv_w_hi")
        w_lo = sem("qkv_w_lo")
        const_bf = sem("const_bf")
        xt_ps = sem("qkv_xt_ps")
        xt_hi = sem("qkv_xt_hi")
        xt_lo = sem("qkv_xt_lo")
        qk_ps = sem("qk_ps")
        qk_f32 = sem("qk_f32")
        qk_hi = sem("qk_hi")
        qk_lo = sem("qk_lo")
        v_ps = sem("v_ps")
        v_ready = sem("v_ready")
        qk_out = [sem(f"qk_out{u}") for u in range(2)]

        sem.start()
        with nc.Block() as block:
            @block.sync
            def _(sp):
                def load_x(it, u, nth):
                    sp.wait_ge(x_in[u], nth * 16 + START)
                    sp.dma_start(g.x[:, ds(it * TPC, TPC), :],
                                 g.x_in[ds(it * CT, CT), :].rearrange("(t p) n -> p t n", p=P)).then_inc(x_in[u], 16)
                load_x(0, 0, 0)
                sp.dma_start(g.const[:, :], g.constants).then_inc(const_in, 16)
                sp.dma_start(w32[:, :, :], g.qkv_w.rearrange("(k p) n -> p k n", p=P)).then_inc(w_in, 16)
                load_x(1, 1, 0)
                sp.dma_start(qk_bias[:, :], g.qk_bias).then_inc(w_in, 16)
                sp.dma_start(v_bias[:, :], g.v_bias.rearrange("(o n) -> o n", o=1)
                             .broadcast_to([P, D])).then_inc(w_in, 16)
                with sp.Fori(1, CHUNKS // 2) as i:
                    for u in range(2):
                        load_x(2 * i + u, u, i)
                with sp.Fori(0, CHUNKS // 2) as i:
                    for u in range(2):
                        it = 2 * i + u
                        sp.wait_ge(qk_hi, it * 4 + 4 + START)
                        sp.wait_ge(qk_lo, it * 4 + 4 + START)
                        sp.dma_start(g.q_k_hi[:, ds(it * CT, CT)].rearrange("(m p) t -> p m t", p=P),
                                     qkh[u][:, :, :].bitcast(F32)).then_inc(qk_out[u], 16)
                        sp.dma_start(g.q_k_lo[:, ds(it * CT, CT)].rearrange("(m p) t -> p m t", p=P),
                                     qkl[u][:, :, :].bitcast(F32)).then_inc(qk_out[u], 16)
                for u in range(2):
                    sp.wait_ge(qk_out[u], CHUNKS // 2 * 32 + START)

            @block.vector
            def _(dve):
                def loaded(it, u):
                    dve.wait_ge(x_in[u], (it - u) * 8 + 16 + START)

                def low(it, u, m):
                    dve.wait_ge(qk_hi, it * 4 + m + 1 + START)
                    dve.tensor_tensor(qkl[u][:, m, :], qk32[:, m % 2, :], qkh[u][:, m, :].bitcast(F32), ALU.subtract)\
                       .then_inc(qk_lo, 1)

                def turned_low(c, u):
                    dve.wait_ge(xt_hi, c + 1 + START)
                    dve.tensor_tensor(xtl[u][:, :, :], ps_t[:, :, :], xth[u][:, :, :].bitcast(F32), ALU.subtract)\
                       .then_inc(xt_lo, 1)

                def norm(c, u):
                    loaded(c, u)
                    ln.spread(dve, c)
                    ln.variance(dve, c)
                    ln.invert(dve, c)
                    dve.wait_ge(xt_ps, c + START)
                    ln.normal(dve, c, xn)

                def step(it, u):
                    if there(it + 1):
                        turned_low(it + 1, 1 - u)
                    dve.wait_ge(qk_out[u], (it - u) * 16 + START)
                    ahead = there(it + 2)
                    if ahead:
                        loaded(it + 2, u)
                        ln.spread(dve, it + 2)
                    low(it, u, 0)
                    if ahead:
                        ln.variance(dve, it + 2)
                    low(it, u, 1)
                    low(it, u, 2)
                    low(it, u, 3)
                    if ahead:
                        ln.invert(dve, it + 2)
                    for j in range(TPC):
                        if j == 2 and ahead:
                            dve.wait_ge(xt_ps, it + 2 + START)
                            ln.normal(dve, it + 2, xn)
                        dve.wait_ge(v_ps, it * TPC + j + 1 + START)
                        dve.tensor_tensor(g.v[:, ds(it * TPC + j, 1), :], ps_v[:, j % 2, 0:D], v_bias[:, :], ALU.add)\
                           .then_inc(v_ready, 1)
                dve.memset(g.eps[:, :], EPS).then_inc(g.started, 1)
                norm(0, 0)
                dve.wait_ge(const_in, 16 + START)
                dve.tensor_copy(g.ident_bf[:, :], g.const[:, C_IDENT:C_IDENT + P]).then_inc(const_bf, 1)
                dve.tensor_copy(g.mask_bf[:, :], g.const[:, C_MASK_QK:C_MASK_QK + 3 * P]).then_inc(const_bf, 1)
                turned_low(0, 0)
                norm(1, 1)
                dve.wait_ge(w_hi, 1 + START)
                dve.tensor_tensor(wl[:, :, :], w32[:, :, :], wh[:, :, :].bitcast(F32), ALU.subtract).then_inc(w_lo, 1)
                in_pairs(dve, step)

            @block.scalar
            def _(act):
                def turned_high(c, u):
                    act.wait_ge(xt_ps, c + 1 + START)
                    if not isinstance(c, int) or c >= 2:
                        act.wait_ge(v_ps, (c - 1) * TPC + START)
                    act.activation(xth[u][:, :, :], ps_t[:, :, :], ACT.Copy).then_inc(xt_hi, 1)

                def high(it, u, m):
                    act.wait_ge(qk_f32, it * 4 + m + 1 + START)
                    act.activation(qkh[u][:, m, :], qk32[:, m % 2, :], ACT.Copy).then_inc(qk_hi, 1)

                def step(it, u):
                    if there(it + 1):
                        turned_high(it + 1, 1 - u)
                    act.wait_ge(qk_out[u], (it - u) * 16 + START)
                    for m in range(4):
                        act.wait_ge(qk_ps, it * 4 + m + 1 + START)
                        act.wait_ge(qk_lo, it * 4 + max(m - 1, 0) + START)
                        act.activation(qk32[:, m % 2, :], ps_qk[:, m % 2, :], ACT.Identity, bias=qk_bias[:, m:m + 1])\
                           .then_inc(qk_f32, 1)
                        if m:
                            high(it, u, m - 1)
                        if m == 1 and there(it + 2):
                            ln.deviation(act, it + 2)
                    high(it, u, 3)
                act.wait_ge(g.started, 1)
                ln.deviation(act, 0)
                turned_high(0, 0)
                ln.deviation(act, 1)
                act.wait_ge(w_in, 48 + START)
                act.activation(wh[:, :, :], w32[:, :, :], ACT.Copy).then_inc(w_hi, 1)
                in_pairs(act, step)

            @block.tensor
            def _(pe):
                def turn(c):
                    pe.wait_ge(ln.ready, c + 1 + START)
                    pe.wait_ge(xt_lo, c + START)
                    for k in range(KD):
                        for j in range(TPC):
                            last = pe.transpose(ps_t[:, k, j * P:(j + 1) * P], xn[:, j, k * P:(k + 1) * P],
                                                g.const[:, C_IDENT:C_IDENT + P])
                    last.then_inc(xt_ps, 1)

                def step(it, u):
                    if there(it + 1):
                        turn(it + 1)
                    else:
                        pe.wait_ge(xt_lo, it + 1 + START)
                    for m in range(4):
                        pe.wait_ge(qk_f32, it * 4 + max(m - 1, 0) + START)
                        for k in range(KD):
                            w = slice(m * P, (m + 1) * P)
                            last = product3(pe, ps_qk[:, m % 2, :], wh[:, k, w], wl[:, k, w], xth[u][:, k, :],
                                            xtl[u][:, k, :], k == 0, k == KD - 1)
                        last.then_inc(qk_ps, 1)
                    for j in range(TPC):
                        pe.wait_ge(v_ready, it * TPC + max(j - 1, 0) + START)
                        for k in range(KD):
                            t = slice(j * P, (j + 1) * P)
                            last = product3(pe, ps_v[:, j % 2, 0:D], xth[u][:, k, t], xtl[u][:, k, t],
                                            wh[:, k, 2 * D:], wl[:, k, 2 * D:], k == 0, k == KD - 1)
                        last.then_inc(v_ps, 1)
                pe.wait_ge(const_in, 16 + START)
                turn(0)
                pe.wait_ge(w_lo, 1 + START)
                in_pairs(pe, step)


TILES_OF = [(c, kt, 0 if kt < c * TPC + 2 else CT // 2) for c in range(4) for kt in range((c + 1) * TPC)]
MAXES = [(i, c, min(CT, (i + 1) * P - c * CT)) for i in range(SEQ // P) for c in range(i // TPC + 1)]
NT = len(TILES_OF)
assert NT == len(MAXES) and NT % TPC == 0
GROUPS = NT // TPC
CHUNK_END = [(c + 1) * (c + 2) // 2 - 1 for c in range(4)]
CHUNK_MAX_AT = {CHUNK_END[c] + 1: c for c in range(4)}
TURN_AT = {3: 0, 4: 1, 7: 2, GROUPS: 3}
O_AT = {CHUNK_END[c] + 1: c for c in range(4)}
SUMS_AT = {5: 0, 6: 1, 8: 2, GROUPS + 1: 3}
NORMALISE_AT = 2
PER_MAX = 2
HEADS = BATCH * H
STACK = 3 * HD
MROW = 96
SCALE = HD ** -0.5


def batch_head(n):
    return n // H, n % H


def phase_attention(nc, top, g):
    with ExitStack() as ctx:
        sb = lambda name, shape, dt=F32: ctx.enter_context(nc.sbuf_tensor(name, shape, dt))
        pb = lambda name, shape, dt=F32: ctx.enter_context(nc.psum_tensor(name, shape, dt))
        sem = Semaphores(nc, ctx)
        q_st = [sb(f"q_stack{u}", [P, SEQ], FR) for u in range(3)]
        k_st = [sb(f"k_stack{u}", [P, SEQ], FR) for u in range(3)]
        v_st = [sb(f"v_stack{u}", [P, SEQ // P, 32]) for u in range(3)]
        probs = sb("probs", [P, 2 * TPC, CT])
        maxes = sb("maxes", [P, SEQ // P, 4])
        mx = sb("mx", [P, SEQ // P])
        mh = sb("mh", [TPC, 4, P], FR)
        ml = sb("ml", [TPC, 4, P], FR)
        o_sb = sb("o_sb", [P, 2, CT])
        rden = sb("rden", [P, SEQ // P, 1])
        ones = sb("att_ones", [1, SEQ])
        onesr = sb("att_onesr", [1, SEQ], FR)
        zeros = sb("att_zeros", [P, CT])
        ps_m = pb("ps_m", [P, 3, CT])
        ps_s = pb("ps_s", [P, 3, CT])
        ps_o = pb("ps_o", [P, CT])
        ps_f = pb("ps_f", [P, CT])
        fin = ps_f[:, 0:SEQ // P * SELW].rearrange("p (t w) -> p t w", w=SELW)
        turned = ps_f[0:TPC, 384:512]

        init = sem("att_init")
        ones_r = sem("att_ones_r")
        ones_in = sem("att_ones_in")
        stack_in = [sem(f"stack_in{u}") for u in range(3)]
        v_in = sem("att_v_in")
        mrow_in = [sem(f"mrow_in{c}") for c in range(4)]
        zeroed = sem("att_zeroed")
        zero_rows = sem("att_zero_rows")
        max_ps = sem("max_ps")
        max_used = sem("max_used")
        chunk_max = sem("chunk_max")
        own = sem("att_dve_own")
        m_turned = sem("m_turned")
        m_hi = sem("m_hi")
        m_lo = sem("m_lo")
        s_ps = sem("s_ps")
        p_ready = sem("p_ready")
        pv_done = sem("pv_done")
        o_copied = sem("o_copied")
        fin_ps = sem("fin_ps")
        fin_used = sem("fin_used")

        def upto(n, per, k):
            return max(n * per + k, 0) if isinstance(n, int) else n * per + k

        def load_stacks(sp, n, u, done):
            sp.wait_ge(s_ps, done * NT + START)
            b, h = batch_head(n)
            rows_q, rows_k = ds(h * HD, HD), ds(h * HD + D, HD)
            t = ds(b * SEQ, SEQ)
            for dst, src in ((q_st[u][0:HD, :], g.q_k_hi[rows_q, t]), (q_st[u][HD:2 * HD, :], g.q_k_hi[rows_q, t]),
                             (q_st[u][2 * HD:STACK, :], g.q_k_lo[rows_q, t]), (k_st[u][0:HD, :], g.q_k_hi[rows_k, t]),
                             (k_st[u][HD:2 * HD, :], g.q_k_lo[rows_k, t]), (k_st[u][2 * HD:STACK, :], g.q_k_hi[rows_k, t])):
                sp.dma_start(dst.bitcast(F32), src).then_inc(stack_in[u], 16)

        def load_mrow(sp, n, u, c):
            sp.wait_ge(m_lo, n * 4 + c + 1 + START)
            for r, part in ((MROW, mh), (MROW + 1, ml)):
                sp.dma_start(q_st[u][r:r + 1, c * CT:(c + 1) * CT].bitcast(F32).rearrange("o (t p) -> o t p", p=P),
                             part[:, c, :].bitcast(F32)).then_inc(mrow_in[c], 16)

        LOADS = 6 * 16
        TRIPLES = (HEADS - 2) // 3
        sem.start()
        with nc.Block() as block:
            @block.sync
            def _(sp):
                sp.wait_ge(zeroed, 6 + START)
                sp.wait_ge(ones_r, 1 + START)
                for u in range(3):
                    for r in (MROW, MROW + 1):
                        sp.dma_start(k_st[u][r:r + 1, :].bitcast(F32), onesr[0:1, :].bitcast(F32)).then_inc(ones_in, 16)
                load_stacks(sp, 0, 0, 0)
                load_stacks(sp, 1, 1, 0)

                def step(n, u, last=None, next_up=None, done=None):
                    if last is not None:
                        load_mrow(sp, last, (u + 2) % 3, 3)
                    if next_up is not None:
                        load_stacks(sp, next_up, (u + 1) % 3, done)
                    for c in range(3):
                        load_mrow(sp, n, u, c)
                step(0, 0)
                step(1, 1, 0, 2, 0)
                with sp.Fori(0, TRIPLES - 1) as i:
                    for v in range(3):
                        step(3 * i + v + 2, (v + 2) % 3, 3 * i + v + 1, 3 * i + v + 3, 3 * i + v + 1)
                for n in range(HEADS - 3, HEADS):
                    step(n, n % 3, n - 1, n + 1 if n + 1 < HEADS else None, n - 1)
                load_mrow(sp, HEADS - 1, (HEADS - 1) % 3, 3)
                for c in range(4):
                    sp.wait_ge(mrow_in[c], HEADS * 32 + START)

            @block.gpsimd
            def _(pool):
                for u in range(3):
                    pool.memset(v_st[u][:, :, :], 0.0).then_inc(init, 1)
                pool.wait_ge(init, 3 + START)
                for u in range(3):
                    pool.memset(v_st[u][:, :, HD:HD + 1], 1.0).then_inc(init, 1)

                def stage_v(n, u, done):
                    pool.wait_ge(pv_done, done * GROUPS + START)
                    on_its_own(pool, g)
                    b, h = batch_head(n)
                    pool.tensor_copy(v_st[u][:, :, 0:HD], g.v[:, ds(b * (SEQ // P), SEQ // P), ds(h * HD, HD)])\
                        .then_inc(v_in, 1)
                stage_v(0, 0, 0)
                stage_v(1, 1, 0)
                with pool.Fori(0, TRIPLES) as i:
                    for v in range(3):
                        stage_v(3 * i + v + 2, (v + 2) % 3, 3 * i + v)

            @block.vector
            def _(dve):
                dve.memset(zeros[:, :], 0.0).then_inc(zero_rows, 1)
                dve.memset(ones[:, :], 1.0).then_inc(own, 1)
                dve.memset(maxes[:, :, :], -3e38).then_inc(own, 1)
                dve.memset(ps_o[:, :], 0.0).then_inc(own, 1)
                dve.wait_ge(own, 3 + START)
                dve.tensor_copy(onesr[:, :], ones[:, :]).then_inc(ones_r, 1)
                dve.wait_ge(zero_rows, 1 + START)
                for st in (*q_st, *k_st):
                    dve.tensor_copy(st[:, :].rearrange("p (c t) -> p c t", t=CT),
                                    zeros[:, :].rearrange("p (o t) -> p o t", o=1).broadcast_to([P, SEQ // CT, CT]))\
                       .then_inc(zeroed, 1)

                def maximum(n, u, x):
                    i, c, w = MAXES[x]
                    dve.wait_ge(max_ps, n * NT + x + 1 + START)
                    dve.reduce_max(maxes[:, i, c:c + 1], ps_m[:, (u + x) % 3, 0:w], AX.X).then_inc(max_used, PER_MAX)

                def chunk(n, c):
                    dve.wait_ge(max_used, (n * NT + (CHUNK_END[c] + 1) * TPC) * PER_MAX + START)
                    dve.wait_ge(m_turned, upto(n, 4, c - 3) + START)
                    dve.reduce_max(mx[:, c * TPC:(c + 1) * TPC], maxes[:, c * TPC:(c + 1) * TPC, :], AX.X)\
                       .then_inc(chunk_max, 1)

                def low(n, c):
                    dve.wait_ge(m_hi, n * 4 + c + 1 + START)
                    dve.scalar_tensor_tensor(out=ml[:, c, :], in0=turned, scalar=-1.0, in1=mh[:, c, :].bitcast(F32),
                                             op0=ALU.mult, op1=ALU.subtract).then_inc(m_lo, 1)

                def reciprocals(n):
                    dve.wait_ge(fin_ps, n * 4 + 4 + START)
                    dve.reciprocal(rden[:, :, :], fin[:, :, HD:HD + 1]).then_inc(own, 1)

                def normalise(n):
                    dve.wait_ge(own, n + 4 + START)
                    b, h = batch_head(n)
                    dve.tensor_tensor(g.att[:, ds(b * (SEQ // P), SEQ // P), ds(h * HD, HD)], fin[:, :, 0:HD],
                                      rden[:, :, :].broadcast_to([P, SEQ // P, HD]), ALU.mult).then_inc(fin_used, 1)

                def step(n, u, last=None, before_last=None):
                    for q in range(GROUPS):
                        for r in range(TPC):
                            if n is not None:
                                maximum(n, u, q * TPC + r)
                            if r == 0 and q == 0 and last is not None:
                                chunk(last, 3)
                            if r == 0 and q in CHUNK_MAX_AT and n is not None:
                                chunk(n, CHUNK_MAX_AT[q])
                            if r == 1 and q == NORMALISE_AT and before_last is not None:
                                reciprocals(before_last)
                        if q == NORMALISE_AT and before_last is not None:
                            normalise(before_last)
                        if q == 0 and last is not None:
                            low(last, 3)
                        if q in TURN_AT and n is not None:
                            low(n, TURN_AT[q])
                step(0, 0)
                step(1, 1, 0)
                with dve.Fori(0, TRIPLES) as i:
                    for v in range(3):
                        step(3 * i + v + 2, (v + 2) % 3, 3 * i + v + 1, 3 * i + v)
                step(None, HEADS % 3, HEADS - 1, HEADS - 2)
                reciprocals(HEADS - 1)
                normalise(HEADS - 1)

            @block.scalar
            def _(act):
                def high(n, c):
                    act.wait_ge(m_turned, n * 4 + c + 1 + START)
                    act.wait_ge(mrow_in[c], n * 32 + START)
                    act.activation(mh[:, c, :], turned, ACT.Copy, scale=-1.0).then_inc(m_hi, 1)

                def exp(n, u, t):
                    c, kt, q0 = TILES_OF[t]
                    act.wait_ge(s_ps, n * NT + t + 1 + START)
                    act.wait_ge(pv_done, upto(n, GROUPS, t // TPC - 1) + START)
                    act.activation(probs[:, t % (2 * TPC), q0:], ps_s[:, (u + t) % 3, q0:], ACT.Exp, scale=SCALE)\
                       .then_inc(p_ready, 1)

                def copy_o(n, c):
                    act.wait_ge(pv_done, n * GROUPS + CHUNK_END[c] + 1 + START)
                    act.wait_ge(fin_ps, upto(n, 4, c - 1) + START)
                    act.activation(o_sb[:, c % 2, :], ps_o[:, :], ACT.Copy).then_inc(o_copied, 1)

                def step(n, u, last, before_last=None):
                    for q in range(GROUPS):
                        if last is not None:
                            for t in range(q * TPC, (q + 1) * TPC):
                                exp(last, (u + 2) % 3, t)
                        if q == 0 and before_last is not None:
                            copy_o(before_last, 3)
                        if q in O_AT and last is not None:
                            copy_o(last, O_AT[q])
                        if q == 0 and last is not None:
                            high(last, 3)
                        if q in TURN_AT and n is not None:
                            high(n, TURN_AT[q])
                act.wait_ge(init, 6 + START)
                step(0, 0, None)
                step(1, 1, 0)
                with act.Fori(0, TRIPLES) as i:
                    for v in range(3):
                        step(3 * i + v + 2, (v + 2) % 3, 3 * i + v + 1, 3 * i + v)
                step(None, HEADS % 3, HEADS - 1, HEADS - 2)
                copy_o(HEADS - 1, 3)

            @block.tensor
            def _(pe):
                pe.wait_ge(ones_in, 6 * 16 + START)
                pe.wait_ge(init, 6 + START)
                pe.wait_ge(own, 3 + START)
                pe.wait_ge(zeroed, 6 + START)

                def scores_for_max(n, u, x):
                    i, c, w = MAXES[x]
                    diagonal = (i + 1) * P == c * CT + w
                    pe.wait_ge(max_used, upto(n, NT * PER_MAX, (x - 2) * PER_MAX) + START)
                    mm = pe.matmul(ps_m[:, (u + x) % 3, 0:w], q_st[u][0:MROW, i * P:(i + 1) * P],
                                   k_st[u][0:MROW, c * CT:c * CT + w], start=True, stop=not diagonal)
                    if diagonal:
                        mm = pe.matmul(ps_m[:, (u + x) % 3, w - P:w], g.ident_bf[:, :], g.mask_bf[:, 0:P],
                                       start=False, stop=True)
                    mm.then_inc(max_ps, 1)

                def turn(n, c, normalised):
                    pe.wait_ge(chunk_max, n * 4 + c + 1 + START)
                    pe.wait_ge(m_lo, n * 4 + c + START)
                    pe.wait_ge(fin_used, normalised + START)
                    pe.transpose(turned, mx[:, c * TPC:(c + 1) * TPC], g.const[:, C_IDENT:C_IDENT + P])\
                      .then_inc(m_turned, 1)

                def scores(n, u, t):
                    c, kt, q0 = TILES_OF[t]
                    out, diag = ps_s[:, (u + t) % 3], kt - c * TPC
                    pe.wait_ge(mrow_in[c], n * 32 + 32 + START)
                    pe.wait_ge(p_ready, upto(n, NT, t - 2) + START)
                    mm = pe.matmul(out[:, q0:], k_st[u][:, kt * P:(kt + 1) * P], q_st[u][:, c * CT + q0:(c + 1) * CT],
                                   start=True, stop=diag < 0)
                    if diag >= 0:
                        w = P * (1 + diag % 2)
                        mm = pe.matmul(out[:, q0:q0 + w], g.ident_bf[:, :], g.mask_bf[:, 3 * P - w:3 * P],
                                       start=False, stop=True)
                    mm.then_inc(s_ps, 1)

                def times_v(n, u, q):
                    pe.wait_ge(p_ready, n * NT + (q + 1) * TPC + START)
                    if TILES_OF[q * TPC][1] == 0:
                        pe.wait_ge(o_copied, n * 4 + TILES_OF[q * TPC][0] + START)
                    for t in range(q * TPC, (q + 1) * TPC):
                        c, kt, q0 = TILES_OF[t]
                        r = 32 * (kt % TPC)
                        mm = pe.matmul(ps_o[r:r + 32, q0:], v_st[u][:, kt, :], probs[:, t % (2 * TPC), q0:],
                                       start=kt < TPC, stop=kt >= c * TPC, tile_position=(0, r))
                    mm.then_inc(pv_done, 1)

                def sums(n, c, turned_read):
                    pe.wait_ge(o_copied, n * 4 + c + 1 + START)
                    pe.wait_ge(m_lo, turned_read + START)
                    if c == 0:
                        pe.wait_ge(fin_used, n + START)
                    for j in range(TPC):
                        rows = P // 2 if c == 0 and j < 2 else P
                        mm = pe.matmul(fin[:, c * TPC + j, :], o_sb[0:rows, c % 2, j * P:(j + 1) * P],
                                       g.const[0:rows, C_SEL:C_SEL + SELW], start=True, stop=True)
                    mm.then_inc(fin_ps, 1)

                def step(n, u, last, before_last=None, nth=0):
                    if n is not None:
                        pe.wait_ge(stack_in[u], (nth + 1) * LOADS + START)
                    if last is not None:
                        pe.wait_ge(v_in, last + 1 + START)
                    for q in range(GROUPS):
                        for r in range(TPC):
                            if r == TPC - 1 and q and last is not None:
                                times_v(last, (u + 2) % 3, q - 1)
                            if r == TPC - 1 and q == 0 and before_last is not None:
                                times_v(before_last, (u + 1) % 3, GROUPS - 1)
                            if last is not None:
                                scores(last, (u + 2) % 3, q * TPC + r)
                            if n is not None:
                                scores_for_max(n, u, q * TPC + r)
                        if q == 0 and last is not None:
                            turn(last, 3, 0 if before_last is None else before_last)
                        if q in TURN_AT and n is not None:
                            turn(n, TURN_AT[q], 0 if before_last is None else before_last + 1)
                        new = sum(at <= q for at in TURN_AT)
                        read = (lambda k: k * 4 + new) if n is not None else (lambda k: HEADS * 4)
                        if q + GROUPS in SUMS_AT and before_last is not None:
                            sums(before_last, SUMS_AT[q + GROUPS], read(n))
                        if q in SUMS_AT and last is not None:
                            sums(last, SUMS_AT[q], read(n))
                step(0, 0, None)
                step(1, 1, 0)
                with pe.Fori(0, TRIPLES) as i:
                    for v in range(3):
                        step(3 * i + v + 2, (v + 2) % 3, 3 * i + v + 1, 3 * i + v, i + (v + 2) // 3)
                step(None, HEADS % 3, HEADS - 1, HEADS - 2)
                times_v(HEADS - 1, (HEADS - 1) % 3, GROUPS - 1)
                sums(HEADS - 1, 3, HEADS * 4)


FF = 1024
KF = FF // P


def phase_ffn(nc, top, g):
    with ExitStack() as ctx:
        sb = lambda name, shape, dt=F32: ctx.enter_context(nc.sbuf_tensor(name, shape, dt))
        pb = lambda name, shape, dt=F32: ctx.enter_context(nc.psum_tensor(name, shape, dt))
        sem = Semaphores(nc, ctx)
        ow32 = sb("ow32", [P, KD, D])
        owh = sb("owh", [P, KD, D], FR)
        owl = sb("owl", [P, KD, D], FR)
        ob = sb("ob", [P, D])
        hf = sb("ffn_h", [P, KF, CT])
        raw = hf[:, :, :].rearrange("p k n -> p (k n)")
        up32 = raw[:, 0:KD * FF].rearrange("p (k n) -> p k n", n=FF)
        dn32 = raw[:, KD * FF:KD * FF + KF * D].rearrange("p (k n) -> p k n", n=D)
        up = sb("up_ternary", [P, KD, FF], FR)
        dn = sb("dn_ternary", [P, KF, D], FR)
        absum = sb("absum", [P, 2])
        alpha = sb("alpha", [P, 2])
        alpha_neg = sb("alpha_neg", [P, 2])
        att_st = sb("att_st", [P, TPC, D])
        ones = sb("ffn_ones", [P, P])
        stats = sb("ffn_stats", [P, TPC, 6])
        mv = sb("ffn_mv", [P, TPC, 2])
        sd = sb("ffn_sd", [P, TPC])
        xn = sb("ffn_xn", [P, TPC, D])
        sv = sb("ffn_sv", [P, TPC])
        rr = sb("ffn_rr", [P, TPC])
        ath = sb("ffn_ath", [P, KD, CT], FR)
        atl = sb("ffn_atl", [P, KD, CT], FR)
        hrms = sb("ffn_hrms", [P, TPC])
        hrr = sb("ffn_hrr", [P, TPC])
        th = sb("ffn_th", [P, KD, CT], FR)
        tl = sb("ffn_tl", [P, KD, CT], FR)
        hh = sb("ffn_hh", [P, KF, CT], FR)
        hl = sb("ffn_hl", [P, KF, CT], FR)
        below = g.v[:, 0:KD * FF // D, :].rearrange("p t n -> p (t n)")
        ps_t = pb("ffn_ps_t", [P, KD, CT])
        ps_y = pb("ffn_ps_y", [P, TPC, D])
        ps_u = pb("ffn_ps_u", [P, 2, CT])
        ps_r = pb("ffn_ps_r", [P, CT])

        ow_in = sem("ow_in")
        w_in = sem("ffn_w_in")
        setup = sem("ffn_setup")
        ones_ready = sem("ffn_ones_ready")
        ow_hi = sem("ow_hi")
        ow_lo = sem("ow_lo")
        al_ps = sem("alpha_ps")
        own_front = sem("ffn_own_front")
        own_back = sem("ffn_own_back")
        staged = sem("att_staged")
        biased = sem("ffn_biased")
        at_ps = sem("at_turned")
        at_hi = sem("at_hi")
        at_lo = sem("at_lo")
        y_ps = sem("proj_ps")
        y_read = sem("proj_read")
        var_ready = sem("ffn_var_ready")
        sd_ready = sem("ffn_sd_ready")
        rr_ready = sem("ffn_rr_ready")
        xn_ready = sem("ffn_xn_ready")
        xt_ps = sem("ffn_xt_turned")
        xt_hi = sem("ffn_xt_hi")
        xt_lo = sem("ffn_xt_lo")
        u_ps = sem("up_ps")
        h_ready = sem("h_ready")
        h_hi = sem("h_hi")
        h_lo = sem("h_lo")
        h_sq = sem("h_sq")
        r_ps = sem("h_sumsq_ps")
        hrms_ready = sem("hrms_ready")
        dn_ps = sem("dn_ps")
        x_done = sem("ffn_x_done")

        EARLY = 3
        sem.start()
        with nc.Block() as block:
            @block.sync
            def _(sp):
                def stage(a):
                    sp.wait_ge(at_ps, a + START)
                    sp.dma_start(att_st[:, :, :], g.att[:, ds(a * TPC, TPC), :]).then_inc(staged, 16)
                sp.dma_start(ow32[:, :, :], g.out_w.rearrange("(k p) n -> p k n", p=P)).then_inc(ow_in, 16)
                sp.dma_start(ob[:, :], g.out_b.rearrange("(o n) -> o n", o=1).broadcast_to([P, D])).then_inc(ow_in, 16)
                stage(0)
                sp.dma_start(up32[:, :, :], g.up_t.rearrange("(k p) n -> p k n", p=P)).then_inc(w_in, 16)
                sp.dma_start(dn32[:, :, :], g.down_t.rearrange("(k p) n -> p k n", p=P)).then_inc(w_in, 16)
                with sp.Fori(1, CHUNKS) as a:
                    stage(a)

            @block.gpsimd
            def _(pool):
                pool.memset(ones[:, :], 1.0).then_inc(ones_ready, 1)
                pool.wait_ge(ow_in, 32 + START)

                def add_bias(a):
                    xs = g.x[:, ds(a * TPC, TPC), :]
                    pool.tensor_tensor(xs, xs, ob[:, :].rearrange("p (o n) -> p o n", o=1)
                                       .broadcast_to([P, TPC, D]), ALU.add).then_inc(biased, 1)

                def squares(b):
                    for m in range(KF):
                        pool.wait_ge(h_hi, b * KF + m + 1 + START)
                        pool.wait_ge(h_lo, b * KF + m + 1 + START)
                        pool.tensor_tensor(hf[:, m, :], hf[:, m, :], hf[:, m, :], ALU.mult).then_inc(h_sq, 1)
                        if m:
                            pool.wait_ge(h_sq, b * (2 * KF - 1) + 2 * m + START)
                            pool.tensor_tensor(hf[:, 0, :], hf[:, 0, :], hf[:, m, :], ALU.add).then_inc(h_sq, 1)
                add_bias(0)
                add_bias(1)
                with pool.Fori(0, CHUNKS - 2) as b:
                    squares(b)
                    add_bias(b + 2)
                squares(CHUNKS - 2)
                squares(CHUNKS - 1)

            @block.vector
            def _(dve):
                dve.wait_ge(ow_hi, 1 + START)
                dve.tensor_tensor(owl[:, :, :], ow32[:, :, :], owh[:, :, :].bitcast(F32), ALU.subtract).then_inc(ow_lo, 1)

                def low(b, m):
                    dve.wait_ge(h_hi, b * KF + m + 1 + START)
                    dve.tensor_tensor(hl[:, m, :], hf[:, m, :], hh[:, m, :].bitcast(F32), ALU.subtract)\
                       .then_inc(h_lo, 1)

                def attention_low(a):
                    dve.wait_ge(at_hi, a + 1 + START)
                    dve.tensor_tensor(atl[:, :, :], ps_t[:, :, :], ath[:, :, :].bitcast(F32), ALU.subtract)\
                       .then_inc(at_lo, 1)

                KA, KB = TPC + 1, 2

                def step(a=None, b=None, ahead=None):
                    if a is not None:
                        st = Steps(dve, own_front, a * KA)
                        xs = g.x[:, ds(a * TPC, TPC), :]
                    if b is not None:
                        dve.wait_ge(dn_ps, b * TPC + START)
                        for m in range(EARLY):
                            low(b, m)
                    if a is not None:
                        dve.wait_ge(biased, a + 1 + START)
                        dve.wait_ge(y_ps, a + 1 + START)
                        dve.tensor_tensor(xs, xs, ps_y[:, :, :], ALU.add).then_inc(y_read, 1)
                    if b is not None:
                        low(b, EARLY)
                    if a is not None:
                        dve.wait_ge(y_read, a + 1 + START)
                        on_its_own(dve, g)
                        for j in range(TPC):
                            st.add(dve.bn_stats(stats[:, j, :], g.x[:, ds(a * TPC + j, 1), :]))
                    if b is not None:
                        low(b, EARLY + 1)
                    if a is not None:
                        st.last()
                        on_its_own(dve, g)
                        for j in range(TPC):
                            last = dve.bn_aggr(mv[:, j, :], stats[:, j, :])
                        last.then_inc(var_ready, 1)
                    if b is not None:
                        for m in range(EARLY + 2, KF):
                            low(b, m)
                    if a is not None:
                        dve.wait_ge(sd_ready, (a + 1) * 2 + START)
                        st.add(dve.scalar_tensor_tensor(out=rr[:, :], in0=sd[:, :], scalar=1e-8, in1=sv[:, :],
                                                        op0=ALU.mult, op1=ALU.add))
                        st.last()
                        dve.reciprocal(rr[:, :], rr[:, :]).then_inc(rr_ready, 1)
                        dve.wait_ge(rr_ready, a + 1 + START)
                        for j in range(TPC):
                            last = dve.tensor_scalar(xn[:, j, :], g.x[:, ds(a * TPC + j, 1), :], mv[:, j, 0:1],
                                                     rr[:, j:j + 1], ALU.subtract, ALU.mult)
                        last.then_inc(xn_ready, 1)
                        assert st.n == KA
                        dve.wait_ge(xt_hi, a + 1 + START)
                        dve.tensor_tensor(tl[:, :, :], ps_t[:, :, :], th[:, :, :].bitcast(F32), ALU.subtract)\
                           .then_inc(xt_lo, 1)
                    if ahead is not None:
                        attention_low(ahead)
                    if b is not None:
                        st = Steps(dve, own_back, b * KB)
                        dve.wait_ge(hrms_ready, b + 1 + START)
                        st.add(dve.tensor_scalar(hrr[:, :], hrms[:, :], 1e-8, None, ALU.add))
                        st.last()
                        st.add(dve.reciprocal(hrr[:, :], hrr[:, :]))
                        st.last()
                        for j in range(TPC):
                            xj = g.x[:, ds(b * TPC + j, 1), :]
                            dve.wait_ge(dn_ps, b * TPC + j // 2 * 2 + 2 + START)
                            dve.scalar_tensor_tensor(out=xj, in0=ps_y[:, j:j + 1, :], scalar=hrr[:, j:j + 1], in1=xj,
                                                     op0=ALU.mult, op1=ALU.add).then_inc(x_done, 1)
                        assert st.n == KB
                attention_low(0)
                step(a=0, ahead=1)
                dve.wait_ge(w_in, 32 + START)
                s = Steps(dve, setup)
                s.add(dve.tensor_reduce(absum[:, 0:1], up32[:, :, :], AX.XY, ALU.add, apply_absolute_value=True))
                s.add(dve.tensor_reduce(absum[:, 1:2], dn32[:, :, :], AX.XY, ALU.add, apply_absolute_value=True))
                dve.wait_ge(al_ps, 1 + START)
                s.add(dve.tensor_scalar(alpha[:, :], ps_r[:, 0:2], 1.0 / (D * FF), 0.5, ALU.mult, ALU.mult))
                s.last()
                s.add(dve.tensor_scalar(alpha_neg[:, :], alpha[:, :], -1.0, None, ALU.mult))
                s.last()
                for i, (src, dst) in enumerate(((up32, up), (dn32, dn))):
                    t = below.rearrange("p (k n) -> p k n", n=src.shape[2])
                    s.add(dve.tensor_scalar(t, src[:, :, :], alpha_neg[:, i:i + 1], None, ALU.is_lt))
                    s.last()
                    s.add(dve.scalar_tensor_tensor(out=dst[:, :, :], in0=src[:, :, :], scalar=alpha[:, i:i + 1],
                                                   in1=t, op0=ALU.is_gt, op1=ALU.subtract))
                    s.last()
                assert s.n == FFN_SETUP
                with dve.Fori(0, CHUNKS - 2) as b:
                    step(b + 1, b, b + 2)
                step(CHUNKS - 1, CHUNKS - 2)
                step(b=CHUNKS - 1)

            @block.scalar
            def _(act):
                act.wait_ge(ow_in, 32 + START)
                act.activation(owh[:, :, :], ow32[:, :, :], ACT.Copy).then_inc(ow_hi, 1)

                def gelu(b, m):
                    act.wait_ge(u_ps, b * KF + m + 1 + START)
                    act.activation(hf[:, m, :], ps_u[:, m % 2, :], ACT.Gelu).then_inc(h_ready, 1)

                def high(b, m):
                    act.wait_ge(h_ready, b * KF + m + 1 + START)
                    act.activation(hh[:, m, :], hf[:, m, :], ACT.Copy).then_inc(h_hi, 1)

                def attention_high(a):
                    act.wait_ge(at_ps, a + 1 + START)
                    act.wait_ge(y_ps, a + START)
                    act.activation(ath[:, :, :], ps_t[:, :, :], ACT.Copy).then_inc(at_hi, 1)

                def step(a=None, b=None, ahead=None):
                    if b is not None:
                        act.wait_ge(r_ps, b + START)
                        act.wait_ge(dn_ps, b * TPC + START)
                        for m in range(KF):
                            gelu(b, m)
                            if m:
                                high(b, m - 1)
                        high(b, KF - 1)
                    if a is not None:
                        act.wait_ge(var_ready, a + 1 + START)
                        act.activation(sd[:, :], mv[:, :, 1], ACT.Sqrt, bias=g.eps[:, 0:1]).then_inc(sd_ready, 1)
                        act.activation(sv[:, :], mv[:, :, 1], ACT.Sqrt).then_inc(sd_ready, 1)
                        act.wait_ge(xt_ps, a + 1 + START)
                        if b is not None:
                            act.wait_ge(u_ps, (b + 1) * KF + START)
                        act.activation(th[:, :, :], ps_t[:, :, :], ACT.Copy).then_inc(xt_hi, 1)
                    if ahead is not None:
                        attention_high(ahead)
                    if b is not None:
                        act.wait_ge(r_ps, b + 1 + START)
                        act.activation(hrms[:, :], ps_r[:, 0:TPC], ACT.Sqrt, scale=1.0 / FF).then_inc(hrms_ready, 1)
                attention_high(0)
                step(a=0, ahead=1)
                act.wait_ge(setup, FFN_SETUP + START)
                with act.Fori(0, CHUNKS - 2) as b:
                    step(b + 1, b, b + 2)
                step(CHUNKS - 1, CHUNKS - 2)
                step(b=CHUNKS - 1)

            @block.tensor
            def _(pe):
                ident = g.const[:, C_IDENT:C_IDENT + P]

                def turn(src, ready):
                    for k in range(KD):
                        for j in range(TPC):
                            last = pe.transpose(ps_t[:, k, j * P:(j + 1) * P], src[:, j, k * P:(k + 1) * P], ident)
                    last.then_inc(ready, 1)

                def project(a, b):
                    pe.wait_ge(at_lo, a + 1 + START)
                    if b is not None:
                        pe.wait_ge(x_done, b * TPC + START)
                    for j in range(TPC):
                        for k in range(KD):
                            t = slice(j * P, (j + 1) * P)
                            last = product3(pe, ps_y[:, j, :], ath[:, k, t], atl[:, k, t], owh[:, k, :], owl[:, k, :],
                                            k == 0, k == KD - 1)
                    last.then_inc(y_ps, 1)

                def up_product(b, m):
                    pe.wait_ge(h_ready, b * KF + max(m - 1, 0) + START)
                    w = slice(m * P, (m + 1) * P)
                    for k in range(KD):
                        pe.matmul(ps_u[:, m % 2, :], up[:, k, w], th[:, k, :], start=k == 0, stop=False)
                        last = pe.matmul(ps_u[:, m % 2, :], up[:, k, w], tl[:, k, :], start=False, stop=k == KD - 1)
                    last.then_inc(u_ps, 1)

                def down_product(b, j):
                    t = slice(j * P, (j + 1) * P)
                    for m in range(KF):
                        if j == 0:
                            pe.wait_ge(h_lo, b * KF + m + 1 + START)
                        pe.matmul(ps_y[:, j, :], hh[:, m, t], dn[:, m, :], start=m == 0, stop=False)
                        last = pe.matmul(ps_y[:, j, :], hl[:, m, t], dn[:, m, :], start=False, stop=m == KF - 1)
                    last.then_inc(dn_ps, 1)

                def sums_of_squares(b):
                    pe.wait_ge(h_sq, (b + 1) * (2 * KF - 1) + START)
                    pe.wait_ge(hrms_ready, b + START)
                    for j in range(TPC):
                        last = pe.matmul(ps_r[:, j:j + 1], hf[:, 0, j * P:(j + 1) * P], ones[:, 0:1],
                                         start=True, stop=True)
                    last.then_inc(r_ps, 1)

                def turn_attention(a):
                    pe.wait_ge(staged, (a + 1) * 16 + START)
                    pe.wait_ge(xt_lo, a + START)
                    turn(att_st, at_ps)

                def step(a=None, b=None, ahead=None):
                    if b is not None:
                        pe.wait_ge(xt_lo, b + 1 + START)
                        for m in range(EARLY):
                            up_product(b, m)
                    if a is not None:
                        project(a, b)
                    if b is not None:
                        for m in range(EARLY, KF):
                            up_product(b, m)
                        if a is not None:
                            pe.wait_ge(y_read, a + 1 + START)
                        for j in range(TPC - 1):
                            down_product(b, j)
                    if a is not None:
                        pe.wait_ge(xn_ready, a + 1 + START)
                        pe.wait_ge(at_lo, a + 1 + START)
                        turn(xn, xt_ps)
                    if b is not None:
                        down_product(b, TPC - 1)
                    if ahead is not None:
                        turn_attention(ahead)
                    if b is not None:
                        sums_of_squares(b)
                turn_attention(0)
                pe.wait_ge(ow_lo, 1 + START)
                step(a=0, ahead=1)
                pe.wait_ge(ones_ready, 1 + START)
                pe.wait_ge(setup, 2 + START)
                pe.matmul(ps_r[:, 0:2], ones[:, :], absum[:, :], start=True, stop=True).then_inc(al_ps, 1)
                pe.wait_ge(setup, FFN_SETUP + START)
                with pe.Fori(0, CHUNKS - 2) as b:
                    step(b + 1, b, b + 2)
                step(CHUNKS - 1, CHUNKS - 2)
                step(b=CHUNKS - 1)


FFN_SETUP = 8


def phase_ssm(nc, top, g):
    with ExitStack() as ctx:
        sb = lambda name, shape, dt=F32: ctx.enter_context(nc.sbuf_tensor(name, shape, dt))
        pb = lambda name, shape, dt=F32: ctx.enter_context(nc.psum_tensor(name, shape, dt))
        sem = Semaphores(nc, ctx)
        rate8 = sb("rate8", [P, D])
        c8 = sb("c8", [P, D])
        rate_b = sb("rate_b", [P, DB])
        c_b = sb("c_b", [P, DB])
        b_raw = sb("b_raw", [P, KD, NSTATE])
        b8 = sb("b8", [P, KD, TAUS, NSTATE])
        dvec = sb("dvec", [P, D])
        powers = sb("powers", [P, MT, D])
        taps = sb("taps", [P, MT, D])
        carry = sb("carry", [P, DB, T])
        decay = sb("decay", [P, DB])
        NBB = BLOCKS // BATCH
        SLOTS = NBB + 1
        scan_a = sb("scan_a", [P, DB, BATCH, SLOTS])
        states = sb("states", [P, DB, BATCH, SLOTS])
        inputs = scan_a[:, :, :, :].rearrange("p a b c -> p (a b c)")[:, 0:TOK]
        shifted = sb("shifted", [P, TOK])
        ln = LayerNorm(g, sb, sem, "ssm_ln")
        xn = [sb(f"ssm_xn{u}", [P, TPC, D]) for u in range(2)]
        xt = sb("ssm_xt", [P, KD, CT])
        ident = g.const[:, C_IDENT:C_IDENT + P]
        ps_t = pb("ssm_ps_t", [P, KD, CT])
        ps_b = pb("ssm_ps_b", [P, 2, CT])
        ps_f = pb("ssm_ps_f", [P, 2 * TPC, D])

        w_in = sem("ssm_w_in")
        rates = sem("ssm_rates")
        b_ready = sem("ssm_b_ready")
        direct = sem("ssm_direct")
        xt_ps = sem("ssm_xt_ps")
        xt_ready = sem("ssm_xt_ready")
        in_ps = sem("ssm_in_ps")
        in_ready = sem("ssm_in_ready")
        shift_in = sem("ssm_shift_in")

        sem.start()
        with nc.Block() as block:
            @block.sync
            def _(sp):
                for t in range(TAUS):
                    rows = slice(t * NSTATE, (t + 1) * NSTATE)
                    sp.dma_start(rate8[rows, :], g.log_a_t).then_inc(w_in, 16)
                    sp.dma_start(c8[rows, :], g.c_t).then_inc(w_in, 16)
                sp.dma_start(rate_b[:, :], g.log_a_blocks).then_inc(w_in, 16)
                sp.dma_start(c_b[:, :], g.c_blocks).then_inc(w_in, 16)
                sp.dma_start(b_raw[:, :, :], g.b_t.rearrange("(k p) s -> p k s", p=P)).then_inc(w_in, 16)
                sp.dma_start(dvec[:, :], g.d_vec.rearrange("(o n) -> o n", o=1).broadcast_to([P, D])).then_inc(w_in, 16)
                sp.wait_ge(in_ready, CHUNKS + START)
                sp.wait_ge(b_ready, 3 + START)
                for t in range(TAUS):
                    rows = slice(t * NSTATE, (t + 1) * NSTATE)
                    sp.dma_start(shifted[rows, t:TOK], inputs[rows, 0:TOK - t]).then_inc(shift_in, 16)
                sp.wait_ge(shift_in, TAUS * 16 + START)

            @block.vector
            def _(dve):
                dve.memset(shifted[:, 0:TAUS], 0.0).then_inc(b_ready, 1)
                dve.wait_ge(w_in, 16 * (2 * TAUS + 4) + START)
                for k in range(KD):
                    dve.tensor_copy(b8[:, k, :, :], b_raw[:, k:k + 1, :].broadcast_to([P, TAUS, NSTATE])).then_inc(b_ready, 1)
                dve.wait_ge(rates, 3 + START)
                dve.tensor_tensor(carry[:, :, :], rate_b[:, :].rearrange("p (b o) -> p b o", o=1).broadcast_to([P, DB, T]),
                                  g.const[:, C_STEP:C_STEP + T].rearrange("p (o r) -> p o r", o=1)
                                  .broadcast_to([P, DB, T]), ALU.mult).then_inc(rates, 1)

                def norm(c, u):
                    ln.spread(dve, c)
                    ln.variance(dve, c)
                    ln.invert(dve, c)
                    if not isinstance(c, int) or c >= 2:
                        dve.wait_ge(xt_ps, c - 1 + START)
                        dve.wait_ge(direct, (c - 1) * 2 + START)
                    ln.normal(dve, c, xn[u])

                def step(it, u):
                    if there(it + 2):
                        norm(it + 2, u)
                    dve.wait_ge(in_ps, it + 1 + START)
                    dve.tensor_copy(inputs[:, ds(it * CT, CT)], ps_b[:, u, :]).then_inc(in_ready, 1)
                norm(0, 0)
                norm(1, 1)
                in_pairs(dve, step)

            @block.gpsimd
            def _(pool):
                def step(it, u):
                    pool.wait_ge(ln.ready, it + 1 + START)
                    pool.wait_ge(w_in, 16 * (2 * TAUS + 4) + START)
                    xs = g.x[:, ds(it * TPC, TPC), :]
                    pool.wait_ge(xt_ps, it + 1 + START)
                    pool.tensor_tensor(xn[u][:, :, :], xn[u][:, :, :], dvec[:, :].rearrange("p (o d) -> p o d", o=1)
                                       .broadcast_to([P, TPC, D]), ALU.mult).then_inc(direct, 1)
                    pool.wait_ge(direct, it * 2 + 1 + START)
                    pool.tensor_tensor(xs, xs, xn[u][:, :, :], ALU.add).then_inc(direct, 1)
                in_pairs(pool, step)

            @block.scalar
            def _(act):
                act.wait_ge(w_in, 16 * (2 * TAUS + 4) + START)
                act.activation(rate8[:, :], rate8[:, :], ACT.Exp).then_inc(rates, 1)
                act.activation(rate_b[:, :], rate_b[:, :], ACT.Exp).then_inc(rates, 1)
                act.wait_ge(rates, 2 + START)
                act.activation(decay[:, :], rate_b[:, :], ACT.Exp, scale=-float(T)).then_inc(rates, 1)
                for m in range(MT):
                    act.activation(powers[:, m, :], rate8[:, :], ACT.Exp,
                                   scale=g.const[:, C_NEG_TAU + m:C_NEG_TAU + m + 1])
                act.wait_ge(rates, 4 + START)
                act.activation(carry[:, :, :], carry[:, :, :], ACT.Exp).then_inc(rates, 1)

                def keep(c):
                    act.wait_ge(xt_ps, c + 1 + START)
                    act.wait_ge(in_ps, c + START)
                    act.activation(xt[:, :, :], ps_t[:, :, :], ACT.Copy).then_inc(xt_ready, 1)

                def step(it, u):
                    if there(it + 2):
                        ln.deviation(act, it + 2)
                    if there(it + 1):
                        keep(it + 1)
                ln.deviation(act, 0)
                ln.deviation(act, 1)
                keep(0)
                in_pairs(act, step)

            @block.tensor
            def _(pe):
                def turn(c, u):
                    pe.wait_ge(ln.ready, c + 1 + START)
                    pe.wait_ge(xt_ready, c + START)
                    for k in range(KD):
                        for j in range(TPC):
                            last = pe.transpose(ps_t[:, k, j * P:(j + 1) * P], xn[u][:, j, k * P:(k + 1) * P], ident)
                    last.then_inc(xt_ps, 1)

                def step(it, u):
                    pe.wait_ge(xt_ready, it + 1 + START)
                    pe.wait_ge(in_ready, it - 1 + START)
                    for k in range(KD):
                        last = pe.matmul(ps_b[:, u, :], b8[:, k, :, :], xt[:, k, :], start=k == 0, stop=k == KD - 1)
                    last.then_inc(in_ps, 1)
                    if there(it + 1):
                        turn(it + 1, 1 - u)
                pe.wait_ge(b_ready, 3 + START)
                turn(0, 0)
                in_pairs(pe, step)

        powers_s = [sb(f"powers_s{u}", [P, MT, TAUS, NSTATE]) for u in range(2)]
        tables = sem("ssm_tables")
        ps_ready = sem("powers_s_ready")
        end_ps = sem("end_ps")
        end_ready = sem("end_ready")
        scanned = sem("scanned")
        same_s = g.const[:, C_SAME_S:C_SAME_S + NSTATE].rearrange("p (a b s) -> p a b s", a=1, b=1)\
            .broadcast_to([P, MT, TAUS, NSTATE])
        sem.start()
        with nc.Block() as block:
            @block.gpsimd
            def _(pool):
                pool.tensor_copy(scan_a[:, :, :, :].rearrange("p a b c -> p a (b c)"),
                                 decay[:, :].rearrange("p (a o) -> p a o", o=1).broadcast_to([P, DB, BATCH * SLOTS]))\
                    .then_inc(tables, 1)
                pool.memset(states[:, :, :, 0:1], 0.0).then_inc(tables, 1)
                pool.wait_ge(tables, 1 + START)
                pool.memset(scan_a[:, :, :, 0:1], 0.0).then_inc(tables, 1)
                pool.tensor_tensor(taps[:, :, :], powers[:, :, :], c8[:, :].rearrange("p (o d) -> p o d", o=1)
                                   .broadcast_to([P, MT, D]), ALU.mult).then_inc(tables, 1)

            @block.vector
            def _(dve):
                with dve.Fori(0, DB // 2) as i:
                    for u in range(2):
                        dve.wait_ge(end_ps, 2 * i + u - 1 + START)
                        pw = powers[:, :, ds((2 * i + u) * TAUS, TAUS)].rearrange("p m (g o) -> p m g o", o=1)
                        dve.tensor_tensor(powers_s[u][:, :, :, :], pw.broadcast_to([P, MT, TAUS, NSTATE]), same_s,
                                          ALU.mult).then_inc(ps_ready, 1)
                dve.wait_ge(end_ready, DB + START)
                dve.wait_ge(tables, 4 + START)
                flat = lambda x: x[:, :, :, :].rearrange("p a b c -> p (a b c)")
                dve.tensor_tensor_scan(flat(states), flat(scan_a), flat(states), 0.0, ALU.mult, ALU.add)\
                    .then_inc(scanned, 1)

            @block.scalar
            def _(act):
                with act.Fori(0, DB // 2) as i:
                    for u in range(2):
                        act.wait_ge(end_ps, 2 * i + u + 1 + START)
                        act.activation(states[:, ds(2 * i + u, 1), :, 1:],
                                       ps_b[:, u, 0:BLOCKS].rearrange("p (o b c) -> p o b c", o=1, b=BATCH), ACT.Copy)\
                            .then_inc(end_ready, 1)

            @block.tensor
            def _(pe):
                ends = shifted[:, :].rearrange("p (c t) -> p c t", t=T)
                with pe.Fori(0, DB // 2) as i:
                    for u in range(2):
                        pe.wait_ge(ps_ready, 2 * i + u + 1 + START)
                        pe.wait_ge(end_ready, 2 * i + u - 1 + START)
                        for m in range(MT):
                            last = pe.matmul(ps_b[:, u, 0:BLOCKS], powers_s[u][:, m, :, :], ends[:, :, T - 1 - TAUS * m],
                                             start=m == 0, stop=m == MT - 1)
                        last.then_inc(end_ps, 1)

        diag = [sb(f"state_diag{u}", [P, TAUS, BATCH, NBB]) for u in range(2)]
        carry_c = [sb(f"carry_c{u}", [P, T]) for u in range(2)]
        diag_ready = sem("diag_ready")
        carry_ready = sem("carry_ready")
        inj_ps = sem("inj_ps")
        inj_ready = sem("inj_ready")
        QG = P // T
        sem.start()
        with nc.Block() as block:
            def diagonal(eng, d, u, w):
                st = states[:, ds(d, 1), :, 0:NBB]
                for b in range(BATCH):
                    last = eng.tensor_tensor(
                        diag[u][:, :, b, :], states[:, ds(d, 1), b, 0:NBB].broadcast_to([P, TAUS, NBB]),
                        g.const[:, C_SAME_G:C_SAME_G + TAUS].rearrange("p (g o) -> p g o", o=1)
                        .broadcast_to([P, TAUS, NBB]), ALU.mult)
                    last.then_inc(diag_ready, 1)

            @block.gpsimd
            def _(pool):
                with pool.Fori(0, DB // 2) as i:
                    for u in range(2):
                        pool.wait_ge(inj_ps, 2 * i + u - 1 + START)
                        pool.tensor_tensor(carry_c[u][:, :], carry[:, ds(2 * i + u, 1), :],
                                           c_b[:, ds(2 * i + u, 1)].broadcast_to([P, T]), ALU.mult)\
                            .then_inc(carry_ready, 1)

            @block.vector
            def _(dve):
                with dve.Fori(0, DB // 2) as i:
                    for u in range(2):
                        dve.wait_ge(inj_ps, 2 * i + u - 1 + START)
                        diagonal(dve, 2 * i + u, u, 0)

            @block.scalar
            def _(act):
                with act.Fori(0, DB // 2) as i:
                    for u in range(2):
                        act.wait_ge(inj_ps, 2 * i + u + 1 + START)
                        act.activation(g.att[:, :, ds((2 * i + u) * TAUS, TAUS)],
                                       ps_b[:, u, 0:D].rearrange("p (g t) -> p t g", g=TAUS), ACT.Copy)\
                            .then_inc(inj_ready, 1)

            @block.tensor
            def _(pe):
                with pe.Fori(0, DB // 2) as i:
                    for u in range(2):
                        pe.wait_ge(diag_ready, (2 * i + u + 1) * BATCH + START)
                        pe.wait_ge(carry_ready, 2 * i + u + 1 + START)
                        pe.wait_ge(inj_ready, 2 * i + u - 1 + START)
                        for q in range(QG):
                            rhs = diag[u][:, :, :, :].rearrange("p g b (t q) -> p (g b) t q", q=QG)[:, :, :, q]
                            last = pe.matmul(ps_b[q * T:(q + 1) * T, u, 0:D], carry_c[u][:, :], rhs, start=True,
                                             stop=True, tile_position=(0, q * T))
                        last.then_inc(inj_ps, 1)

        BPC = CT // T
        delayed = [sb(f"delayed{u}", [P, MT, BPC, T]) for u in range(2)]
        pad_zero = sem("pad_zero")
        pad_ready = sem("pad_ready")
        fir_ps = sem("fir_ps")
        x_own = sem("ssm_x_own")
        x_ready = sem("ssm_x_ready")
        sem.start()
        with nc.Block() as block:
            @block.gpsimd
            def _(pool):
                for u in range(2):
                    pool.memset(delayed[u][:, :, :, :], 0.0).then_inc(pad_zero, 1)
                pool.wait_ge(pad_zero, 2 + START)
                with pool.Fori(0, CHUNKS // 2) as i:
                    for u in range(2):
                        it = 2 * i + u
                        pool.wait_ge(fir_ps, it - 1 + START)
                        for m in range(MT):
                            n = T - TAUS * m
                            b = shifted[:, ds(it * CT, CT)].rearrange("p (c t) -> p c t", t=T)
                            pool.tensor_tensor(delayed[u][:, m, :, TAUS * m:], b[:, :, 0:n],
                                               g.const[:, C_TAU_MASK:C_TAU_MASK + n].rearrange("p (o t) -> p o t", o=1)
                                               .broadcast_to([P, BPC, n]), ALU.mult).then_inc(pad_ready, 1)

            @block.vector
            def _(dve):
                with dve.Fori(0, CHUNKS // 2) as i:
                    for u in range(2):
                        it = 2 * i + u
                        xs = g.x[:, ds(it * TPC, TPC), :]
                        dve.tensor_tensor(xs, xs, g.att[:, ds(it * TPC, TPC), :], ALU.add).then_inc(x_own, 1)
                        dve.wait_ge(x_own, it + 1 + START)
                        dve.wait_ge(fir_ps, it + 1 + START)
                        dve.tensor_tensor(xs, xs, ps_f[:, u * TPC:(u + 1) * TPC, :], ALU.add).then_inc(x_ready, 1)

            @block.tensor
            def _(pe):
                with pe.Fori(0, CHUNKS // 2) as i:
                    for u in range(2):
                        pe.wait_ge(pad_ready, (2 * i + u + 1) * MT + START)
                        pe.wait_ge(x_ready, 2 * i + u - 1 + START)
                        for j in range(TPC):
                            for m in range(MT):
                                w = delayed[u][:, m, j * QG:(j + 1) * QG, :]
                                last = pe.matmul(ps_f[:, u * TPC + j, :], w, taps[:, m, :], start=m == 0,
                                                 stop=m == MT - 1)
                        last.then_inc(fir_ps, 1)


FI = 938
KI = -(-FI // P)
FLAST = FI - (KI - 1) * P
RUNS = CHUNKS + ROUTED
SHARED = E
MOE_ROWS = ROUTED * CT


def fw(m):
    return P if m < KI - 1 else FLAST


def phase_moe(nc, top, g):
    slots_in = nc.dram_tensor("slots_in", (MOE_ROWS, D), F32, kind="Internal").ap()
    slots_out = nc.dram_tensor("slots_out", (MOE_ROWS, D), F32, kind="Internal").ap()
    with ExitStack() as ctx:
        sem = Semaphores(nc, ctx)
        keep = lambda name, shape, dt=F32: ctx.enter_context(nc.sbuf_tensor(name, shape, dt))
        slot = keep("slot", [P, TOPK, TILES], mybir.dt.int32)
        weight = keep("weight", [P, TOPK, TILES])
        experts = keep("experts", [P, ROUTED], mybir.dt.int32)
        logits = keep("logits", [P, TILES, E])
        moe_norm(nc, g, sem, slots_in, logits)
        moe_route(nc, g, sem, logits, slot, weight, experts)
        moe_experts(nc, g, sem, slots_in, slots_out, slot, experts)
        moe_combine(nc, g, sem, slots_out, slot, weight)


def moe_norm(nc, g, sem, slots_in, logits):
    with ExitStack() as ctx:
        sb = lambda name, shape, dt=F32: ctx.enter_context(nc.sbuf_tensor(name, shape, dt))
        pb = lambda name, shape, dt=F32: ctx.enter_context(nc.psum_tensor(name, shape, dt))
        gate = sb("gate", [P, KD, E])
        zero = sb("moe_zero", [P, TPC, D])
        ln = LayerNorm(g, sb, sem, "moe_ln")
        xn = [sb(f"moe_xn{u}", [P, TPC, D]) for u in range(2)]
        xt = sb("moe_xt", [P, KD, CT])
        ident = g.const[:, C_IDENT:C_IDENT + P]
        ps_t = pb("moe_ps_t", [P, KD, CT])
        ps_l = pb("moe_ps_l", [P, 2, CT])
        gate_in = sem("gate_in")
        zero_ready = sem("moe_zero_ready")
        zero_out = sem("moe_zero_out")
        kept = sem("moe_xn_kept")
        xt_ps = sem("moe_xt_ps")
        xt_ready = sem("moe_xt_ready")
        lg_ps = sem("logits_ps")
        lg_ready = sem("logits_ready")
        sem.start()
        with nc.Block() as block:
            @block.sync
            def _(sp):
                sp.dma_start(gate[:, :, :], g.gate_t.rearrange("(k p) e -> p k e", p=P)).then_inc(gate_in, 16)
                sp.wait_ge(zero_ready, 1 + START)
                with sp.Fori(0, ROUTED) as i:
                    sp.dma_start(slots_in[ds(i * CT, CT), :].rearrange("(p t) n -> p t n", p=P),
                                 zero[:, :, :]).then_inc(zero_out, 16)
                sp.wait_ge(zero_out, ROUTED * 16 + START)

            @block.gpsimd
            def _(pool):
                def step(it, u):
                    pool.wait_ge(ln.ready, it + 1 + START)
                    on_its_own(pool, g)
                    pool.tensor_copy(g.v[:, ds(it * TPC, TPC), :], xn[u][:, :, :]).then_inc(kept, 1)
                in_pairs(pool, step)

            @block.vector
            def _(dve):
                def norm(c, u):
                    ln.spread(dve, c)
                    ln.variance(dve, c)
                    ln.invert(dve, c)
                    if not isinstance(c, int) or c >= 2:
                        dve.wait_ge(xt_ps, c - 1 + START)
                        dve.wait_ge(kept, c - 1 + START)
                    ln.normal(dve, c, xn[u])

                def step(it, u):
                    if there(it + 2):
                        norm(it + 2, u)
                    dve.wait_ge(lg_ps, it + 1 + START)
                    dve.tensor_copy(logits[:, ds(it * TPC, TPC), :],
                                    ps_l[:, u, 0:TPC * E].rearrange("p (t e) -> p t e", e=E)).then_inc(lg_ready, 1)
                dve.memset(zero[:, :, :], 0.0).then_inc(zero_ready, 1)
                norm(0, 0)
                norm(1, 1)
                in_pairs(dve, step)

            @block.scalar
            def _(act):
                def keep(c):
                    act.wait_ge(xt_ps, c + 1 + START)
                    act.wait_ge(lg_ps, c + START)
                    act.activation(xt[:, :, :], ps_t[:, :, :], ACT.Copy).then_inc(xt_ready, 1)

                def step(it, u):
                    if there(it + 2):
                        ln.deviation(act, it + 2)
                    if there(it + 1):
                        keep(it + 1)
                ln.deviation(act, 0)
                ln.deviation(act, 1)
                keep(0)
                in_pairs(act, step)

            @block.tensor
            def _(pe):
                def turn(c, u):
                    pe.wait_ge(ln.ready, c + 1 + START)
                    pe.wait_ge(xt_ready, c + START)
                    for k in range(KD):
                        for j in range(TPC):
                            last = pe.transpose(ps_t[:, k, j * P:(j + 1) * P], xn[u][:, j, k * P:(k + 1) * P], ident)
                    last.then_inc(xt_ps, 1)

                def step(it, u):
                    pe.wait_ge(xt_ready, it + 1 + START)
                    pe.wait_ge(lg_ready, it - 1 + START)
                    for j in range(TPC):
                        for k in range(KD):
                            last = pe.matmul(ps_l[:, u, j * E:(j + 1) * E], xt[:, k, j * P:(j + 1) * P], gate[:, k, :],
                                             start=k == 0, stop=k == KD - 1)
                    last.then_inc(lg_ps, 1)
                    if there(it + 1):
                        turn(it + 1, 1 - u)
                pe.wait_ge(gate_in, 16 + START)
                turn(0, 0)
                in_pairs(pe, step)


def moe_route(nc, g, sem, logits, slot, weight, experts):
    with ExitStack() as ctx:
        sb = lambda name, shape, dt=F32: ctx.enter_context(nc.sbuf_tensor(name, shape, dt))
        pb = lambda name, shape, dt=F32: ctx.enter_context(nc.psum_tensor(name, shape, dt))
        ones = sb("rt_ones", [P, P])
        top_l = sb("top_logit", [P, TILES, 1])
        probs = sb("rt_probs", [P, TILES, E])
        psum_e = sb("rt_sum", [P, TILES, 1])
        score = sb("rt_score", [P, TILES, E])
        best = sb("rt_best", [P, TOPK, TILES, 1])
        place = sb("rt_place", [P, TILES, 1])
        chosen = sb("rt_chosen", [P, TOPK, TILES, E])
        member = sb("rt_member", [P, E, TILES])
        counts = sb("rt_counts", [P, E, TILES])
        keep_s = sb("rt_keep", [P, E, TILES])
        running = sb("rt_running", [P, E, TILES])
        where = sb("rt_where", [P, E, TILES])
        over = sb("rt_over", [P, E, CHUNKS])
        tiles = sb("rt_tiles", [P, E])
        tiles_upto = sb("rt_tiles_upto", [P, E])
        base = sb("rt_base", [P, E])
        past = sb("rt_past", [P, ROUTED, E])
        ex_f = sb("rt_experts", [P, ROUTED])
        slot_f = sb("rt_slot", [P, TOPK, TILES])
        denom = sb("rt_denom", [P, TILES])
        ps_rank = pb("ps_rank", [P, E, TILES])
        ps_count = pb("ps_count", [P, E, TILES])
        own = sem("rt_own")
        less_max = sem("rt_less_max")
        exp_done = sem("rt_exp_done")
        members = sem("rt_members")
        rank_ps = sem("rank_ps")
        slots = sem("rt_slots")
        sem.start()
        with nc.Block() as block:
            col = lambda a, w, n: g.const[:, a:a + w].rearrange("p (o e) -> p o e", o=1).broadcast_to([P, n, w])

            @block.vector
            def _(dve):
                st = Steps(dve, own)

                def do(instruction):
                    st.add(instruction)
                    st.last()
                each = lambda x: x.broadcast_to([P, TILES, E])
                do(dve.memset(ones[:, :], 1.0))
                do(dve.reduce_max(top_l[:, :, :], logits[:, :, :], AX.X))
                dve.tensor_tensor(probs[:, :, :], logits[:, :, :], each(top_l[:, :, :]), ALU.subtract).then_inc(less_max, 1)
                dve.wait_ge(exp_done, 1 + START)
                do(dve.reduce_sum(psum_e[:, :, :], probs[:, :, :], AX.X))
                do(dve.reciprocal(psum_e[:, :, :], psum_e[:, :, :]))
                do(dve.tensor_tensor(probs[:, :, :], probs[:, :, :], each(psum_e[:, :, :]), ALU.mult))
                for n in range(TOPK):
                    do(dve.reduce_max(best[:, n, :, :], probs[:, :, :], AX.X))
                    do(dve.tensor_tensor(score[:, :, :], probs[:, :, :], each(best[:, n, :, :]), ALU.is_equal))
                    do(dve.tensor_tensor(score[:, :, :], score[:, :, :], col(C_LEFT, E, TILES), ALU.mult))
                    do(dve.reduce_max(place[:, :, :], score[:, :, :], AX.X))
                    do(dve.tensor_tensor(chosen[:, n, :, :], each(place[:, :, :]), col(C_LEFT, E, TILES), ALU.is_equal))
                    if n == 0:
                        do(dve.scalar_tensor_tensor(out=probs[:, :, :], in0=chosen[:, 0, :, :], scalar=-2.0,
                                                    in1=probs[:, :, :], op0=ALU.mult, op1=ALU.add))
                do(dve.tensor_tensor(denom[:, :], best[:, 0, :, 0], best[:, 1, :, 0], ALU.add))
                do(dve.tensor_scalar(denom[:, :], denom[:, :], 1e-8, None, ALU.add))
                do(dve.reciprocal(denom[:, :], denom[:, :]))
                for n in range(TOPK):
                    do(dve.tensor_tensor(weight[:, n, :], best[:, n, :, 0], denom[:, :], ALU.mult))
                dve.tensor_tensor(member[:, :, :].rearrange("p e t -> p t e"), chosen[:, 0, :, :], chosen[:, 1, :, :],
                                  ALU.add).then_inc(members, 1)
                do(dve.memset(keep_s[:, :, :], 1.0))
                do(dve.memset(keep_s[:, :, 0:1], 0.0))
                dve.wait_ge(rank_ps, 1 + START)
                flat = lambda x: x[:, :, :].rearrange("p e t -> p (e t)")
                do(dve.tensor_copy(counts[:, :, :], ps_count[:, :, :]))
                do(dve.tensor_tensor_scan(flat(running), flat(keep_s), flat(counts), 0.0, ALU.mult, ALU.add))
                do(dve.tensor_tensor(over[:, :, :], running[:, :, TILES - 1:TILES].broadcast_to([P, E, CHUNKS]),
                                     col(C_LIMITS, CHUNKS, E), ALU.is_gt))
                do(dve.reduce_sum(tiles[:, :].rearrange("p (e o) -> p e o", o=1), over[:, :, :], AX.X))
                do(dve.tensor_tensor_scan(tiles_upto[:, :], ones[:, 0:E], tiles[:, :], 0.0, ALU.mult, ALU.add))
                do(dve.tensor_tensor(base[:, :], tiles_upto[:, :], tiles[:, :], ALU.subtract))
                do(dve.tensor_scalar(base[:, :], base[:, :], float(CT), None, ALU.mult))
                do(dve.tensor_tensor(where[:, :, :], running[:, :, :], counts[:, :, :], ALU.subtract))
                do(dve.tensor_tensor(where[:, :, :], where[:, :, :], ps_rank[:, :, :], ALU.add))
                do(dve.tensor_tensor(where[:, :, :], where[:, :, :], base[:, :].rearrange("p (e o) -> p e o", o=1)
                                     .broadcast_to([P, E, TILES]), ALU.add))
                for n in range(TOPK):
                    do(dve.tensor_tensor(chosen[:, n, :, :], chosen[:, n, :, :], where[:, :, :].rearrange("p e t -> p t e"),
                                         ALU.mult))
                    do(dve.reduce_sum(slot_f[:, n, :].rearrange("p (t o) -> p t o", o=1), chosen[:, n, :, :], AX.X))
                dve.tensor_copy(slot[:, :, :], slot_f[:, :, :]).then_inc(slots, 1)
                do(dve.tensor_tensor(past[:, :, :], tiles_upto[:, :].rearrange("p (o e) -> p o e", o=1)
                                     .broadcast_to([P, ROUTED, E]),
                                     g.const[:, C_TILE:C_TILE + ROUTED].rearrange("p (n o) -> p n o", o=1)
                                     .broadcast_to([P, ROUTED, E]), ALU.is_le))
                do(dve.reduce_sum(ex_f[:, :].rearrange("p (n o) -> p n o", o=1), past[:, :, :], AX.X))
                do(dve.tensor_scalar(ex_f[:, :], ex_f[:, :], float(E - 1), None, ALU.min))
                dve.tensor_copy(experts[:, :], ex_f[:, :]).then_inc(slots, 1)

            @block.scalar
            def _(act):
                act.wait_ge(less_max, 1 + START)
                act.activation(probs[:, :, :], probs[:, :, :], ACT.Exp).then_inc(exp_done, 1)

            @block.tensor
            def _(pe):
                pe.wait_ge(members, 1 + START)
                pe.matmul(ps_rank[:, :, :], g.const[:, C_UPPER:C_UPPER + P], member[:, :, :], start=True, stop=True)
                pe.matmul(ps_count[:, :, :], ones[:, :], member[:, :, :], start=True, stop=True).then_inc(rank_ps, 1)


def moe_experts(nc, g, sem, slots_in, slots_out, slot, experts):
    with ExitStack() as ctx:
        sb = lambda name, shape, dt=F32: ctx.enter_context(nc.sbuf_tensor(name, shape, dt))
        pb = lambda name, shape, dt=F32: ctx.enter_context(nc.psum_tensor(name, shape, dt))
        up32 = sb("moe_up32", [P, KD, 2 * FI])
        uph = sb("moe_uph", [P, KD, 2 * FI], FR)
        upl = sb("moe_upl", [P, KD, 2 * FI], FR)
        dn32 = sb("moe_dn32", [P, KI, D])
        dnh = sb("moe_dnh", [P, KI, D], FR)
        dnl = sb("moe_dnl", [P, KI, D], FR)
        rows = sb("moe_rows", [P, TPC, D])
        xth = sb("moe_xth", [P, KD, CT], FR)
        xtl = sb("moe_xtl", [P, KD, CT], FR)
        silu = sb("moe_silu", [P, 2, CT])
        h32 = sb("moe_h32", [P, 2, CT])
        hh = sb("moe_hh", [P, KI, CT], FR)
        hl = sb("moe_hl", [P, KI, CT], FR)
        y = sb("moe_y", [P, TPC, D])
        ident = g.const[:, C_IDENT:C_IDENT + P]
        ps_t = pb("ex_ps_t", [P, KD, CT])
        ps_g = pb("ex_ps_g", [P, 2, CT])
        ps_u = pb("ex_ps_u", [P, 2, CT])
        ps_y = pb("ex_ps_y", [P, 2, CT])
        up_in = sem("ex_up_in")
        rows_in = sem("ex_rows_in")
        dn_in = sem("ex_dn_in")
        up_hi = sem("ex_up_hi")
        up_lo = sem("ex_up_lo")
        dn_hi = sem("ex_dn_hi")
        dn_lo = sem("ex_dn_lo")
        xt_ps = sem("ex_xt_ps")
        xt_hi = sem("ex_xt_hi")
        xt_lo = sem("ex_xt_lo")
        gu_ps = sem("ex_gu_ps")
        silu_ready = sem("ex_silu")
        h_ready = sem("ex_h")
        h_hi = sem("ex_h_hi")
        h_lo = sem("ex_h_lo")
        y_ps = sem("ex_y_ps")
        y_read = sem("ex_y_read")
        sent = sem.from_zero("rows_sent")
        y_out = sem("ex_y_out")
        sem.start()
        with nc.Block() as block:
            @block.sync
            def _(sp):
                def load_up(w, expert):
                    sp.wait_ge(up_lo, w * KD + START)
                    sp.dma_start(up32[:, :, :], g.w_up[ds(expert * D, D), :].rearrange("(k p) n -> p k n", p=P))\
                      .then_inc(up_in, 16)

                def load_down(w, expert):
                    sp.wait_ge(dn_lo, w * KI + START)
                    sp.dma_start(dn32[:, 0:KI - 1, :], g.w_down[ds(expert * FI, (KI - 1) * P), :]
                                 .rearrange("(m p) n -> p m n", p=P)).then_inc(dn_in, 16)
                    sp.dma_start(dn32[0:FLAST, KI - 1, :], g.w_down[ds(expert * FI + (KI - 1) * P, FLAST), :])\
                      .then_inc(dn_in, 16)

                def load_rows(i, src):
                    sp.wait_ge(xt_ps, i + START)
                    sp.dma_start(rows[:, :, :], src).then_inc(rows_in, 16)
                sp.dma_start(rows[:, :, :], g.v[:, 0:TPC, :]).then_inc(rows_in, 16)
                load_up(0, SHARED)
                load_down(0, SHARED)
                with sp.Fori(1, CHUNKS) as i:
                    load_rows(i, g.v[:, ds(i * TPC, TPC), :])
                first = sp.value_load(experts[0:1, 0:1], min_val=0, max_val=E - 1)
                load_up(1, first)
                load_down(1, first)
                sp.wait_ge(sent, TILES * TOPK * 16)
                routed = lambda i: slots_in[ds((i - CHUNKS) * CT, CT), :].rearrange("(t p) n -> p t n", p=P)
                load_rows(CHUNKS, routed(CHUNKS))
                with sp.Fori(CHUNKS, RUNS - 1) as i:
                    expert = sp.value_load(experts[0:1, ds(i - CHUNKS + 1, 1)], min_val=0, max_val=E - 1)
                    load_up(i - CHUNKS + 2, expert)
                    load_rows(i + 1, routed(i + 1))
                    load_down(i - CHUNKS + 2, expert)

            @block.gpsimd
            def _(pool):
                for t in range(TILES):
                    for n in range(TOPK):
                        pool.indirect_dma_start(out=slots_in, out_offset=bass.IndirectOffsetOnAxis(
                            ap=slot[:, n, t:t + 1], axis=0), in_=g.v[:, t, :], in_offset=None).then_inc(sent, 16)

            @block.vector
            def _(dve):
                def low(i, m):
                    dve.wait_ge(h_hi, i * KI + m + 1 + START)
                    dve.tensor_tensor(hl[0:fw(m), m, :], h32[0:fw(m), m % 2, :],
                                      hh[0:fw(m), m, :].bitcast(F32), ALU.subtract).then_inc(h_lo, 1)

                def step(i, w=None, shared=None):
                    dve.wait_ge(xt_hi, i + 1 + START)
                    dve.tensor_tensor(xtl[:, :, :], ps_t[:, :, :], xth[:, :, :].bitcast(F32), ALU.subtract)\
                       .then_inc(xt_lo, 1)
                    if w is not None:
                        for k in range(KD):
                            dve.wait_ge(up_hi, w * KD + k + 1 + START)
                            dve.tensor_tensor(upl[:, k, :], up32[:, k, :], uph[:, k, :].bitcast(F32), ALU.subtract)\
                               .then_inc(up_lo, 1)
                    if shared is not None:
                        for j in range(TPC):
                            x = g.x[:, ds(shared * TPC + j, 1), :]
                            dve.wait_ge(y_ps, shared * TPC + j + 1 + START)
                            dve.tensor_tensor(x, x, ps_y[:, j % 2:j % 2 + 1, 0:D], ALU.add).then_inc(y_read, 1)
                    for m in range(KI):
                        dve.wait_ge(silu_ready, i * KI + m + 1 + START)
                        dve.wait_ge(h_lo, i * KI + max(m - 1, 0) + START)
                        dve.tensor_tensor(h32[0:fw(m), m % 2, :], silu[0:fw(m), m % 2, :], ps_u[0:fw(m), m % 2, :],
                                          ALU.mult).then_inc(h_ready, 1)
                        if w is not None:
                            dve.wait_ge(dn_hi, w * KI + m + 1 + START)
                            dve.tensor_tensor(dnl[0:fw(m), m, :], dn32[0:fw(m), m, :],
                                              dnh[0:fw(m), m, :].bitcast(F32), ALU.subtract).then_inc(dn_lo, 1)
                        if m:
                            low(i, m - 1)
                    low(i, KI - 1)
                step(0, w=0)
                with dve.Fori(1, CHUNKS) as i:
                    step(i, shared=i - 1)
                step(CHUNKS, w=1, shared=CHUNKS - 1)
                with dve.Fori(CHUNKS + 1, RUNS) as i:
                    step(i, w=i - CHUNKS + 1)

            @block.scalar
            def _(act):
                def outputs(i):
                    act.wait_ge(y_out, (i - CHUNKS) * 16 + START)
                    for j in range(TPC):
                        act.wait_ge(y_ps, i * TPC + j + 1 + START)
                        act.activation(y[:, j, :], ps_y[:, j % 2, 0:D], ACT.Copy).then_inc(y_read, 1)
                    act.wait_ge(y_read, (i + 1) * TPC + START)
                    act.dma_start(slots_out[ds((i - CHUNKS) * CT, CT), :].rearrange("(t p) n -> p t n", p=P), y[:, :, :])\
                       .then_inc(y_out, 16)

                def high(i, m):
                    act.wait_ge(h_ready, i * KI + m + 1 + START)
                    act.activation(hh[0:fw(m), m, :], h32[0:fw(m), m % 2, :], ACT.Copy).then_inc(h_hi, 1)

                def step(i, w=None, before=None):
                    act.wait_ge(xt_ps, i + 1 + START)
                    act.wait_ge(gu_ps, i * KI + START)
                    act.activation(xth[:, :, :], ps_t[:, :, :], ACT.Copy).then_inc(xt_hi, 1)
                    if w is not None:
                        act.wait_ge(up_in, (w + 1) * 16 + START)
                        for k in range(KD):
                            act.activation(uph[:, k, :], up32[:, k, :], ACT.Copy).then_inc(up_hi, 1)
                    if before is not None:
                        outputs(before)
                    for m in range(KI):
                        act.wait_ge(gu_ps, i * KI + m + 1 + START)
                        act.wait_ge(h_ready, i * KI + max(m - 1, 0) + START)
                        act.activation(silu[0:fw(m), m % 2, :], ps_g[0:fw(m), m % 2, :], ACT.Silu).then_inc(silu_ready, 1)
                        if m == 0:
                            act.wait_ge(y_ps, i * TPC + START)
                            if w is not None:
                                act.wait_ge(dn_in, (w + 1) * 32 + START)
                        if w is not None:
                            act.activation(dnh[0:fw(m), m, :], dn32[0:fw(m), m, :], ACT.Copy).then_inc(dn_hi, 1)
                        if m:
                            high(i, m - 1)
                    high(i, KI - 1)
                step(0, w=0)
                with act.Fori(1, CHUNKS) as i:
                    step(i)
                step(CHUNKS, w=1)
                with act.Fori(CHUNKS + 1, RUNS) as i:
                    step(i, w=i - CHUNKS + 1, before=i - 1)
                outputs(RUNS - 1)
                act.wait_ge(y_out, ROUTED * 16 + START)

            @block.tensor
            def _(pe):
                def turn(i):
                    pe.wait_ge(rows_in, (i + 1) * 16 + START)
                    pe.wait_ge(xt_lo, i + START)
                    for k in range(KD):
                        for j in range(TPC):
                            last = pe.transpose(ps_t[:, k, j * P:(j + 1) * P], rows[:, j, k * P:(k + 1) * P], ident)
                    last.then_inc(xt_ps, 1)

                def up(i, w=None):
                    pe.wait_ge(xt_lo, i + 1 + START)
                    if w is not None:
                        pe.wait_ge(up_lo, (w + 1) * KD + START)
                    for m in range(KI):
                        pe.wait_ge(h_ready, i * KI + max(m - 1, 0) + START)
                        for ps, first in ((ps_g, 0), (ps_u, FI)):
                            cols = slice(first + m * P, first + m * P + fw(m))
                            for k in range(KD):
                                last = product3(pe, ps[0:fw(m), m % 2, :], uph[:, k, cols], upl[:, k, cols],
                                                xth[:, k, :], xtl[:, k, :], k == 0, k == KD - 1)
                        last.then_inc(gu_ps, 1)

                def down(i, w=None):
                    if w is not None:
                        pe.wait_ge(dn_lo, (w + 1) * KI + START)
                    for j in range(TPC):
                        pe.wait_ge(y_read, i * TPC + max(j - 1, 0) + START)
                        t = slice(j * P, (j + 1) * P)
                        for m in range(KI):
                            if j == 0:
                                pe.wait_ge(h_lo, i * KI + m + 1 + START)
                            last = product3(pe, ps_y[:, j % 2, 0:D], hh[0:fw(m), m, t], hl[0:fw(m), m, t],
                                            dnh[0:fw(m), m, :], dnl[0:fw(m), m, :], m == 0, m == KI - 1)
                        last.then_inc(y_ps, 1)
                turn(0)
                up(0, w=0)
                turn(1)
                down(0, w=0)
                up(1)
                with pe.Fori(2, CHUNKS) as i:
                    turn(i)
                    down(i - 1)
                    up(i)
                turn(CHUNKS)
                down(CHUNKS - 1)
                up(CHUNKS, w=1)
                with pe.Fori(CHUNKS + 1, RUNS) as i:
                    turn(i)
                    down(i - 1, w=i - CHUNKS)
                    up(i, w=i - CHUNKS + 1)
                down(RUNS - 1, w=ROUTED)


def moe_combine(nc, g, sem, slots_out, slot, weight):
    with ExitStack() as ctx:
        N = 4
        sb = lambda name, shape, dt=F32: ctx.enter_context(nc.sbuf_tensor(name, shape, dt))
        picked = sb("picked", [P, N, TOPK, D])
        picked_in = [sem.from_zero(f"cb_picked_in{u}") for u in range(N)]
        own = sem("cb_own")
        out_ready = sem("cb_ready")
        stored = sem("cb_stored")
        sem.start()
        with nc.Block() as block:
            @block.gpsimd
            def _(pool):
                for t in range(TILES):
                    if t >= N:
                        pool.wait_ge(out_ready, t - N + 1 + START)
                    for n in range(TOPK):
                        pool.indirect_dma_start(out=picked[:, t % N, n, :], out_offset=None, in_=slots_out,
                                                in_offset=bass.IndirectOffsetOnAxis(ap=slot[:, n, t:t + 1], axis=0))\
                            .then_inc(picked_in[t % N], 16)

            @block.vector
            def _(dve):
                st = Steps(dve, own)
                for t in range(TILES):
                    x = g.x[:, t, :]
                    dve.wait_ge(picked_in[t % N], 16 * TOPK * (t // N + 1))
                    for n in range(TOPK):
                        if n:
                            st.last()
                        last = dve.scalar_tensor_tensor(out=x, in0=picked[:, t % N, n, :], scalar=weight[:, n, t:t + 1],
                                                        in1=x, op0=ALU.mult, op1=ALU.add)
                        if n < TOPK - 1:
                            st.add(last)
                    last.then_inc(out_ready, 1)

            @block.scalar
            def _(act):
                for t in range(0, TILES, 2):
                    act.wait_ge(out_ready, t + 2 + START)
                    act.dma_start(g.out[t * P:(t + 2) * P, :].rearrange("(t p) n -> p t n", p=P), g.x[:, t:t + 2, :])\
                       .then_inc(stored, 16)
                act.wait_ge(stored, TILES // 2 * 16 + START)


class Shared:
    pass


def program(nc, names):
    g = Shared()
    g.constants = names["constants"]
    g.x_in = names["x_in"]
    g.qkv_w = names["qkv_w"]
    g.qk_bias = names["qk_bias"]
    g.v_bias = names["v_bias"]
    g.out_w = names["out_w"]
    g.out_b = names["out_b"]
    g.up_t = names["up_t"]
    g.down_t = names["down_t"]
    g.log_a_t = names["log_a_t"]
    g.c_t = names["c_t"]
    g.log_a_blocks = names["log_a_blocks"]
    g.c_blocks = names["c_blocks"]
    g.b_t = names["b_t"]
    g.d_vec = names["d_vec"]
    g.gate_t = names["gate_t"]
    g.w_up = names["w_up"]
    g.w_down = names["w_down"]
    g.out = names["out"]
    with ExitStack() as ctx:
        sb = lambda name, shape, dt=F32: ctx.enter_context(nc.sbuf_tensor(name, shape, dt))
        g.const = sb("const", [P, C_END])
        g.ident_bf = sb("ident_bf", [P, P], BF16)
        g.mask_bf = sb("mask_bf", [P, 3 * P], BF16)
        g.eps = sb("eps", [P, 1])
        g.started = ctx.enter_context(nc.semaphore("started"))
        g.passed = ctx.enter_context(nc.semaphore("passed"))
        g.x = sb("x", [P, TILES, D])
        g.v = sb("v", [P, TILES, D])
        g.q_k_hi = nc.dram_tensor("q_k_hi", (2 * D, TOK), F32, kind="Internal").ap()
        g.q_k_lo = nc.dram_tensor("q_k_lo", (2 * D, TOK), F32, kind="Internal").ap()
        phase_qkv(nc, ctx, g)
        with nc.sbuf_tensor("att", [P, TILES, D], F32) as att:
            g.att = att
            phase_attention(nc, ctx, g)
            phase_ffn(nc, ctx, g)
            phase_ssm(nc, ctx, g)
        phase_moe(nc, ctx, g)


def kernel(**inputs):
    import concourse.bacc as bacc
    from concourse.bass_utils import run_bass_kernel_spmd

    a = {k: np.asarray(v) for k, v in inputs.items()}
    lay = np.ascontiguousarray
    up = np.concatenate([a["L1_ffn_experts_gate_up"], a["L1_ffn_shared_gate_up"][None]])
    down = np.concatenate([a["L1_ffn_experts_down"], a["L1_ffn_shared_down"][None]])
    log_a, c = a["L1_attn_log_A_diag"], a["L1_attn_C_w"]
    arrays = {
        "constants": host_constants(),
        "x_in": a["L0_attn_x"].reshape(TOK, D),
        "qkv_w": a["L0_attn_qkv_w"],
        "qk_bias": lay(a["L0_attn_qkv_b"][:2 * D].reshape(-1, P).T),
        "v_bias": lay(a["L0_attn_qkv_b"][2 * D:]),
        "out_w": a["L0_attn_out_w"],
        "out_b": a["L0_attn_out_b"],
        "up_t": lay(a["L0_ffn_w_up"].T),
        "down_t": lay(a["L0_ffn_w_down"].T),
        "log_a_t": lay(log_a.T),
        "c_t": lay(c.T),
        "log_a_blocks": lay(log_a.reshape(-1, P).T),
        "c_blocks": lay(c.reshape(-1, P).T),
        "b_t": lay(a["L1_attn_B_w"].T),
        "d_vec": a["L1_attn_D_vec"],
        "gate_t": lay(a["L1_ffn_gate_weight"].T),
        "w_up": lay(up.transpose(0, 2, 1)).reshape(-1, up.shape[1]),
        "w_down": lay(down.transpose(0, 2, 1)).reshape(-1, D),
    }
    nc = bacc.Bacc("TRN2", target_bir_lowering=False, num_devices=1)
    names = {n: nc.dram_tensor(f"in_{n}", v.shape, mybir.dt.from_np(v.dtype), kind="ExternalInput").ap()
             for n, v in arrays.items()}
    names["out"] = nc.dram_tensor("out", (TOK, D), F32, kind="ExternalOutput").ap()
    program(nc, names)
    result = run_bass_kernel_spmd(nc, [{f"in_{n}": v for n, v in arrays.items()}], core_ids=[0])
    return result.results[0]["out"].reshape(BATCH, SEQ, D)
```

```python
from contextlib import ExitStack

import numpy as np

import concourse.bass as bass
from concourse import mybir

F32 = mybir.dt.float32
FR = mybir.dt.float32r
BF16 = mybir.dt.bfloat16
ALU = mybir.AluOpType
ACT = mybir.ActivationFunctionType
AX = mybir.AxisListType

P = 128
BATCH, SEQ, D = 2, 2048, 256
TOK = BATCH * SEQ
TILES = TOK // P
CT = 512
TPC = CT // P
CHUNKS = TOK // CT
KD = D // P
H, HD = 16, 16
EPS = 1e-5
MASKED = -1e30

C_IDENT = 0
C_MASK_QK = 128
C_MASK_KQ = 256
C_SEL = 512
SELW = 18
C_NEG_TAU = 536
C_TAU_MASK = 540
C_STEP = 572
C_SAME_S = 604
C_SAME_G = 620
C_UPPER = 628
C_LEFT = 756
C_LIMITS = 764
C_TILE = 772
C_END = 804


def host_constants():
    c = np.zeros((P, C_END), np.float32)
    i = np.arange(P)
    c[:, C_IDENT:C_IDENT + P] = np.eye(P)
    c[:, C_MASK_QK:C_MASK_QK + P] = np.where(i[None, :] > i[:, None], MASKED, 0)
    c[:, C_MASK_KQ:C_MASK_KQ + P] = MASKED
    c[:, C_MASK_KQ + P:C_MASK_KQ + 2 * P] = np.where(i[:, None] > i[None, :], MASKED, 0)
    for j in range(HD + 1):
        c[i % 32 == j, C_SEL + j] = 1
    tau, s = i // NSTATE, i % NSTATE
    m, r = np.arange(MT), np.arange(T)
    c[:, C_NEG_TAU:C_NEG_TAU + MT] = -(TAUS * m[None, :] + tau[:, None])
    c[:, C_TAU_MASK:C_TAU_MASK + T] = r[None, :] >= tau[:, None]
    c[:, C_STEP:C_STEP + T] = -(r[None, :] + 1)
    c[:, C_SAME_S:C_SAME_S + NSTATE] = s[:, None] == np.arange(NSTATE)[None, :]
    c[:, C_SAME_G:C_SAME_G + TAUS] = tau[:, None] == np.arange(TAUS)[None, :]
    c[:, C_UPPER:C_UPPER + P] = i[:, None] < i[None, :]
    c[:, C_LEFT:C_LEFT + E] = E - np.arange(E)
    c[:, C_LIMITS:C_LIMITS + CHUNKS] = np.arange(CHUNKS) * CT
    c[:, C_TILE:C_TILE + ROUTED] = np.arange(ROUTED)
    return c


E, TOPK = 8, 2
ROUTED = (TOPK * TOK + E * (CT - 1)) // CT
NSTATE = 16
TAUS = P // NSTATE
T = 32
MT = T // TAUS
BLOCKS = TOK // T
DB = D // TAUS


START = 4


class Semaphores:

    def __init__(self, nc, ctx):
        self.nc, self.ctx, self.new = nc, ctx, []

    def __call__(self, name):
        self.new.append(self.ctx.enter_context(self.nc.semaphore(name)))
        return self.new[-1]

    def from_zero(self, name):
        return self.ctx.enter_context(self.nc.semaphore(name))

    def start(self):
        new, self.new = self.new, []
        with self.nc.Block() as block:
            @block.sync
            def _(sp):
                for s in new:
                    sp.sem_inc(s, START)


class Steps:

    def __init__(self, eng, sem, base=0):
        self.eng, self.sem, self.base, self.n = eng, sem, base, 0

    def add(self, instruction):
        instruction.then_inc(self.sem, 1)
        self.n += 1

    def last(self):
        self.eng.wait_ge(self.sem, self.base + self.n + START)


def on_its_own(eng, g):
    eng.sem_inc(g.passed, 1)


def product3(pe, out, wh, wl, xh, xl, start, stop):
    pe.matmul(out, wh, xh, start=start, stop=False)
    pe.matmul(out, wh, xl, start=False, stop=False)
    return pe.matmul(out, wl, xh, start=False, stop=stop)


def ds(start, size):
    return bass.ds(start, size)


class LayerNorm:

    def __init__(self, g, sb, sem, name):
        self.g = g
        self.stats = sb(name + "_stats", [P, 2, TPC, 6])
        self.mv = sb(name + "_mv", [P, TPC, 2])
        self.sd = sb(name + "_sd", [P, TPC])
        self.rstd = sb(name + "_rstd", [P, TPC])
        self.spread_ready = sem(name + "_spread_ready")
        self.var_ready = sem(name + "_var_ready")
        self.sd_ready = sem(name + "_sd_ready")
        self.rstd_ready = sem(name + "_rstd_ready")
        self.ready = sem(name + "_ready")

    def spread(self, dve, c, u):
        dve.wait_ge(self.var_ready, c - 1 + START)
        on_its_own(dve, self.g)
        for j in range(TPC):
            dve.bn_stats(self.stats[:, u, j, :], self.g.x[:, ds(c * TPC + j, 1), :]).then_inc(self.spread_ready, 1)

    def variance(self, dve, c, u):
        dve.wait_ge(self.spread_ready, (c + 1) * TPC + START)
        dve.wait_ge(self.ready, c + START)
        on_its_own(dve, self.g)
        for j in range(TPC):
            last = dve.bn_aggr(self.mv[:, j, :], self.stats[:, u, j, :])
        last.then_inc(self.var_ready, 1)

    def deviation(self, act, c):
        act.wait_ge(self.var_ready, c + 1 + START)
        act.activation(self.sd[:, :], self.mv[:, :, 1], ACT.Sqrt, bias=self.g.eps[:, 0:1]).then_inc(self.sd_ready, 1)

    def invert(self, dve, c):
        dve.wait_ge(self.sd_ready, c + 1 + START)
        dve.reciprocal(self.rstd[:, :], self.sd[:, :]).then_inc(self.rstd_ready, 1)

    def normal(self, dve, c, out):
        dve.wait_ge(self.rstd_ready, c + 1 + START)
        for j in range(TPC):
            last = dve.tensor_scalar(out[:, j, :], self.g.x[:, ds(c * TPC + j, 1), :], self.mv[:, j, 0:1],
                                     self.rstd[:, j:j + 1], ALU.subtract, ALU.mult)
        last.then_inc(self.ready, 1)


def in_pairs(eng, step, peeled=1):
    with eng.Fori(0, CHUNKS // 2 - peeled) as i:
        step(2 * i, 0)
        step(2 * i + 1, 1)
    for it in range(CHUNKS - 2 * peeled, CHUNKS):
        step(it, it % 2)


def there(c):
    return not isinstance(c, int) or c < CHUNKS


def phase_qkv(nc, top, g):
    with ExitStack() as ctx:
        sb = lambda name, shape, dt=F32: ctx.enter_context(nc.sbuf_tensor(name, shape, dt))
        pb = lambda name, shape, dt=F32: ctx.enter_context(nc.psum_tensor(name, shape, dt))
        sem = Semaphores(nc, ctx)
        NW = 3 * D
        w32 = sb("qkv_w32", [P, KD, NW])
        wh = sb("qkv_wh", [P, KD, NW], FR)
        wl = sb("qkv_wl", [P, KD, NW], FR)
        qk_bias = sb("qk_bias", [P, 4])
        v_bias = sb("v_bias", [P, D])
        ln = LayerNorm(g, sb, sem, "qkv_ln")
        xn = sb("qkv_xn", [P, TPC, D])
        xth = [sb(f"qkv_xth{u}", [P, KD, CT], FR) for u in range(2)]
        xtl = [sb(f"qkv_xtl{u}", [P, KD, CT], FR) for u in range(2)]
        qk32 = sb("qk32", [P, 4, CT])
        qkh = [sb(f"qkh{u}", [P, 4, CT], FR) for u in range(2)]
        qkl = [sb(f"qkl{u}", [P, 4, CT], FR) for u in range(2)]
        ps_t = pb("qkv_ps_t", [P, KD, CT])
        ps_qk = pb("ps_qk", [P, 2, CT])
        ps_v = pb("ps_v", [P, TPC, D])

        const_in = sem("const_in")
        w_in = sem("qkv_w_in")
        x_in = [sem(f"x_in{u}") for u in range(2)]
        w_hi = sem("qkv_w_hi")
        w_lo = sem("qkv_w_lo")
        const_bf = sem("const_bf")
        xt_ps = sem("qkv_xt_ps")
        xt_hi = sem("qkv_xt_hi")
        xt_lo = sem("qkv_xt_lo")
        qk_ps = sem("qk_ps")
        qk_f32 = sem("qk_f32")
        qk_hi = sem("qk_hi")
        qk_lo = sem("qk_lo")
        v_ps = sem("v_ps")
        v_ready = sem("v_ready")
        qk_out = [sem(f"qk_out{u}") for u in range(2)]

        sem.start()
        with nc.Block() as block:
            @block.sync
            def _(sp):
                def load_x(it, u, nth):
                    sp.wait_ge(x_in[u], nth * 16 + START)
                    sp.dma_start(g.x[:, ds(it * TPC, TPC), :],
                                 g.x_in[ds(it * CT, CT), :].rearrange("(t p) n -> p t n", p=P)).then_inc(x_in[u], 16)
                load_x(0, 0, 0)
                sp.dma_start(g.const[:, :], g.constants).then_inc(const_in, 16)
                sp.dma_start(w32[:, :, :], g.qkv_w.rearrange("(k p) n -> p k n", p=P)).then_inc(w_in, 16)
                load_x(1, 1, 0)
                sp.dma_start(qk_bias[:, :], g.qk_bias).then_inc(w_in, 16)
                sp.dma_start(v_bias[:, :], g.v_bias.rearrange("(o n) -> o n", o=1)
                             .broadcast_to([P, D])).then_inc(w_in, 16)
                with sp.Fori(1, CHUNKS // 2) as i:
                    for u in range(2):
                        load_x(2 * i + u, u, i)
                with sp.Fori(0, CHUNKS // 2) as i:
                    for u in range(2):
                        it = 2 * i + u
                        sp.wait_ge(qk_hi, it * 4 + 4 + START)
                        sp.wait_ge(qk_lo, it * 4 + 4 + START)
                        sp.dma_start(g.q_k_hi[:, ds(it * CT, CT)].rearrange("(m p) t -> p m t", p=P),
                                     qkh[u][:, :, :].bitcast(F32)).then_inc(qk_out[u], 16)
                        sp.dma_start(g.q_k_lo[:, ds(it * CT, CT)].rearrange("(m p) t -> p m t", p=P),
                                     qkl[u][:, :, :].bitcast(F32)).then_inc(qk_out[u], 16)
                for u in range(2):
                    sp.wait_ge(qk_out[u], CHUNKS // 2 * 32 + START)

            @block.vector
            def _(dve):
                def loaded(it, u):
                    dve.wait_ge(x_in[u], (it - u) * 8 + 16 + START)

                def low(it, u, m):
                    dve.wait_ge(qk_hi, it * 4 + m + 1 + START)
                    dve.tensor_tensor(qkl[u][:, m, :], qk32[:, m, :], qkh[u][:, m, :].bitcast(F32), ALU.subtract)\
                       .then_inc(qk_lo, 1)

                def turned_low(c, u):
                    dve.wait_ge(xt_hi, c + 1 + START)
                    dve.tensor_tensor(xtl[u][:, :, :], ps_t[:, :, :], xth[u][:, :, :].bitcast(F32), ALU.subtract)\
                       .then_inc(xt_lo, 1)

                def add_bias(it, half):
                    dve.wait_ge(v_ps, it * TPC + 2 * half + 2 + START)
                    dve.tensor_tensor(g.v[:, ds(it * TPC + 2 * half, 2), :], ps_v[:, 2 * half:2 * half + 2, :],
                                      v_bias[:, :].rearrange("p (o n) -> p o n", o=1).broadcast_to([P, 2, D]),
                                      ALU.add).then_inc(v_ready, 1)

                def norm(c, u):
                    loaded(c, u)
                    ln.spread(dve, c, u)
                    ln.variance(dve, c, u)
                    ln.invert(dve, c)
                    dve.wait_ge(xt_ps, c + START)
                    ln.normal(dve, c, xn)

                def step(it, u):
                    if there(it + 1):
                        turned_low(it + 1, 1 - u)
                    dve.wait_ge(qk_out[u], (it - u) * 16 + START)
                    ahead = there(it + 2)
                    if ahead:
                        loaded(it + 2, u)
                        ln.spread(dve, it + 2, u)
                    low(it, u, 0)
                    if ahead:
                        ln.variance(dve, it + 2, u)
                    low(it, u, 1)
                    low(it, u, 2)
                    add_bias(it, 0)
                    if ahead:
                        ln.invert(dve, it + 2)
                        dve.wait_ge(xt_ps, it + 2 + START)
                        ln.normal(dve, it + 2, xn)
                    low(it, u, 3)
                    add_bias(it, 1)
                dve.memset(g.eps[:, :], EPS).then_inc(g.started, 1)
                norm(0, 0)
                dve.wait_ge(const_in, 16 + START)
                dve.tensor_copy(g.ident_bf[:, :], g.const[:, C_IDENT:C_IDENT + P]).then_inc(const_bf, 1)
                dve.tensor_copy(g.mask_bf[:, :], g.const[:, C_MASK_QK:C_MASK_QK + 3 * P]).then_inc(const_bf, 1)
                turned_low(0, 0)
                norm(1, 1)
                dve.wait_ge(w_hi, 1 + START)
                dve.tensor_tensor(wl[:, :, :], w32[:, :, :], wh[:, :, :].bitcast(F32), ALU.subtract).then_inc(w_lo, 1)
                in_pairs(dve, step)

            @block.scalar
            def _(act):
                def turned_high(c, u):
                    act.wait_ge(xt_ps, c + 1 + START)
                    if not isinstance(c, int) or c >= 2:
                        act.wait_ge(v_ps, (c - 1) * TPC + START)
                    act.activation(xth[u][:, :, :], ps_t[:, :, :], ACT.Copy).then_inc(xt_hi, 1)

                def high(it, u, m):
                    act.wait_ge(qk_f32, it * 4 + m + 1 + START)
                    act.activation(qkh[u][:, m, :], qk32[:, m, :], ACT.Copy).then_inc(qk_hi, 1)

                def step(it, u):
                    if there(it + 1):
                        turned_high(it + 1, 1 - u)
                    act.wait_ge(qk_out[u], (it - u) * 16 + START)
                    act.wait_ge(qk_lo, it * 4 + START)
                    for m in range(4):
                        act.wait_ge(qk_ps, it * 4 + m + 1 + START)
                        act.activation(qk32[:, m, :], ps_qk[:, m % 2, :], ACT.Identity, bias=qk_bias[:, m:m + 1])\
                           .then_inc(qk_f32, 1)
                        if m:
                            high(it, u, m - 1)
                        if m == 1 and there(it + 2):
                            ln.deviation(act, it + 2)
                    high(it, u, 3)
                act.wait_ge(g.started, 1)
                ln.deviation(act, 0)
                turned_high(0, 0)
                ln.deviation(act, 1)
                act.wait_ge(w_in, 48 + START)
                act.activation(wh[:, :, :], w32[:, :, :], ACT.Copy).then_inc(w_hi, 1)
                in_pairs(act, step)

            @block.tensor
            def _(pe):
                def turn(c):
                    pe.wait_ge(ln.ready, c + 1 + START)
                    pe.wait_ge(xt_lo, c + START)
                    for k in range(KD):
                        for j in range(TPC):
                            last = pe.transpose(ps_t[:, k, j * P:(j + 1) * P], xn[:, j, k * P:(k + 1) * P],
                                                g.const[:, C_IDENT:C_IDENT + P])
                    last.then_inc(xt_ps, 1)

                def step(it, u):
                    if there(it + 1):
                        turn(it + 1)
                    else:
                        pe.wait_ge(xt_lo, it + 1 + START)
                    for m in range(4):
                        pe.wait_ge(qk_f32, it * 4 + max(m - 1, 0) + START)
                        for k in range(KD):
                            w = slice(m * P, (m + 1) * P)
                            last = product3(pe, ps_qk[:, m % 2, :], wh[:, k, w], wl[:, k, w], xth[u][:, k, :],
                                            xtl[u][:, k, :], k == 0, k == KD - 1)
                        last.then_inc(qk_ps, 1)
                    for j in range(TPC):
                        pe.wait_ge(v_ready, it * 2 - 1 + j // 2 + START)
                        for k in range(KD):
                            t = slice(j * P, (j + 1) * P)
                            last = product3(pe, ps_v[:, j, :], xth[u][:, k, t], xtl[u][:, k, t],
                                            wh[:, k, 2 * D:], wl[:, k, 2 * D:], k == 0, k == KD - 1)
                        last.then_inc(v_ps, 1)
                pe.wait_ge(const_in, 16 + START)
                turn(0)
                pe.wait_ge(w_lo, 1 + START)
                in_pairs(pe, step)


TILES_OF = [(c, kt, 0 if kt < c * TPC + 2 else CT // 2) for c in range(4) for kt in range((c + 1) * TPC)]
MAXES = [(i, c, min(CT, (i + 1) * P - c * CT)) for i in range(SEQ // P) for c in range(i // TPC + 1)]
NT = len(TILES_OF)
assert NT == len(MAXES) and NT % TPC == 0
GROUPS = NT // TPC
CHUNK_END = [(c + 1) * (c + 2) // 2 - 1 for c in range(4)]
CHUNK_MAX_AT = {CHUNK_END[c] + 1: c for c in range(4)}
TURN_AT = {3: 0, 4: 1, 7: 2, GROUPS: 3}
O_AT = {CHUNK_END[c] + 1: c for c in range(4)}
SUMS_AT = {5: 0, 6: 1, 8: 2, GROUPS + 1: 3}
NORMALISE_AT = 2
PER_MAX = 2
HEADS = BATCH * H
STACK = 3 * HD
MROW = 96
SCALE = HD ** -0.5


def batch_head(n):
    return n // H, n % H


def phase_attention(nc, top, g):
    with ExitStack() as ctx:
        sb = lambda name, shape, dt=F32: ctx.enter_context(nc.sbuf_tensor(name, shape, dt))
        pb = lambda name, shape, dt=F32: ctx.enter_context(nc.psum_tensor(name, shape, dt))
        sem = Semaphores(nc, ctx)
        q_st = [sb(f"q_stack{u}", [P, SEQ], FR) for u in range(3)]
        k_st = [sb(f"k_stack{u}", [P, SEQ], FR) for u in range(3)]
        v_st = [sb(f"v_stack{u}", [P, SEQ // P, 32]) for u in range(3)]
        probs = sb("probs", [P, 2 * TPC, CT])
        maxes = sb("maxes", [P, SEQ // P, 4])
        mx = sb("mx", [P, SEQ // P])
        mh = sb("mh", [TPC, 4, P], FR)
        ml = sb("ml", [TPC, 4, P], FR)
        o_sb = sb("o_sb", [P, 2, CT])
        rden = sb("rden", [P, SEQ // P, 1])
        ones = sb("att_ones", [1, CT])
        onesr = sb("att_onesr", [1, 1, CT], FR)
        zeros = sb("att_zeros", [P, CT])
        ps_m = pb("ps_m", [P, 3, CT])
        ps_s = pb("ps_s", [P, 3, CT])
        ps_o = pb("ps_o", [P, CT])
        ps_f = pb("ps_f", [P, CT])
        fin = ps_f[:, 0:SEQ // P * SELW].rearrange("p (t w) -> p t w", w=SELW)
        turned = ps_f[0:TPC, 384:512]

        init = sem("att_init")
        ones_r = sem("att_ones_r")
        stack_in = [sem(f"stack_in{u}") for u in range(3)]
        v_in = sem("att_v_in")
        mrow_in = [sem(f"mrow_in{c}") for c in range(4)]
        zeroed = sem("att_zeroed")
        zero_rows = sem("att_zero_rows")
        max_ps = sem("max_ps")
        max_used = sem("max_used")
        chunk_max = sem("chunk_max")
        own = sem("att_dve_own")
        m_turned = sem("m_turned")
        m_hi = sem("m_hi")
        m_lo = sem("m_lo")
        s_ps = sem("s_ps")
        p_ready = sem("p_ready")
        pv_done = sem("pv_done")
        o_copied = sem("o_copied")
        fin_ps = sem("fin_ps")
        fin_used = sem("fin_used")

        def upto(n, per, k):
            return max(n * per + k, 0) if isinstance(n, int) else n * per + k

        def load_stacks(sp, n, u, done):
            sp.wait_ge(s_ps, done * NT + START)
            b, h = batch_head(n)
            rows_q, rows_k = ds(h * HD, HD), ds(h * HD + D, HD)
            t = ds(b * SEQ, SEQ)
            for dst, src in ((q_st[u][0:HD, :], g.q_k_hi[rows_q, t]), (q_st[u][HD:2 * HD, :], g.q_k_hi[rows_q, t]),
                             (q_st[u][2 * HD:STACK, :], g.q_k_lo[rows_q, t]), (k_st[u][0:HD, :], g.q_k_hi[rows_k, t]),
                             (k_st[u][HD:2 * HD, :], g.q_k_lo[rows_k, t]), (k_st[u][2 * HD:STACK, :], g.q_k_hi[rows_k, t])):
                sp.dma_start(dst.bitcast(F32), src).then_inc(stack_in[u], 16)

        def load_mrow(sp, n, u, c):
            sp.wait_ge(m_lo, n * 4 + c + 1 + START)
            for r, part in ((MROW, mh), (MROW + 1, ml)):
                sp.dma_start(q_st[u][r:r + 1, c * CT:(c + 1) * CT].bitcast(F32).rearrange("o (t p) -> o t p", p=P),
                             part[:, c, :].bitcast(F32)).then_inc(mrow_in[c], 16)

        ONES, LOADS = 2 * 16, 6 * 16
        TRIPLES = (HEADS - 2) // 3
        sem.start()
        with nc.Block() as block:
            @block.sync
            def _(sp):
                sp.wait_ge(ones_r, 1 + START)
                for u in range(3):
                    sp.wait_ge(zeroed, 2 * u + 2 + START)
                    for r in (MROW, MROW + 1):
                        sp.dma_start(k_st[u][r:r + 1, :].bitcast(F32).rearrange("o (c t) -> o c t", t=CT),
                                     onesr[0:1, :, :].bitcast(F32).broadcast_to([1, SEQ // CT, CT]))\
                          .then_inc(stack_in[u], 16)
                    if u < 2:
                        load_stacks(sp, u, u, 0)

                def step(n, u, last=None, next_up=None, done=None):
                    if last is not None:
                        load_mrow(sp, last, (u + 2) % 3, 3)
                    if next_up is not None:
                        load_stacks(sp, next_up, (u + 1) % 3, done)
                    for c in range(3):
                        load_mrow(sp, n, u, c)
                step(0, 0)
                step(1, 1, 0, 2, 0)
                with sp.Fori(0, TRIPLES - 1) as i:
                    for v in range(3):
                        step(3 * i + v + 2, (v + 2) % 3, 3 * i + v + 1, 3 * i + v + 3, 3 * i + v + 1)
                for n in range(HEADS - 3, HEADS):
                    step(n, n % 3, n - 1, n + 1 if n + 1 < HEADS else None, n - 1)
                load_mrow(sp, HEADS - 1, (HEADS - 1) % 3, 3)
                for c in range(4):
                    sp.wait_ge(mrow_in[c], HEADS * 32 + START)

            @block.gpsimd
            def _(pool):
                for u in range(3):
                    pool.memset(v_st[u][:, :, :], 0.0).then_inc(init, 1)
                pool.wait_ge(init, 3 + START)
                for u in range(3):
                    pool.memset(v_st[u][:, :, HD:HD + 1], 1.0).then_inc(init, 1)

                def stage_v(n, u, done):
                    pool.wait_ge(pv_done, done * GROUPS + START)
                    on_its_own(pool, g)
                    b, h = batch_head(n)
                    pool.tensor_copy(v_st[u][:, :, 0:HD], g.v[:, ds(b * (SEQ // P), SEQ // P), ds(h * HD, HD)])\
                        .then_inc(v_in, 1)
                stage_v(0, 0, 0)
                stage_v(1, 1, 0)
                with pool.Fori(0, TRIPLES) as i:
                    for v in range(3):
                        stage_v(3 * i + v + 2, (v + 2) % 3, 3 * i + v)

            @block.vector
            def _(dve):
                dve.memset(zeros[:, :], 0.0).then_inc(zero_rows, 1)
                dve.memset(ones[:, :], 1.0).then_inc(own, 1)
                dve.memset(maxes[:, :, :], -3e38).then_inc(own, 1)
                dve.memset(ps_o[:, :], 0.0).then_inc(own, 1)
                dve.wait_ge(own, 3 + START)
                dve.tensor_copy(onesr[:, 0, :], ones[:, :]).then_inc(ones_r, 1)
                dve.wait_ge(zero_rows, 1 + START)
                for st in (q_st[0], k_st[0], q_st[1], k_st[1], q_st[2], k_st[2]):
                    dve.tensor_copy(st[:, :].rearrange("p (c t) -> p c t", t=CT),
                                    zeros[:, :].rearrange("p (o t) -> p o t", o=1).broadcast_to([P, SEQ // CT, CT]))\
                       .then_inc(zeroed, 1)

                def maximum(n, u, x):
                    i, c, w = MAXES[x]
                    dve.wait_ge(max_ps, n * NT + x + 1 + START)
                    dve.reduce_max(maxes[:, i, c:c + 1], ps_m[:, (u + x) % 3, 0:w], AX.X).then_inc(max_used, PER_MAX)

                def chunk(n, c):
                    dve.wait_ge(max_used, (n * NT + (CHUNK_END[c] + 1) * TPC) * PER_MAX + START)
                    dve.wait_ge(m_turned, upto(n, 4, c - 3) + START)
                    dve.reduce_max(mx[:, c * TPC:(c + 1) * TPC], maxes[:, c * TPC:(c + 1) * TPC, :], AX.X)\
                       .then_inc(chunk_max, 1)

                def low(n, c):
                    dve.wait_ge(m_hi, n * 4 + c + 1 + START)
                    dve.scalar_tensor_tensor(out=ml[:, c, :], in0=turned, scalar=-1.0, in1=mh[:, c, :].bitcast(F32),
                                             op0=ALU.mult, op1=ALU.subtract).then_inc(m_lo, 1)

                def reciprocals(n):
                    dve.wait_ge(fin_ps, n * 4 + 4 + START)
                    dve.reciprocal(rden[:, :, :], fin[:, :, HD:HD + 1]).then_inc(own, 1)

                def normalise(n):
                    dve.wait_ge(own, n + 4 + START)
                    b, h = batch_head(n)
                    dve.tensor_tensor(g.att[:, ds(b * (SEQ // P), SEQ // P), ds(h * HD, HD)], fin[:, :, 0:HD],
                                      rden[:, :, :].broadcast_to([P, SEQ // P, HD]), ALU.mult).then_inc(fin_used, 1)

                def step(n, u, last=None, before_last=None):
                    for q in range(GROUPS):
                        for r in range(TPC):
                            if n is not None:
                                maximum(n, u, q * TPC + r)
                            if r == 0 and q == 0 and last is not None:
                                chunk(last, 3)
                            if r == 0 and q in CHUNK_MAX_AT and n is not None:
                                chunk(n, CHUNK_MAX_AT[q])
                            if r == 1 and q == NORMALISE_AT and before_last is not None:
                                reciprocals(before_last)
                        if q == NORMALISE_AT and before_last is not None:
                            normalise(before_last)
                        if q == 0 and last is not None:
                            low(last, 3)
                        if q in TURN_AT and n is not None:
                            low(n, TURN_AT[q])
                step(0, 0)
                step(1, 1, 0)
                with dve.Fori(0, TRIPLES) as i:
                    for v in range(3):
                        step(3 * i + v + 2, (v + 2) % 3, 3 * i + v + 1, 3 * i + v)
                step(None, HEADS % 3, HEADS - 1, HEADS - 2)
                reciprocals(HEADS - 1)
                normalise(HEADS - 1)

            @block.scalar
            def _(act):
                def high(n, c):
                    act.wait_ge(m_turned, n * 4 + c + 1 + START)
                    act.wait_ge(mrow_in[c], n * 32 + START)
                    act.activation(mh[:, c, :], turned, ACT.Copy, scale=-1.0).then_inc(m_hi, 1)

                def exp(n, u, t):
                    q0 = TILES_OF[t][2]
                    act.wait_ge(s_ps, n * NT + t + 1 + START)
                    act.wait_ge(pv_done, upto(n, GROUPS, t // TPC - 1) + START)
                    act.activation(probs[:, t % (2 * TPC), q0:], ps_s[:, (u + t) % 3, q0:], ACT.Exp, scale=SCALE)\
                       .then_inc(p_ready, 1)

                def copy_o(n, c):
                    act.wait_ge(pv_done, n * GROUPS + CHUNK_END[c] + 1 + START)
                    act.wait_ge(fin_ps, upto(n, 4, c - 1) + START)
                    act.activation(o_sb[:, c % 2, :], ps_o[:, :], ACT.Copy).then_inc(o_copied, 1)

                def step(n, u, last, before_last=None):
                    for q in range(GROUPS):
                        if last is not None:
                            for t in range(q * TPC, (q + 1) * TPC):
                                exp(last, (u + 2) % 3, t)
                        if q == 0 and before_last is not None:
                            copy_o(before_last, 3)
                        if q in O_AT and last is not None:
                            copy_o(last, O_AT[q])
                        if q == 0 and last is not None:
                            high(last, 3)
                        if q in TURN_AT and n is not None:
                            high(n, TURN_AT[q])
                act.wait_ge(init, 6 + START)
                step(0, 0, None)
                step(1, 1, 0)
                with act.Fori(0, TRIPLES) as i:
                    for v in range(3):
                        step(3 * i + v + 2, (v + 2) % 3, 3 * i + v + 1, 3 * i + v)
                step(None, HEADS % 3, HEADS - 1, HEADS - 2)
                copy_o(HEADS - 1, 3)

            @block.tensor
            def _(pe):
                pe.wait_ge(init, 6 + START)
                pe.wait_ge(own, 3 + START)

                def scores_for_max(n, u, x):
                    i, c, w = MAXES[x]
                    diagonal = (i + 1) * P == c * CT + w
                    pe.wait_ge(max_used, upto(n, NT * PER_MAX, (x - 2) * PER_MAX) + START)
                    mm = pe.matmul(ps_m[:, (u + x) % 3, 0:w], q_st[u][0:MROW, i * P:(i + 1) * P],
                                   k_st[u][0:MROW, c * CT:c * CT + w], start=True, stop=not diagonal)
                    if diagonal:
                        mm = pe.matmul(ps_m[:, (u + x) % 3, w - P:w], g.ident_bf[:, :], g.mask_bf[:, 0:P],
                                       start=False, stop=True)
                    mm.then_inc(max_ps, 1)

                def turn(n, c, normalised):
                    pe.wait_ge(chunk_max, n * 4 + c + 1 + START)
                    pe.wait_ge(m_lo, n * 4 + c + START)
                    pe.wait_ge(fin_used, normalised + START)
                    pe.transpose(turned, mx[:, c * TPC:(c + 1) * TPC], g.const[:, C_IDENT:C_IDENT + P])\
                      .then_inc(m_turned, 1)

                def scores(n, u, t):
                    c, kt, q0 = TILES_OF[t]
                    out, diag = ps_s[:, (u + t) % 3], kt - c * TPC
                    pe.wait_ge(mrow_in[c], n * 32 + 32 + START)
                    pe.wait_ge(p_ready, upto(n, NT, t - 2) + START)
                    mm = pe.matmul(out[:, q0:], k_st[u][:, kt * P:(kt + 1) * P], q_st[u][:, c * CT + q0:(c + 1) * CT],
                                   start=True, stop=diag < 0)
                    if diag >= 0:
                        w = P * (1 + diag % 2)
                        mm = pe.matmul(out[:, q0:q0 + w], g.ident_bf[:, :], g.mask_bf[:, 3 * P - w:3 * P],
                                       start=False, stop=True)
                    mm.then_inc(s_ps, 1)

                def times_v(n, u, q):
                    pe.wait_ge(p_ready, n * NT + (q + 1) * TPC + START)
                    if TILES_OF[q * TPC][1] == 0:
                        pe.wait_ge(o_copied, n * 4 + TILES_OF[q * TPC][0] + START)
                    for t in range(q * TPC, (q + 1) * TPC):
                        c, kt, q0 = TILES_OF[t]
                        r = 32 * (kt % TPC)
                        mm = pe.matmul(ps_o[r:r + 32, q0:], v_st[u][:, kt, :], probs[:, t % (2 * TPC), q0:],
                                       start=kt < TPC, stop=kt >= c * TPC, tile_position=(0, r))
                    mm.then_inc(pv_done, 1)

                def sums(n, c, turned_read):
                    pe.wait_ge(o_copied, n * 4 + c + 1 + START)
                    pe.wait_ge(m_lo, turned_read + START)
                    if c == 0:
                        pe.wait_ge(fin_used, n + START)
                    for j in range(TPC):
                        rows = P // 2 if c == 0 and j < 2 else P
                        mm = pe.matmul(fin[:, c * TPC + j, :], o_sb[0:rows, c % 2, j * P:(j + 1) * P],
                                       g.const[0:rows, C_SEL:C_SEL + SELW], start=True, stop=True)
                    mm.then_inc(fin_ps, 1)

                def step(n, u, last, before_last=None, nth=0):
                    if n is not None:
                        pe.wait_ge(stack_in[u], ONES + (nth + 1) * LOADS + START)
                    if last is not None:
                        pe.wait_ge(v_in, last + 1 + START)
                    for q in range(GROUPS):
                        for r in range(TPC):
                            if r == TPC - 1 and q and last is not None:
                                times_v(last, (u + 2) % 3, q - 1)
                            if r == TPC - 1 and q == 0 and before_last is not None:
                                times_v(before_last, (u + 1) % 3, GROUPS - 1)
                            if last is not None:
                                scores(last, (u + 2) % 3, q * TPC + r)
                            if n is not None:
                                scores_for_max(n, u, q * TPC + r)
                        if q == 0 and last is not None:
                            turn(last, 3, 0 if before_last is None else before_last)
                        if q in TURN_AT and n is not None:
                            turn(n, TURN_AT[q], 0 if before_last is None else before_last + 1)
                        new = sum(at <= q for at in TURN_AT)
                        read = (lambda k: k * 4 + new) if n is not None else (lambda k: HEADS * 4)
                        if q + GROUPS in SUMS_AT and before_last is not None:
                            sums(before_last, SUMS_AT[q + GROUPS], read(n))
                        if q in SUMS_AT and last is not None:
                            sums(last, SUMS_AT[q], read(n))
                step(0, 0, None)
                step(1, 1, 0)
                with pe.Fori(0, TRIPLES) as i:
                    for v in range(3):
                        step(3 * i + v + 2, (v + 2) % 3, 3 * i + v + 1, 3 * i + v, i + (v + 2) // 3)
                step(None, HEADS % 3, HEADS - 1, HEADS - 2)
                times_v(HEADS - 1, (HEADS - 1) % 3, GROUPS - 1)
                sums(HEADS - 1, 3, HEADS * 4)


FF = 1024
KF = FF // P


def phase_ffn(nc, top, g):
    with ExitStack() as ctx:
        sb = lambda name, shape, dt=F32: ctx.enter_context(nc.sbuf_tensor(name, shape, dt))
        pb = lambda name, shape, dt=F32: ctx.enter_context(nc.psum_tensor(name, shape, dt))
        sem = Semaphores(nc, ctx)
        ow32 = sb("ow32", [P, KD, D])
        owh = sb("owh", [P, KD, D], FR)
        owl = sb("owl", [P, KD, D], FR)
        ob = sb("ob", [P, D])
        hf = sb("ffn_h", [P, KF, CT])
        raw = hf[:, :, :].rearrange("p k n -> p (k n)")
        up32 = raw[:, 0:KD * FF].rearrange("p (k n) -> p k n", n=FF)
        dn32 = raw[:, KD * FF:KD * FF + KF * D].rearrange("p (k n) -> p k n", n=D)
        up = sb("up_ternary", [P, KD, FF], FR)
        dn = sb("dn_ternary", [P, KF, D], FR)
        absum = sb("absum", [P, 2])
        alpha = sb("alpha", [P, 2])
        alpha_neg = sb("alpha_neg", [P, 2])
        att_st = sb("att_st", [P, TPC, D])
        ones = sb("ffn_ones", [P, P])
        stats = sb("ffn_stats", [P, TPC, 6])
        mv = sb("ffn_mv", [P, TPC, 2])
        sd = sb("ffn_sd", [P, TPC])
        xn = sb("ffn_xn", [P, TPC, D])
        sv = sb("ffn_sv", [P, TPC])
        rr = sb("ffn_rr", [P, TPC])
        ath = sb("ffn_ath", [P, KD, CT], FR)
        atl = sb("ffn_atl", [P, KD, CT], FR)
        hrms = sb("ffn_hrms", [P, TPC])
        hrr = sb("ffn_hrr", [P, TPC])
        th = sb("ffn_th", [P, KD, CT], FR)
        tl = sb("ffn_tl", [P, KD, CT], FR)
        hh = sb("ffn_hh", [P, KF, CT], FR)
        hl = sb("ffn_hl", [P, KF, CT], FR)
        below = g.v[:, 0:KD * FF // D, :].rearrange("p t n -> p (t n)")
        ps_t = pb("ffn_ps_t", [P, KD, CT])
        ps_y = pb("ffn_ps_y", [P, TPC, D])
        ps_u = pb("ffn_ps_u", [P, 2, CT])
        ps_r = pb("ffn_ps_r", [P, CT])

        ow_in = sem("ow_in")
        w_in = sem("ffn_w_in")
        setup = sem("ffn_setup")
        ones_ready = sem("ffn_ones_ready")
        ow_hi = sem("ow_hi")
        ow_lo = sem("ow_lo")
        al_ps = sem("alpha_ps")
        own_front = sem("ffn_own_front")
        own_back = sem("ffn_own_back")
        staged = sem("att_staged")
        biased = sem("ffn_biased")
        at_ps = sem("at_turned")
        at_hi = sem("at_hi")
        at_lo = sem("at_lo")
        y_ps = sem("proj_ps")
        y_read = sem("proj_read")
        var_ready = sem("ffn_var_ready")
        sd_ready = sem("ffn_sd_ready")
        rr_ready = sem("ffn_rr_ready")
        xn_ready = sem("ffn_xn_ready")
        xt_ps = sem("ffn_xt_turned")
        xt_hi = sem("ffn_xt_hi")
        xt_lo = sem("ffn_xt_lo")
        u_ps = sem("up_ps")
        h_ready = sem("h_ready")
        h_hi = sem("h_hi")
        h_lo = sem("h_lo")
        h_sq = sem("h_sq")
        r_ps = sem("h_sumsq_ps")
        hrms_ready = sem("hrms_ready")
        dn_ps = sem("dn_ps")
        x_done = sem("ffn_x_done")

        EARLY = 5
        sem.start()
        with nc.Block() as block:
            @block.sync
            def _(sp):
                def stage(a):
                    sp.wait_ge(at_ps, a + START)
                    sp.dma_start(att_st[:, :, :], g.att[:, ds(a * TPC, TPC), :]).then_inc(staged, 16)
                sp.dma_start(ow32[:, :, :], g.out_w.rearrange("(k p) n -> p k n", p=P)).then_inc(ow_in, 16)
                sp.dma_start(ob[:, :], g.out_b.rearrange("(o n) -> o n", o=1).broadcast_to([P, D])).then_inc(ow_in, 16)
                stage(0)
                sp.dma_start(up32[:, :, :], g.up_t.rearrange("(k p) n -> p k n", p=P)).then_inc(w_in, 16)
                sp.dma_start(dn32[:, :, :], g.down_t.rearrange("(k p) n -> p k n", p=P)).then_inc(w_in, 16)
                with sp.Fori(1, CHUNKS) as a:
                    stage(a)

            @block.gpsimd
            def _(pool):
                pool.memset(ones[:, :], 1.0).then_inc(ones_ready, 1)
                pool.wait_ge(ow_in, 32 + START)

                def add_bias(a):
                    xs = g.x[:, ds(a * TPC, TPC), :]
                    pool.tensor_tensor(xs, xs, ob[:, :].rearrange("p (o n) -> p o n", o=1)
                                       .broadcast_to([P, TPC, D]), ALU.add).then_inc(biased, 1)

                def squares(b):
                    for m in range(KF):
                        pool.wait_ge(h_hi, b * KF + m + 1 + START)
                        pool.wait_ge(h_lo, b * KF + m + 1 + START)
                        pool.tensor_tensor(hf[:, m, :], hf[:, m, :], hf[:, m, :], ALU.mult).then_inc(h_sq, 1)
                        if m:
                            pool.wait_ge(h_sq, b * (2 * KF - 1) + 2 * m + START)
                            pool.tensor_tensor(hf[:, 0, :], hf[:, 0, :], hf[:, m, :], ALU.add).then_inc(h_sq, 1)
                add_bias(0)
                add_bias(1)
                with pool.Fori(0, CHUNKS - 2) as b:
                    squares(b)
                    add_bias(b + 2)
                squares(CHUNKS - 2)
                squares(CHUNKS - 1)

            @block.vector
            def _(dve):
                dve.wait_ge(ow_hi, 1 + START)
                dve.tensor_tensor(owl[:, :, :], ow32[:, :, :], owh[:, :, :].bitcast(F32), ALU.subtract).then_inc(ow_lo, 1)

                def low(b, m):
                    dve.wait_ge(h_hi, b * KF + m + 1 + START)
                    dve.tensor_tensor(hl[:, m, :], hf[:, m, :], hh[:, m, :].bitcast(F32), ALU.subtract)\
                       .then_inc(h_lo, 1)

                def attention_low(a):
                    dve.wait_ge(at_hi, a + 1 + START)
                    dve.tensor_tensor(atl[:, :, :], ps_t[:, :, :], ath[:, :, :].bitcast(F32), ALU.subtract)\
                       .then_inc(at_lo, 1)

                KA, KB = TPC + 1, 2

                def step(a=None, b=None, ahead=None):
                    if a is not None:
                        st = Steps(dve, own_front, a * KA)
                        xs = g.x[:, ds(a * TPC, TPC), :]
                    if b is not None:
                        dve.wait_ge(dn_ps, b * TPC + START)
                        for m in range(EARLY):
                            low(b, m)
                    if a is not None:
                        dve.wait_ge(biased, a + 1 + START)
                        dve.wait_ge(y_ps, a + 1 + START)
                        dve.tensor_tensor(xs, xs, ps_y[:, :, :], ALU.add).then_inc(y_read, 1)
                    if b is not None:
                        for m in range(EARLY, KF - 2):
                            low(b, m)
                    if a is not None:
                        dve.wait_ge(y_read, a + 1 + START)
                        on_its_own(dve, g)
                        for j in range(TPC):
                            st.add(dve.bn_stats(stats[:, j, :], g.x[:, ds(a * TPC + j, 1), :]))
                    if b is not None:
                        for m in range(KF - 2, KF):
                            low(b, m)
                    if a is not None:
                        st.last()
                        on_its_own(dve, g)
                        for j in range(TPC):
                            last = dve.bn_aggr(mv[:, j, :], stats[:, j, :])
                        last.then_inc(var_ready, 1)
                    if a is not None:
                        dve.wait_ge(sd_ready, (a + 1) * 2 + START)
                        st.add(dve.scalar_tensor_tensor(out=rr[:, :], in0=sd[:, :], scalar=1e-8, in1=sv[:, :],
                                                        op0=ALU.mult, op1=ALU.add))
                        st.last()
                        dve.reciprocal(rr[:, :], rr[:, :]).then_inc(rr_ready, 1)
                        dve.wait_ge(rr_ready, a + 1 + START)
                        for j in range(TPC):
                            last = dve.tensor_scalar(xn[:, j, :], g.x[:, ds(a * TPC + j, 1), :], mv[:, j, 0:1],
                                                     rr[:, j:j + 1], ALU.subtract, ALU.mult)
                        last.then_inc(xn_ready, 1)
                        assert st.n == KA
                        dve.wait_ge(xt_hi, a + 1 + START)
                        dve.tensor_tensor(tl[:, :, :], ps_t[:, :, :], th[:, :, :].bitcast(F32), ALU.subtract)\
                           .then_inc(xt_lo, 1)
                    if ahead is not None:
                        attention_low(ahead)
                    if b is not None:
                        st = Steps(dve, own_back, b * KB)
                        dve.wait_ge(hrms_ready, b + 1 + START)
                        st.add(dve.tensor_scalar(hrr[:, :], hrms[:, :], 1e-8, None, ALU.add))
                        st.last()
                        st.add(dve.reciprocal(hrr[:, :], hrr[:, :]))
                        st.last()
                        for j in range(TPC):
                            xj = g.x[:, ds(b * TPC + j, 1), :]
                            dve.wait_ge(dn_ps, b * TPC + j // 2 * 2 + 2 + START)
                            dve.scalar_tensor_tensor(out=xj, in0=ps_y[:, j:j + 1, :], scalar=hrr[:, j:j + 1], in1=xj,
                                                     op0=ALU.mult, op1=ALU.add).then_inc(x_done, 1)
                        assert st.n == KB
                attention_low(0)
                step(a=0, ahead=1)
                dve.wait_ge(w_in, 32 + START)
                s = Steps(dve, setup)
                s.add(dve.tensor_reduce(absum[:, 0:1], up32[:, :, :], AX.XY, ALU.add, apply_absolute_value=True))
                s.add(dve.tensor_reduce(absum[:, 1:2], dn32[:, :, :], AX.XY, ALU.add, apply_absolute_value=True))
                dve.wait_ge(al_ps, 1 + START)
                s.add(dve.tensor_scalar(alpha[:, :], ps_r[:, 0:2], 1.0 / (D * FF), 0.5, ALU.mult, ALU.mult))
                s.last()
                s.add(dve.tensor_scalar(alpha_neg[:, :], alpha[:, :], -1.0, None, ALU.mult))
                s.last()
                for i, (src, dst) in enumerate(((up32, up), (dn32, dn))):
                    t = below.rearrange("p (k n) -> p k n", n=src.shape[2])
                    s.add(dve.tensor_scalar(t, src[:, :, :], alpha_neg[:, i:i + 1], None, ALU.is_lt))
                    s.last()
                    s.add(dve.scalar_tensor_tensor(out=dst[:, :, :], in0=src[:, :, :], scalar=alpha[:, i:i + 1],
                                                   in1=t, op0=ALU.is_gt, op1=ALU.subtract))
                    s.last()
                assert s.n == FFN_SETUP
                with dve.Fori(0, CHUNKS - 2) as b:
                    step(b + 1, b, b + 2)
                step(CHUNKS - 1, CHUNKS - 2)
                step(b=CHUNKS - 1)

            @block.scalar
            def _(act):
                act.wait_ge(ow_in, 32 + START)
                act.activation(owh[:, :, :], ow32[:, :, :], ACT.Copy).then_inc(ow_hi, 1)

                def gelu(b, m):
                    act.wait_ge(u_ps, b * KF + m + 1 + START)
                    act.activation(hf[:, m, :], ps_u[:, m % 2, :], ACT.Gelu).then_inc(h_ready, 1)

                def high(b, m):
                    act.wait_ge(h_ready, b * KF + m + 1 + START)
                    act.activation(hh[:, m, :], hf[:, m, :], ACT.Copy).then_inc(h_hi, 1)

                def attention_high(a):
                    act.wait_ge(at_ps, a + 1 + START)
                    act.wait_ge(y_ps, a + START)
                    act.activation(ath[:, :, :], ps_t[:, :, :], ACT.Copy).then_inc(at_hi, 1)

                def step(a=None, b=None, ahead=None):
                    if b is not None:
                        act.wait_ge(r_ps, b + START)
                        act.wait_ge(dn_ps, b * TPC + START)
                        for m in range(KF):
                            gelu(b, m)
                            if m:
                                high(b, m - 1)
                        high(b, KF - 1)
                    if a is not None:
                        act.wait_ge(var_ready, a + 1 + START)
                        act.activation(sd[:, :], mv[:, :, 1], ACT.Sqrt, bias=g.eps[:, 0:1]).then_inc(sd_ready, 1)
                        act.activation(sv[:, :], mv[:, :, 1], ACT.Sqrt).then_inc(sd_ready, 1)
                        act.wait_ge(xt_ps, a + 1 + START)
                        if b is not None:
                            act.wait_ge(u_ps, (b + 1) * KF + START)
                        act.activation(th[:, :, :], ps_t[:, :, :], ACT.Copy).then_inc(xt_hi, 1)
                    if ahead is not None:
                        attention_high(ahead)
                    if b is not None:
                        act.wait_ge(r_ps, b + 1 + START)
                        act.activation(hrms[:, :], ps_r[:, 0:TPC], ACT.Sqrt, scale=1.0 / FF).then_inc(hrms_ready, 1)
                attention_high(0)
                step(a=0, ahead=1)
                act.wait_ge(setup, FFN_SETUP + START)
                with act.Fori(0, CHUNKS - 2) as b:
                    step(b + 1, b, b + 2)
                step(CHUNKS - 1, CHUNKS - 2)
                step(b=CHUNKS - 1)

            @block.tensor
            def _(pe):
                ident = g.const[:, C_IDENT:C_IDENT + P]

                def turn(src, ready):
                    for k in range(KD):
                        for j in range(TPC):
                            last = pe.transpose(ps_t[:, k, j * P:(j + 1) * P], src[:, j, k * P:(k + 1) * P], ident)
                    last.then_inc(ready, 1)

                def project(a, b):
                    pe.wait_ge(at_lo, a + 1 + START)
                    if b is not None:
                        pe.wait_ge(x_done, b * TPC + START)
                    for j in range(TPC):
                        for k in range(KD):
                            t = slice(j * P, (j + 1) * P)
                            last = product3(pe, ps_y[:, j, :], ath[:, k, t], atl[:, k, t], owh[:, k, :], owl[:, k, :],
                                            k == 0, k == KD - 1)
                    last.then_inc(y_ps, 1)

                def up_product(b, m):
                    pe.wait_ge(h_ready, b * KF + max(m - 1, 0) + START)
                    w = slice(m * P, (m + 1) * P)
                    for k in range(KD):
                        pe.matmul(ps_u[:, m % 2, :], up[:, k, w], th[:, k, :], start=k == 0, stop=False)
                        last = pe.matmul(ps_u[:, m % 2, :], up[:, k, w], tl[:, k, :], start=False, stop=k == KD - 1)
                    last.then_inc(u_ps, 1)

                def down_product(b, j):
                    t = slice(j * P, (j + 1) * P)
                    for m in range(KF):
                        if j == 0:
                            pe.wait_ge(h_lo, b * KF + m + 1 + START)
                        pe.matmul(ps_y[:, j, :], hh[:, m, t], dn[:, m, :], start=m == 0, stop=False)
                        last = pe.matmul(ps_y[:, j, :], hl[:, m, t], dn[:, m, :], start=False, stop=m == KF - 1)
                    last.then_inc(dn_ps, 1)

                def sums_of_squares(b):
                    pe.wait_ge(h_sq, (b + 1) * (2 * KF - 1) + START)
                    pe.wait_ge(hrms_ready, b + START)
                    for j in range(TPC):
                        last = pe.matmul(ps_r[:, j:j + 1], hf[:, 0, j * P:(j + 1) * P], ones[:, 0:1],
                                         start=True, stop=True)
                    last.then_inc(r_ps, 1)

                def turn_attention(a):
                    pe.wait_ge(staged, (a + 1) * 16 + START)
                    pe.wait_ge(xt_lo, a + START)
                    turn(att_st, at_ps)

                def step(a=None, b=None, ahead=None):
                    if b is not None:
                        pe.wait_ge(xt_lo, b + 1 + START)
                        for m in range(EARLY):
                            up_product(b, m)
                    if a is not None:
                        project(a, b)
                    if b is not None:
                        for m in range(EARLY, KF):
                            up_product(b, m)
                        if a is not None:
                            pe.wait_ge(y_read, a + 1 + START)
                        for j in range(TPC - 1):
                            down_product(b, j)
                    if a is not None:
                        pe.wait_ge(xn_ready, a + 1 + START)
                        pe.wait_ge(at_lo, a + 1 + START)
                        turn(xn, xt_ps)
                    if b is not None:
                        down_product(b, TPC - 1)
                    if ahead is not None:
                        turn_attention(ahead)
                    if b is not None:
                        sums_of_squares(b)
                turn_attention(0)
                pe.wait_ge(ow_lo, 1 + START)
                step(a=0, ahead=1)
                pe.wait_ge(ones_ready, 1 + START)
                pe.wait_ge(setup, 2 + START)
                pe.matmul(ps_r[:, 0:2], ones[:, :], absum[:, :], start=True, stop=True).then_inc(al_ps, 1)
                pe.wait_ge(setup, FFN_SETUP + START)
                with pe.Fori(0, CHUNKS - 2) as b:
                    step(b + 1, b, b + 2)
                step(CHUNKS - 1, CHUNKS - 2)
                step(b=CHUNKS - 1)


FFN_SETUP = 8


def phase_ssm(nc, top, g):
    with ExitStack() as ctx:
        sb = lambda name, shape, dt=F32: ctx.enter_context(nc.sbuf_tensor(name, shape, dt))
        pb = lambda name, shape, dt=F32: ctx.enter_context(nc.psum_tensor(name, shape, dt))
        sem = Semaphores(nc, ctx)
        rate8 = sb("rate8", [P, D])
        c8 = sb("c8", [P, D])
        rate_b = sb("rate_b", [P, DB])
        c_b = sb("c_b", [P, DB])
        b_raw = sb("b_raw", [P, KD, NSTATE])
        b8 = sb("b8", [P, KD, TAUS, NSTATE])
        dvec = sb("dvec", [P, D])
        powers = sb("powers", [P, MT, D])
        taps = sb("taps", [P, MT, D])
        carry = sb("carry", [P, DB, T])
        decay = sb("decay", [P, DB])
        NBB = BLOCKS // BATCH
        SLOTS = NBB + 1
        scan_a = sb("scan_a", [P, DB, BATCH, SLOTS])
        states = sb("states", [P, DB, BATCH, SLOTS])
        inputs = scan_a[:, :, :, :].rearrange("p a b c -> p (a b c)")[:, 0:TOK]
        shifted = sb("shifted", [P, TOK])
        ln = LayerNorm(g, sb, sem, "ssm_ln")
        xn = [sb(f"ssm_xn{u}", [P, TPC, D]) for u in range(2)]
        xt = [g.v[:, u * TPC:(u + 1) * TPC, :].rearrange("p t n -> p (t n)").rearrange("p (k n) -> p k n", n=CT)
              for u in range(2)]
        ident = g.const[:, C_IDENT:C_IDENT + P]
        ps_t = pb("ssm_ps_t", [P, KD, CT])
        ps_b = pb("ssm_ps_b", [P, 2, CT])
        ps_f = pb("ssm_ps_f", [P, 2 * TPC, D])

        w_in = sem("ssm_w_in")
        rates = sem("ssm_rates")
        b_ready = sem("ssm_b_ready")
        direct = sem("ssm_direct")
        xt_ps = sem("ssm_xt_ps")
        xt_ready = sem("ssm_xt_ready")
        in_ps = sem("ssm_in_ps")
        in_ready = sem("ssm_in_ready")
        shift_in = sem("ssm_shift_in")

        sem.start()
        with nc.Block() as block:
            @block.sync
            def _(sp):
                for t in range(TAUS):
                    rows = slice(t * NSTATE, (t + 1) * NSTATE)
                    sp.dma_start(rate8[rows, :], g.log_a_t).then_inc(w_in, 16)
                    sp.dma_start(c8[rows, :], g.c_t).then_inc(w_in, 16)
                sp.dma_start(rate_b[:, :], g.log_a_blocks).then_inc(w_in, 16)
                sp.dma_start(c_b[:, :], g.c_blocks).then_inc(w_in, 16)
                sp.dma_start(b_raw[:, :, :], g.b_t.rearrange("(k p) s -> p k s", p=P)).then_inc(w_in, 16)
                sp.dma_start(dvec[:, :], g.d_vec.rearrange("(o n) -> o n", o=1).broadcast_to([P, D])).then_inc(w_in, 16)
                sp.wait_ge(in_ready, CHUNKS + START)
                sp.wait_ge(b_ready, 3 + START)
                for t in range(TAUS):
                    rows = slice(t * NSTATE, (t + 1) * NSTATE)
                    sp.dma_start(shifted[rows, t:TOK], inputs[rows, 0:TOK - t]).then_inc(shift_in, 16)
                sp.wait_ge(shift_in, TAUS * 16 + START)

            @block.vector
            def _(dve):
                dve.memset(shifted[:, 0:TAUS], 0.0).then_inc(b_ready, 1)

                def start(c, u):
                    ln.variance(dve, c, u)
                    if there(c + 1):
                        ln.spread(dve, c + 1, 1 - u)

                def norm(c, u):
                    ln.invert(dve, c)
                    if not isinstance(c, int) or c >= 2:
                        dve.wait_ge(xt_ps, c - 1 + START)
                        dve.wait_ge(direct, (c - 1) * 2 + START)
                    ln.normal(dve, c, xn[u])

                def step(it, u):
                    if there(it + 2):
                        start(it + 2, u)
                        norm(it + 2, u)
                    dve.wait_ge(in_ps, it + 1 + START)
                    dve.tensor_copy(inputs[:, ds(it * CT, CT)], ps_b[:, u, :]).then_inc(in_ready, 1)
                ln.spread(dve, 0, 0)
                start(0, 0)
                norm(0, 0)
                start(1, 1)
                norm(1, 1)
                dve.wait_ge(w_in, 16 * (2 * TAUS + 4) + START)
                for k in range(KD):
                    dve.tensor_copy(b8[:, k, :, :], b_raw[:, k:k + 1, :].broadcast_to([P, TAUS, NSTATE])).then_inc(b_ready, 1)
                dve.wait_ge(rates, 3 + START)
                dve.tensor_tensor(carry[:, :, :], rate_b[:, :].rearrange("p (b o) -> p b o", o=1).broadcast_to([P, DB, T]),
                                  g.const[:, C_STEP:C_STEP + T].rearrange("p (o r) -> p o r", o=1)
                                  .broadcast_to([P, DB, T]), ALU.mult).then_inc(rates, 1)
                in_pairs(dve, step, 2)

            @block.gpsimd
            def _(pool):
                def step(it, u):
                    pool.wait_ge(ln.ready, it + 1 + START)
                    pool.wait_ge(w_in, 16 * (2 * TAUS + 4) + START)
                    xs = g.x[:, ds(it * TPC, TPC), :]
                    pool.wait_ge(xt_ps, it + 1 + START)
                    pool.tensor_tensor(xn[u][:, :, :], xn[u][:, :, :], dvec[:, :].rearrange("p (o d) -> p o d", o=1)
                                       .broadcast_to([P, TPC, D]), ALU.mult).then_inc(direct, 1)
                    pool.wait_ge(direct, it * 2 + 1 + START)
                    pool.tensor_tensor(xs, xs, xn[u][:, :, :], ALU.add).then_inc(direct, 1)
                in_pairs(pool, step)

            @block.scalar
            def _(act):

                def keep(c, u):
                    act.wait_ge(xt_ps, c + 1 + START)
                    act.wait_ge(in_ps, c - 1 + START)
                    act.activation(xt[u][:, :, :], ps_t[:, :, :], ACT.Copy).then_inc(xt_ready, 1)

                def step(it, u):
                    if there(it + 1):
                        keep(it + 1, 1 - u)
                    if there(it + 2):
                        ln.deviation(act, it + 2)
                ln.deviation(act, 0)
                ln.deviation(act, 1)
                keep(0, 0)
                act.wait_ge(w_in, 16 * (2 * TAUS + 4) + START)
                act.activation(rate8[:, :], rate8[:, :], ACT.Exp).then_inc(rates, 1)
                act.activation(rate_b[:, :], rate_b[:, :], ACT.Exp).then_inc(rates, 1)
                act.wait_ge(rates, 2 + START)
                act.activation(decay[:, :], rate_b[:, :], ACT.Exp, scale=-float(T)).then_inc(rates, 1)
                for m in range(MT):
                    act.activation(powers[:, m, :], rate8[:, :], ACT.Exp,
                                   scale=g.const[:, C_NEG_TAU + m:C_NEG_TAU + m + 1])
                act.wait_ge(rates, 4 + START)
                act.activation(carry[:, :, :], carry[:, :, :], ACT.Exp).then_inc(rates, 1)
                in_pairs(act, step)

            @block.tensor
            def _(pe):
                def turn(c, u):
                    pe.wait_ge(ln.ready, c + 1 + START)
                    pe.wait_ge(xt_ready, c + START)
                    for k in range(KD):
                        for j in range(TPC):
                            last = pe.transpose(ps_t[:, k, j * P:(j + 1) * P], xn[u][:, j, k * P:(k + 1) * P], ident)
                    last.then_inc(xt_ps, 1)

                def step(it, u):
                    if there(it + 1):
                        turn(it + 1, 1 - u)
                    pe.wait_ge(xt_ready, it + 1 + START)
                    pe.wait_ge(in_ready, it - 1 + START)
                    for k in range(KD):
                        last = pe.matmul(ps_b[:, u, :], b8[:, k, :, :], xt[u][:, k, :], start=k == 0, stop=k == KD - 1)
                    last.then_inc(in_ps, 1)
                turn(0, 0)
                pe.wait_ge(b_ready, 3 + START)
                in_pairs(pe, step)

        powers_s = [sb(f"powers_s{u}", [P, MT, TAUS, NSTATE]) for u in range(2)]
        BPC = CT // T
        delayed = [sb(f"delayed{u}", [P, MT, BPC, T]) for u in range(2)]
        tables = sem("ssm_tables")
        ps_ready = sem("powers_s_ready")
        end_ps = sem("end_ps")
        end_ready = sem("end_ready")
        scanned = sem("scanned")
        same_s = g.const[:, C_SAME_S:C_SAME_S + NSTATE].rearrange("p (a b s) -> p a b s", a=1, b=1)\
            .broadcast_to([P, MT, TAUS, NSTATE])
        sem.start()
        with nc.Block() as block:
            @block.gpsimd
            def _(pool):
                pool.tensor_copy(scan_a[:, :, :, :].rearrange("p a b c -> p a (b c)"),
                                 decay[:, :].rearrange("p (a o) -> p a o", o=1).broadcast_to([P, DB, BATCH * SLOTS]))\
                    .then_inc(tables, 1)
                pool.memset(states[:, :, :, 0:1], 0.0).then_inc(tables, 1)
                pool.wait_ge(tables, 1 + START)
                pool.memset(scan_a[:, :, :, 0:1], 0.0).then_inc(tables, 1)
                pool.tensor_tensor(taps[:, :, :], powers[:, :, :], c8[:, :].rearrange("p (o d) -> p o d", o=1)
                                   .broadcast_to([P, MT, D]), ALU.mult).then_inc(tables, 1)
                for u in range(2):
                    pool.memset(delayed[u][:, :, :, :], 0.0).then_inc(tables, 1)

            @block.vector
            def _(dve):
                with dve.Fori(0, DB // 2) as i:
                    for u in range(2):
                        dve.wait_ge(end_ps, 2 * i + u - 1 + START)
                        pw = powers[:, :, ds((2 * i + u) * TAUS, TAUS)].rearrange("p m (g o) -> p m g o", o=1)
                        dve.tensor_tensor(powers_s[u][:, :, :, :], pw.broadcast_to([P, MT, TAUS, NSTATE]), same_s,
                                          ALU.mult).then_inc(ps_ready, 1)
                dve.wait_ge(end_ready, DB + START)
                dve.wait_ge(tables, 4 + START)
                flat = lambda x: x[:, :, :, :].rearrange("p a b c -> p (a b c)")
                dve.tensor_tensor_scan(flat(states), flat(scan_a), flat(states), 0.0, ALU.mult, ALU.add)\
                    .then_inc(scanned, 1)

            @block.scalar
            def _(act):
                with act.Fori(0, DB // 2) as i:
                    for u in range(2):
                        act.wait_ge(end_ps, 2 * i + u + 1 + START)
                        act.activation(states[:, ds(2 * i + u, 1), :, 1:],
                                       ps_b[:, u, 0:BLOCKS].rearrange("p (o b c) -> p o b c", o=1, b=BATCH), ACT.Copy)\
                            .then_inc(end_ready, 1)

            @block.tensor
            def _(pe):
                ends = shifted[:, :].rearrange("p (c t) -> p c t", t=T)
                with pe.Fori(0, DB // 2) as i:
                    for u in range(2):
                        pe.wait_ge(ps_ready, 2 * i + u + 1 + START)
                        pe.wait_ge(end_ready, 2 * i + u - 1 + START)
                        for m in range(MT):
                            last = pe.matmul(ps_b[:, u, 0:BLOCKS], powers_s[u][:, m, :, :], ends[:, :, T - 1 - TAUS * m],
                                             start=m == 0, stop=m == MT - 1)
                        last.then_inc(end_ps, 1)

        NB = 4
        diag = [g.v[:, (2 + u) * TPC:(3 + u) * TPC, :].rearrange("p t n -> p (t n)")
                .rearrange("p (a b c) -> p a b c", a=TAUS, b=BATCH) for u in range(NB)]
        carry_c = [sb(f"carry_c{u}", [P, T]) for u in range(NB)]
        diag_ready = sem("diag_ready")
        carry_ready = sem("carry_ready")
        inj_ps = sem("inj_ps")
        inj_ready = sem("inj_ready")
        QG = P // T
        sem.start()
        with nc.Block() as block:
            def diagonal(eng, d, u, b, ready):
                eng.tensor_tensor(diag[u][:, :, b, :], states[:, ds(d, 1), b, 0:NBB].broadcast_to([P, TAUS, NBB]),
                                  g.const[:, C_SAME_G:C_SAME_G + TAUS].rearrange("p (g o) -> p g o", o=1)
                                  .broadcast_to([P, TAUS, NBB]), ALU.mult).then_inc(ready, 1)

            @block.gpsimd
            def _(pool):
                with pool.Fori(0, DB // NB) as i:
                    for u in range(NB):
                        pool.wait_ge(inj_ps, NB * (i - 1) + u + 1 + START)
                        pool.tensor_tensor(carry_c[u][:, :], carry[:, ds(NB * i + u, 1), :],
                                           c_b[:, ds(NB * i + u, 1)].broadcast_to([P, T]), ALU.mult)\
                            .then_inc(carry_ready, 1)
                        if u % 2:
                            diagonal(pool, NB * i + u, u, 1, carry_ready)

            @block.vector
            def _(dve):
                with dve.Fori(0, DB // NB) as i:
                    for u in range(NB):
                        dve.wait_ge(inj_ps, NB * (i - 1) + u + 1 + START)
                        for b in range(BATCH - u % 2):
                            diagonal(dve, NB * i + u, u, b, diag_ready)

            @block.scalar
            def _(act):
                with act.Fori(0, DB // NB) as i:
                    for u in range(NB):
                        act.wait_ge(inj_ps, NB * i + u + 1 + START)
                        act.activation(g.att[:, :, ds((NB * i + u) * TAUS, TAUS)],
                                       ps_b[:, u % 2, 0:D].rearrange("p (g t) -> p t g", g=TAUS), ACT.Copy)\
                            .then_inc(inj_ready, 1)

            @block.tensor
            def _(pe):
                with pe.Fori(0, DB // NB) as i:
                    for u in range(NB):
                        pe.wait_ge(diag_ready, 3 * (2 * i + u // 2) + 2 + u % 2 + START)
                        pe.wait_ge(carry_ready, 3 * (2 * i + u // 2) + 1 + 2 * (u % 2) + START)
                        pe.wait_ge(inj_ready, NB * i + u - 1 + START)
                        for q in range(QG):
                            rhs = diag[u][:, :, :, :].rearrange("p g b (t q) -> p (g b) t q", q=QG)[:, :, :, q]
                            last = pe.matmul(ps_b[q * T:(q + 1) * T, u % 2, 0:D], carry_c[u][:, :], rhs, start=True,
                                             stop=True, tile_position=(0, q * T))
                        last.then_inc(inj_ps, 1)

        pad_ready = sem("pad_ready")
        fir_ps = sem("fir_ps")
        x_own = sem("ssm_x_own")
        x_ready = sem("ssm_x_ready")
        sem.start()
        with nc.Block() as block:
            @block.gpsimd
            def _(pool):
                with pool.Fori(0, CHUNKS // 2) as i:
                    for u in range(2):
                        it = 2 * i + u
                        pool.wait_ge(fir_ps, it - 1 + START)
                        for m in range(MT):
                            n = T - TAUS * m
                            b = shifted[:, ds(it * CT, CT)].rearrange("p (c t) -> p c t", t=T)
                            pool.tensor_tensor(delayed[u][:, m, :, TAUS * m:], b[:, :, 0:n],
                                               g.const[:, C_TAU_MASK:C_TAU_MASK + n].rearrange("p (o t) -> p o t", o=1)
                                               .broadcast_to([P, BPC, n]), ALU.mult).then_inc(pad_ready, 1)

            @block.vector
            def _(dve):
                with dve.Fori(0, CHUNKS // 2) as i:
                    for u in range(2):
                        it = 2 * i + u
                        xs = g.x[:, ds(it * TPC, TPC), :]
                        dve.tensor_tensor(xs, xs, g.att[:, ds(it * TPC, TPC), :], ALU.add).then_inc(x_own, 1)
                        dve.wait_ge(x_own, it + 1 + START)
                        dve.wait_ge(fir_ps, it + 1 + START)
                        dve.tensor_tensor(xs, xs, ps_f[:, u * TPC:(u + 1) * TPC, :], ALU.add).then_inc(x_ready, 1)

            @block.tensor
            def _(pe):
                with pe.Fori(0, CHUNKS // 2) as i:
                    for u in range(2):
                        pe.wait_ge(pad_ready, (2 * i + u + 1) * MT + START)
                        pe.wait_ge(x_ready, 2 * i + u - 1 + START)
                        for j in range(TPC):
                            for m in range(MT):
                                w = delayed[u][:, m, j * QG:(j + 1) * QG, :]
                                last = pe.matmul(ps_f[:, u * TPC + j, :], w, taps[:, m, :], start=m == 0,
                                                 stop=m == MT - 1)
                        last.then_inc(fir_ps, 1)


FI = 938
KI = -(-FI // P)
FLAST = FI - (KI - 1) * P
FMAIN = FI - FLAST
UP_AT = 64
NUP = 2 * FMAIN + UP_AT + FLAST
RUNS = CHUNKS + ROUTED
ORDER = [KI - 1, *range(KI - 1)]
SHARED = E
MOE_ROWS = ROUTED * CT


def fw(m):
    return P if m < KI - 1 else FLAST


def phase_moe(nc, top, g):
    slots_in = nc.dram_tensor("slots_in", (MOE_ROWS, D), F32, kind="Internal").ap()
    slots_out = nc.dram_tensor("slots_out", (MOE_ROWS, D), F32, kind="Internal").ap()
    with ExitStack() as ctx:
        sem = Semaphores(nc, ctx)
        keep = lambda name, shape, dt=F32: ctx.enter_context(nc.sbuf_tensor(name, shape, dt))
        slot = keep("slot", [P, TOPK, TILES], mybir.dt.int32)
        weight = keep("weight", [P, TOPK, TILES])
        experts = keep("experts", [P, ROUTED], mybir.dt.int32)
        logits = keep("logits", [P, TILES, E])
        weights = Weights(keep, sem)
        moe_norm(nc, g, sem, weights, slots_in, logits)
        moe_route(nc, g, sem, weights, logits, slot, weight, experts)
        moe_experts(nc, g, sem, weights, slots_in, slots_out, slot, experts)
        moe_combine(nc, g, sem, slots_out, slot, weight)


class Weights:

    def __init__(self, sb, sem):
        self.up32 = sb("moe_up32", [P, KD, NUP])
        self.uph = sb("moe_uph", [P, KD, NUP], FR)
        self.upl = sb("moe_upl", [P, KD, NUP], FR)
        self.dn32 = sb("moe_dn32", [P, KI, D])
        self.up_in = sem("ex_up_in")
        self.dn_in = sem("ex_dn_in")
        self.up_hi = sem("ex_up_hi")
        self.up_lo = sem("ex_up_lo")
        self.dn_lo = sem("ex_dn_lo")

    def load_up(self, sp, g, w, expert):
        sp.wait_ge(self.up_lo, w * KD + START)
        sp.dma_start(self.up32[:, :, :], g.w_up[ds(expert * D, D), :].rearrange("(k p) n -> p k n", p=P))\
          .then_inc(self.up_in, 16)

    def load_down(self, sp, g, w, expert):
        sp.wait_ge(self.dn_lo, w * KI + START)
        sp.dma_start(self.dn32[:, 0:KI - 1, :], g.w_down[ds(expert * FI, (KI - 1) * P), :]
                     .rearrange("(m p) n -> p m n", p=P)).then_inc(self.dn_in, 16)
        sp.dma_start(self.dn32[0:FLAST, KI - 1, :], g.w_down[ds(expert * FI + (KI - 1) * P, FLAST), :])\
          .then_inc(self.dn_in, 16)


def moe_norm(nc, g, sem, weights, slots_in, logits):
    with ExitStack() as ctx:
        sb = lambda name, shape, dt=F32: ctx.enter_context(nc.sbuf_tensor(name, shape, dt))
        pb = lambda name, shape, dt=F32: ctx.enter_context(nc.psum_tensor(name, shape, dt))
        gate = sb("gate", [P, KD, E])
        zero = sb("moe_zero", [P, TPC, D])
        ln = LayerNorm(g, sb, sem, "moe_ln")
        xn = [sb(f"moe_xn{u}", [P, TPC, D]) for u in range(2)]
        xt = [sb(f"moe_xt{u}", [P, KD, CT]) for u in range(2)]
        ident = g.const[:, C_IDENT:C_IDENT + P]
        ps_t = pb("moe_ps_t", [P, KD, CT])
        ps_l = pb("moe_ps_l", [P, 2, CT])
        gate_in = sem("gate_in")
        zero_ready = sem("moe_zero_ready")
        zero_out = sem("moe_zero_out")
        kept = sem("moe_xn_kept")
        xt_ps = sem("moe_xt_ps")
        xt_ready = sem("moe_xt_ready")
        lg_ps = sem("logits_ps")
        lg_ready = sem("logits_ready")
        sem.start()
        with nc.Block() as block:
            @block.sync
            def _(sp):
                sp.dma_start(gate[:, :, :], g.gate_t.rearrange("(k p) e -> p k e", p=P)).then_inc(gate_in, 16)
                sp.wait_ge(zero_ready, 1 + START)
                with sp.Fori(0, ROUTED) as i:
                    sp.dma_start(slots_in[ds(i * CT, CT), :].rearrange("(p t) n -> p t n", p=P),
                                 zero[:, :, :]).then_inc(zero_out, 16)
                weights.load_up(sp, g, 0, SHARED)
                weights.load_down(sp, g, 0, SHARED)
                sp.wait_ge(zero_out, ROUTED * 16 + START)

            @block.gpsimd
            def _(pool):
                def step(it, u):
                    pool.wait_ge(ln.ready, it + 1 + START)
                    on_its_own(pool, g)
                    pool.tensor_copy(g.v[:, ds(it * TPC, TPC), :], xn[u][:, :, :]).then_inc(kept, 1)
                in_pairs(pool, step)

            @block.vector
            def _(dve):
                def start(c, u):
                    ln.variance(dve, c, u)
                    if there(c + 1):
                        ln.spread(dve, c + 1, 1 - u)

                def norm(c, u):
                    ln.invert(dve, c)
                    if not isinstance(c, int) or c >= 2:
                        dve.wait_ge(xt_ps, c - 1 + START)
                        dve.wait_ge(kept, c - 1 + START)
                    ln.normal(dve, c, xn[u])

                def step(it, u):
                    if there(it + 2):
                        start(it + 2, u)
                        norm(it + 2, u)
                    dve.wait_ge(lg_ps, it + 1 + START)
                    dve.tensor_copy(logits[:, ds(it * TPC, TPC), :],
                                    ps_l[:, u, 0:TPC * E].rearrange("p (t e) -> p t e", e=E)).then_inc(lg_ready, 1)
                dve.memset(zero[:, :, :], 0.0).then_inc(zero_ready, 1)
                ln.spread(dve, 0, 0)
                start(0, 0)
                norm(0, 0)
                start(1, 1)
                norm(1, 1)
                in_pairs(dve, step, 2)

            @block.scalar
            def _(act):
                def keep(c, u):
                    act.wait_ge(xt_ps, c + 1 + START)
                    act.wait_ge(lg_ps, c - 1 + START)
                    act.activation(xt[u][:, :, :], ps_t[:, :, :], ACT.Copy).then_inc(xt_ready, 1)

                def step(it, u):
                    if there(it + 1):
                        keep(it + 1, 1 - u)
                    if there(it + 2):
                        ln.deviation(act, it + 2)
                ln.deviation(act, 0)
                ln.deviation(act, 1)
                keep(0, 0)
                in_pairs(act, step)

            @block.tensor
            def _(pe):
                def turn(c, u):
                    pe.wait_ge(ln.ready, c + 1 + START)
                    pe.wait_ge(xt_ready, c + START)
                    for k in range(KD):
                        for j in range(TPC):
                            last = pe.transpose(ps_t[:, k, j * P:(j + 1) * P], xn[u][:, j, k * P:(k + 1) * P], ident)
                    last.then_inc(xt_ps, 1)

                def step(it, u):
                    if there(it + 1):
                        turn(it + 1, 1 - u)
                    pe.wait_ge(xt_ready, it + 1 + START)
                    pe.wait_ge(lg_ready, it - 1 + START)
                    for j in range(TPC):
                        for k in range(KD):
                            last = pe.matmul(ps_l[:, u, j * E:(j + 1) * E], xt[u][:, k, j * P:(j + 1) * P], gate[:, k, :],
                                             start=k == 0, stop=k == KD - 1)
                    last.then_inc(lg_ps, 1)
                pe.wait_ge(gate_in, 16 + START)
                turn(0, 0)
                in_pairs(pe, step)


def moe_route(nc, g, sem, weights, logits, slot, weight, experts):
    with ExitStack() as ctx:
        sb = lambda name, shape, dt=F32: ctx.enter_context(nc.sbuf_tensor(name, shape, dt))
        pb = lambda name, shape, dt=F32: ctx.enter_context(nc.psum_tensor(name, shape, dt))
        ones = sb("rt_ones", [P, P])
        top_l = sb("top_logit", [P, TILES, 1])
        probs = sb("rt_probs", [P, TILES, E])
        psum_e = sb("rt_sum", [P, TILES, 1])
        score = sb("rt_score", [P, TILES, E])
        best = sb("rt_best", [P, TOPK, TILES, 1])
        place = sb("rt_place", [P, TILES, 1])
        chosen = sb("rt_chosen", [P, TOPK, TILES, E])
        member = sb("rt_member", [P, E, TILES])
        counts = sb("rt_counts", [P, E, TILES])
        keep_s = sb("rt_keep", [P, E, TILES])
        running = sb("rt_running", [P, E, TILES])
        where = sb("rt_where", [P, E, TILES])
        over = sb("rt_over", [P, E, CHUNKS])
        tiles = sb("rt_tiles", [P, E])
        tiles_upto = sb("rt_tiles_upto", [P, E])
        base = sb("rt_base", [P, E])
        past = sb("rt_past", [P, ROUTED, E])
        ex_f = sb("rt_experts", [P, ROUTED])
        slot_f = sb("rt_slot", [P, TOPK, TILES])
        denom = sb("rt_denom", [P, TILES])
        ps_rank = pb("ps_rank", [P, E, TILES])
        ps_count = pb("ps_count", [P, E, TILES])
        own = sem("rt_own")
        less_max = sem("rt_less_max")
        exp_done = sem("rt_exp_done")
        members = sem("rt_members")
        rank_ps = sem("rank_ps")
        slots = sem("rt_slots")
        sem.start()
        with nc.Block() as block:
            col = lambda a, w, n: g.const[:, a:a + w].rearrange("p (o e) -> p o e", o=1).broadcast_to([P, n, w])

            @block.vector
            def _(dve):
                st = Steps(dve, own)

                def do(instruction):
                    st.add(instruction)
                    st.last()
                each = lambda x: x.broadcast_to([P, TILES, E])
                do(dve.memset(ones[:, :], 1.0))
                do(dve.reduce_max(top_l[:, :, :], logits[:, :, :], AX.X))
                dve.tensor_tensor(probs[:, :, :], logits[:, :, :], each(top_l[:, :, :]), ALU.subtract).then_inc(less_max, 1)
                dve.wait_ge(exp_done, 1 + START)
                do(dve.reduce_sum(psum_e[:, :, :], probs[:, :, :], AX.X))
                do(dve.reciprocal(psum_e[:, :, :], psum_e[:, :, :]))
                do(dve.tensor_tensor(probs[:, :, :], probs[:, :, :], each(psum_e[:, :, :]), ALU.mult))
                for n in range(TOPK):
                    do(dve.reduce_max(best[:, n, :, :], probs[:, :, :], AX.X))
                    do(dve.tensor_tensor(score[:, :, :], probs[:, :, :], each(best[:, n, :, :]), ALU.is_equal))
                    do(dve.tensor_tensor(score[:, :, :], score[:, :, :], col(C_LEFT, E, TILES), ALU.mult))
                    do(dve.reduce_max(place[:, :, :], score[:, :, :], AX.X))
                    do(dve.tensor_tensor(chosen[:, n, :, :], each(place[:, :, :]), col(C_LEFT, E, TILES), ALU.is_equal))
                    if n == 0:
                        do(dve.scalar_tensor_tensor(out=probs[:, :, :], in0=chosen[:, 0, :, :], scalar=-2.0,
                                                    in1=probs[:, :, :], op0=ALU.mult, op1=ALU.add))
                do(dve.tensor_tensor(denom[:, :], best[:, 0, :, 0], best[:, 1, :, 0], ALU.add))
                do(dve.tensor_scalar(denom[:, :], denom[:, :], 1e-8, None, ALU.add))
                do(dve.reciprocal(denom[:, :], denom[:, :]))
                for n in range(TOPK):
                    do(dve.tensor_tensor(weight[:, n, :], best[:, n, :, 0], denom[:, :], ALU.mult))
                dve.tensor_tensor(member[:, :, :].rearrange("p e t -> p t e"), chosen[:, 0, :, :], chosen[:, 1, :, :],
                                  ALU.add).then_inc(members, 1)
                do(dve.memset(keep_s[:, :, :], 1.0))
                do(dve.memset(keep_s[:, :, 0:1], 0.0))
                dve.wait_ge(rank_ps, 1 + START)
                flat = lambda x: x[:, :, :].rearrange("p e t -> p (e t)")
                do(dve.tensor_copy(counts[:, :, :], ps_count[:, :, :]))
                do(dve.tensor_tensor_scan(flat(running), flat(keep_s), flat(counts), 0.0, ALU.mult, ALU.add))
                do(dve.tensor_tensor(over[:, :, :], running[:, :, TILES - 1:TILES].broadcast_to([P, E, CHUNKS]),
                                     col(C_LIMITS, CHUNKS, E), ALU.is_gt))
                do(dve.reduce_sum(tiles[:, :].rearrange("p (e o) -> p e o", o=1), over[:, :, :], AX.X))
                do(dve.tensor_tensor_scan(tiles_upto[:, :], ones[:, 0:E], tiles[:, :], 0.0, ALU.mult, ALU.add))
                do(dve.tensor_tensor(base[:, :], tiles_upto[:, :], tiles[:, :], ALU.subtract))
                do(dve.tensor_scalar(base[:, :], base[:, :], float(CT), None, ALU.mult))
                do(dve.tensor_tensor(where[:, :, :], running[:, :, :], counts[:, :, :], ALU.subtract))
                do(dve.tensor_tensor(where[:, :, :], where[:, :, :], ps_rank[:, :, :], ALU.add))
                do(dve.tensor_tensor(where[:, :, :], where[:, :, :], base[:, :].rearrange("p (e o) -> p e o", o=1)
                                     .broadcast_to([P, E, TILES]), ALU.add))
                for n in range(TOPK):
                    do(dve.tensor_tensor(chosen[:, n, :, :], chosen[:, n, :, :], where[:, :, :].rearrange("p e t -> p t e"),
                                         ALU.mult))
                    do(dve.reduce_sum(slot_f[:, n, :].rearrange("p (t o) -> p t o", o=1), chosen[:, n, :, :], AX.X))
                dve.tensor_copy(slot[:, :, :], slot_f[:, :, :]).then_inc(slots, 1)
                do(dve.tensor_tensor(past[:, :, :], tiles_upto[:, :].rearrange("p (o e) -> p o e", o=1)
                                     .broadcast_to([P, ROUTED, E]),
                                     g.const[:, C_TILE:C_TILE + ROUTED].rearrange("p (n o) -> p n o", o=1)
                                     .broadcast_to([P, ROUTED, E]), ALU.is_le))
                do(dve.reduce_sum(ex_f[:, :].rearrange("p (n o) -> p n o", o=1), past[:, :, :], AX.X))
                do(dve.tensor_scalar(ex_f[:, :], ex_f[:, :], float(E - 1), None, ALU.min))
                dve.tensor_copy(experts[:, :], ex_f[:, :]).then_inc(slots, 1)

            @block.scalar
            def _(act):
                act.wait_ge(less_max, 1 + START)
                act.activation(probs[:, :, :], probs[:, :, :], ACT.Exp).then_inc(exp_done, 1)
                act.wait_ge(weights.up_in, 16 + START)
                for k in range(KD):
                    act.activation(weights.uph[:, k, :], weights.up32[:, k, :], ACT.Copy).then_inc(weights.up_hi, 1)

            @block.gpsimd
            def _(pool):
                for k in range(KD):
                    pool.wait_ge(weights.up_hi, k + 1 + START)
                    pool.tensor_tensor(weights.upl[:, k, :], weights.up32[:, k, :], weights.uph[:, k, :].bitcast(F32),
                                       ALU.subtract).then_inc(weights.up_lo, 1)

            @block.tensor
            def _(pe):
                pe.wait_ge(members, 1 + START)
                pe.matmul(ps_rank[:, :, :], g.const[:, C_UPPER:C_UPPER + P], member[:, :, :], start=True, stop=True)
                pe.matmul(ps_count[:, :, :], ones[:, :], member[:, :, :], start=True, stop=True).then_inc(rank_ps, 1)


def moe_experts(nc, g, sem, weights, slots_in, slots_out, slot, experts):
    with ExitStack() as ctx:
        sb = lambda name, shape, dt=F32: ctx.enter_context(nc.sbuf_tensor(name, shape, dt))
        pb = lambda name, shape, dt=F32: ctx.enter_context(nc.psum_tensor(name, shape, dt))
        up32, uph, upl, dn32 = weights.up32, weights.uph, weights.upl, weights.dn32
        dnh = sb("moe_dnh", [P, KI, D], FR)
        dnl = sb("moe_dnl", [P, KI, D], FR)
        rows = sb("moe_rows", [P, TPC, D])
        xth = sb("moe_xth", [P, KD, CT], FR)
        xtl = sb("moe_xtl", [P, KD, CT], FR)
        silu = sb("moe_silu", [P, 2, CT])
        h32 = sb("moe_h32", [P, 2, CT])
        hh = sb("moe_hh", [P, KI, CT], FR)
        hl = sb("moe_hl", [P, KI, CT], FR)
        y = sb("moe_y", [P, TPC, D])
        ident = g.const[:, C_IDENT:C_IDENT + P]
        ps_t = pb("ex_ps_t", [P, KD, CT])
        ps_g = pb("ex_ps_g", [P, 2, CT])
        ps_u = pb("ex_ps_u", [P, 2, CT])
        ps_y = pb("ex_ps_y", [P, TPC, D])
        up_in, dn_in, up_hi, up_lo, dn_lo = weights.up_in, weights.dn_in, weights.up_hi, weights.up_lo, weights.dn_lo
        rows_in = sem("ex_rows_in")
        dn_hi = sem("ex_dn_hi")
        xt_ps = sem("ex_xt_ps")
        xt_hi = sem("ex_xt_hi")
        xt_lo = sem("ex_xt_lo")
        gu_ps = sem("ex_gu_ps")
        silu_ready = sem("ex_silu")
        h_ready = sem("ex_h")
        h_hi = sem("ex_h_hi")
        h_lo = sem("ex_h_lo")
        y_ps = sem("ex_y_ps")
        y_read = sem("ex_y_read")
        sent = sem.from_zero("rows_sent")
        y_out = sem("ex_y_out")
        sem.start()
        with nc.Block() as block:
            @block.sync
            def _(sp):
                def load_rows(i, src):
                    sp.wait_ge(xt_ps, i + START)
                    sp.dma_start(rows[:, :, :], src).then_inc(rows_in, 16)
                sp.dma_start(rows[:, :, :], g.v[:, 0:TPC, :]).then_inc(rows_in, 16)
                with sp.Fori(1, CHUNKS) as i:
                    load_rows(i, g.v[:, ds(i * TPC, TPC), :])
                first = sp.value_load(experts[0:1, 0:1], min_val=0, max_val=E - 1)
                weights.load_up(sp, g, 1, first)
                weights.load_down(sp, g, 1, first)
                sp.wait_ge(sent, TILES * TOPK * 16)
                routed = lambda i: slots_in[ds((i - CHUNKS) * CT, CT), :].rearrange("(t p) n -> p t n", p=P)
                load_rows(CHUNKS, routed(CHUNKS))
                with sp.Fori(CHUNKS, RUNS - 1) as i:
                    expert = sp.value_load(experts[0:1, ds(i - CHUNKS + 1, 1)], min_val=0, max_val=E - 1)
                    weights.load_up(sp, g, i - CHUNKS + 2, expert)
                    load_rows(i + 1, routed(i + 1))
                    weights.load_down(sp, g, i - CHUNKS + 2, expert)

            @block.gpsimd
            def _(pool):
                for t in range(TILES):
                    for n in range(TOPK):
                        pool.indirect_dma_start(out=slots_in, out_offset=bass.IndirectOffsetOnAxis(
                            ap=slot[:, n, t:t + 1], axis=0), in_=g.v[:, t, :], in_offset=None).then_inc(sent, 16)

            @block.vector
            def _(dve):
                def low(i, n):
                    m = ORDER[n]
                    dve.wait_ge(h_hi, i * KI + n + 1 + START)
                    dve.tensor_tensor(hl[0:fw(m), m, :], h32[0:fw(m), n % 2, :],
                                      hh[0:fw(m), m, :].bitcast(F32), ALU.subtract).then_inc(h_lo, 1)

                def step(i, w=None, shared=None, split_up=True):
                    dve.wait_ge(xt_hi, i + 1 + START)
                    dve.tensor_tensor(xtl[:, :, :], ps_t[:, :, :], xth[:, :, :].bitcast(F32), ALU.subtract)\
                       .then_inc(xt_lo, 1)
                    if w is not None and split_up:
                        for k in range(KD):
                            dve.wait_ge(up_hi, w * KD + k + 1 + START)
                            dve.tensor_tensor(upl[:, k, :], up32[:, k, :], uph[:, k, :].bitcast(F32), ALU.subtract)\
                               .then_inc(up_lo, 1)
                    if shared is not None:
                        for j in range(0, TPC, 2):
                            x = g.x[:, ds(shared * TPC + j, 2), :]
                            dve.wait_ge(y_ps, shared * TPC + j + 2 + START)
                            dve.tensor_tensor(x, x, ps_y[:, j:j + 2, :], ALU.add).then_inc(y_read, 1)
                    for n, m in enumerate(ORDER):
                        dve.wait_ge(silu_ready, i * KI + n + 1 + START)
                        dve.wait_ge(h_lo, i * KI + n - 1 + START)
                        ups = ps_u[0:P, n % 2, :] if m < KI - 1 else ps_g[UP_AT:UP_AT + FLAST, n % 2, :]
                        dve.tensor_tensor(h32[0:fw(m), n % 2, :], silu[0:fw(m), n % 2, :], ups, ALU.mult)\
                           .then_inc(h_ready, 1)
                        if n:
                            low(i, n - 1)
                        if w is not None:
                            dve.wait_ge(dn_hi, w * KI + n + 1 + START)
                            dve.tensor_tensor(dnl[0:fw(m), m, :], dn32[0:fw(m), m, :],
                                              dnh[0:fw(m), m, :].bitcast(F32), ALU.subtract).then_inc(dn_lo, 1)
                    low(i, KI - 1)
                step(0, w=0, split_up=False)
                with dve.Fori(1, CHUNKS) as i:
                    step(i, shared=i - 1)
                step(CHUNKS, w=1, shared=CHUNKS - 1)
                with dve.Fori(CHUNKS + 1, RUNS) as i:
                    step(i, w=i - CHUNKS + 1)

            @block.scalar
            def _(act):
                def outputs(i):
                    act.wait_ge(y_out, (i - CHUNKS) * 16 + START)
                    for j in range(0, TPC, 2):
                        act.wait_ge(y_ps, i * TPC + j + 2 + START)
                        act.activation(y[:, j:j + 2, :], ps_y[:, j:j + 2, :], ACT.Copy).then_inc(y_read, 1)
                    act.wait_ge(y_read, (i + 1) * 2 + START)
                    act.dma_start(slots_out[ds((i - CHUNKS) * CT, CT), :].rearrange("(t p) n -> p t n", p=P), y[:, :, :])\
                       .then_inc(y_out, 16)

                def high(i, n):
                    m = ORDER[n]
                    act.wait_ge(h_ready, i * KI + n + 1 + START)
                    act.activation(hh[0:fw(m), m, :], h32[0:fw(m), n % 2, :], ACT.Copy).then_inc(h_hi, 1)

                def step(i, w=None, before=None, split_up=True):
                    act.wait_ge(xt_ps, i + 1 + START)
                    act.wait_ge(gu_ps, i * KI + START)
                    act.activation(xth[:, :, :], ps_t[:, :, :], ACT.Copy).then_inc(xt_hi, 1)
                    if w is not None and split_up:
                        act.wait_ge(up_in, (w + 1) * 16 + START)
                        for k in range(KD):
                            act.activation(uph[:, k, :], up32[:, k, :], ACT.Copy).then_inc(up_hi, 1)
                    if before is not None:
                        outputs(before)
                    for n, m in enumerate(ORDER):
                        act.wait_ge(gu_ps, i * KI + n + 1 + START)
                        act.wait_ge(h_ready, i * KI + n - 1 + START)
                        act.activation(silu[0:fw(m), n % 2, :], ps_g[0:fw(m), n % 2, :], ACT.Silu).then_inc(silu_ready, 1)
                        if n == 0:
                            act.wait_ge(y_ps, i * TPC + START)
                            if w is not None:
                                act.wait_ge(dn_in, (w + 1) * 32 + START)
                        if n:
                            high(i, n - 1)
                        if w is not None:
                            act.activation(dnh[0:fw(m), m, :], dn32[0:fw(m), m, :], ACT.Copy).then_inc(dn_hi, 1)
                    high(i, KI - 1)
                step(0, w=0, split_up=False)
                with act.Fori(1, CHUNKS) as i:
                    step(i)
                step(CHUNKS, w=1)
                with act.Fori(CHUNKS + 1, RUNS) as i:
                    step(i, w=i - CHUNKS + 1, before=i - 1)
                outputs(RUNS - 1)
                act.wait_ge(y_out, ROUTED * 16 + START)

            @block.tensor
            def _(pe):
                def turn(i):
                    pe.wait_ge(rows_in, (i + 1) * 16 + START)
                    pe.wait_ge(xt_lo, i + START)
                    for k in range(KD):
                        for j in range(TPC):
                            last = pe.transpose(ps_t[:, k, j * P:(j + 1) * P], rows[:, j, k * P:(k + 1) * P], ident)
                    last.then_inc(xt_ps, 1)

                def up(i, w=None):
                    pe.wait_ge(xt_lo, i + 1 + START)
                    if w is not None:
                        pe.wait_ge(up_lo, (w + 1) * KD + START)
                    for n, m in enumerate(ORDER):
                        pe.wait_ge(h_ready, i * KI + n - 1 + START)
                        if m < KI - 1:
                            parts = ((ps_g, m * P, P), (ps_u, FMAIN + m * P, P))
                        else:
                            parts = ((ps_g, 2 * FMAIN, UP_AT + FLAST),)
                        for ps, first, width in parts:
                            cols = slice(first, first + width)
                            for k in range(KD):
                                last = product3(pe, ps[0:width, n % 2, :], uph[:, k, cols], upl[:, k, cols],
                                                xth[:, k, :], xtl[:, k, :], k == 0, k == KD - 1)
                        last.then_inc(gu_ps, 1)

                def down(i, w=None):
                    for j in range(TPC):
                        pe.wait_ge(y_read, i * 2 - 1 + j // 2 + START)
                        t = slice(j * P, (j + 1) * P)
                        for n, m in enumerate(ORDER):
                            if j == 0:
                                pe.wait_ge(h_lo, i * KI + n + 1 + START)
                            if j == 0 and w is not None:
                                pe.wait_ge(dn_lo, w * KI + n + 1 + START)
                            last = product3(pe, ps_y[:, j, :], hh[0:fw(m), m, t], hl[0:fw(m), m, t],
                                            dnh[0:fw(m), m, :], dnl[0:fw(m), m, :], n == 0, n == KI - 1)
                        last.then_inc(y_ps, 1)
                turn(0)
                up(0, w=0)
                turn(1)
                down(0, w=0)
                up(1)
                with pe.Fori(2, CHUNKS) as i:
                    turn(i)
                    down(i - 1)
                    up(i)
                turn(CHUNKS)
                down(CHUNKS - 1)
                up(CHUNKS, w=1)
                with pe.Fori(CHUNKS + 1, RUNS) as i:
                    turn(i)
                    down(i - 1, w=i - CHUNKS)
                    up(i, w=i - CHUNKS + 1)
                down(RUNS - 1, w=ROUTED)


def moe_combine(nc, g, sem, slots_out, slot, weight):
    with ExitStack() as ctx:
        N = 4
        sb = lambda name, shape, dt=F32: ctx.enter_context(nc.sbuf_tensor(name, shape, dt))
        picked = sb("picked", [P, N, TOPK, D])
        picked_in = [sem.from_zero(f"cb_picked_in{u}") for u in range(N)]
        own = sem("cb_own")
        out_ready = sem("cb_ready")
        stored = sem("cb_stored")
        sem.start()
        with nc.Block() as block:
            @block.gpsimd
            def _(pool):
                for t in range(TILES):
                    if t >= N:
                        pool.wait_ge(out_ready, t - N + 1 + START)
                    for n in range(TOPK):
                        pool.indirect_dma_start(out=picked[:, t % N, n, :], out_offset=None, in_=slots_out,
                                                in_offset=bass.IndirectOffsetOnAxis(ap=slot[:, n, t:t + 1], axis=0))\
                            .then_inc(picked_in[t % N], 16)

            @block.vector
            def _(dve):
                st = Steps(dve, own)
                for t in range(TILES):
                    x = g.x[:, t, :]
                    dve.wait_ge(picked_in[t % N], 16 * TOPK * (t // N + 1))
                    for n in range(TOPK):
                        if n:
                            st.last()
                        last = dve.scalar_tensor_tensor(out=x, in0=picked[:, t % N, n, :], scalar=weight[:, n, t:t + 1],
                                                        in1=x, op0=ALU.mult, op1=ALU.add)
                        if n < TOPK - 1:
                            st.add(last)
                    last.then_inc(out_ready, 1)

            @block.scalar
            def _(act):
                for t in range(0, TILES, 2):
                    act.wait_ge(out_ready, t + 2 + START)
                    act.dma_start(g.out[t * P:(t + 2) * P, :].rearrange("(t p) n -> p t n", p=P), g.x[:, t:t + 2, :])\
                       .then_inc(stored, 16)
                act.wait_ge(stored, TILES // 2 * 16 + START)


class Shared:
    pass


def program(nc, names):
    g = Shared()
    g.constants = names["constants"]
    g.x_in = names["x_in"]
    g.qkv_w = names["qkv_w"]
    g.qk_bias = names["qk_bias"]
    g.v_bias = names["v_bias"]
    g.out_w = names["out_w"]
    g.out_b = names["out_b"]
    g.up_t = names["up_t"]
    g.down_t = names["down_t"]
    g.log_a_t = names["log_a_t"]
    g.c_t = names["c_t"]
    g.log_a_blocks = names["log_a_blocks"]
    g.c_blocks = names["c_blocks"]
    g.b_t = names["b_t"]
    g.d_vec = names["d_vec"]
    g.gate_t = names["gate_t"]
    g.w_up = names["w_up"]
    g.w_down = names["w_down"]
    g.out = names["out"]
    with ExitStack() as ctx:
        sb = lambda name, shape, dt=F32: ctx.enter_context(nc.sbuf_tensor(name, shape, dt))
        g.const = sb("const", [P, C_END])
        g.ident_bf = sb("ident_bf", [P, P], BF16)
        g.mask_bf = sb("mask_bf", [P, 3 * P], BF16)
        g.eps = sb("eps", [P, 1])
        g.started = ctx.enter_context(nc.semaphore("started"))
        g.passed = ctx.enter_context(nc.semaphore("passed"))
        g.x = sb("x", [P, TILES, D])
        g.v = sb("v", [P, TILES, D])
        g.q_k_hi = nc.dram_tensor("q_k_hi", (2 * D, TOK), F32, kind="Internal").ap()
        g.q_k_lo = nc.dram_tensor("q_k_lo", (2 * D, TOK), F32, kind="Internal").ap()
        phase_qkv(nc, ctx, g)
        with nc.sbuf_tensor("att", [P, TILES, D], F32) as att:
            g.att = att
            phase_attention(nc, ctx, g)
            phase_ffn(nc, ctx, g)
            phase_ssm(nc, ctx, g)
        phase_moe(nc, ctx, g)


def kernel(**inputs):
    import concourse.bacc as bacc
    from concourse.bass_utils import run_bass_kernel_spmd

    a = {k: np.asarray(v) for k, v in inputs.items()}
    lay = np.ascontiguousarray
    gate_up = np.concatenate([a["L1_ffn_experts_gate_up"], a["L1_ffn_shared_gate_up"][None]]).transpose(0, 2, 1)
    gate, up = gate_up[..., :FI], gate_up[..., FI:]
    down = np.concatenate([a["L1_ffn_experts_down"], a["L1_ffn_shared_down"][None]])
    log_a, c = a["L1_attn_log_A_diag"], a["L1_attn_C_w"]
    arrays = {
        "constants": host_constants(),
        "x_in": a["L0_attn_x"].reshape(TOK, D),
        "qkv_w": a["L0_attn_qkv_w"],
        "qk_bias": lay(a["L0_attn_qkv_b"][:2 * D].reshape(-1, P).T),
        "v_bias": lay(a["L0_attn_qkv_b"][2 * D:]),
        "out_w": a["L0_attn_out_w"],
        "out_b": a["L0_attn_out_b"],
        "up_t": lay(a["L0_ffn_w_up"].T),
        "down_t": lay(a["L0_ffn_w_down"].T),
        "log_a_t": lay(log_a.T),
        "c_t": lay(c.T),
        "log_a_blocks": lay(log_a.reshape(-1, P).T),
        "c_blocks": lay(c.reshape(-1, P).T),
        "b_t": lay(a["L1_attn_B_w"].T),
        "d_vec": a["L1_attn_D_vec"],
        "gate_t": lay(a["L1_ffn_gate_weight"].T),
        "w_up": np.concatenate([gate[..., :FMAIN], up[..., :FMAIN], gate[..., FMAIN:],
                                np.zeros((E + 1, D, UP_AT - FLAST), np.float32), up[..., FMAIN:]],
                               axis=2).reshape(-1, NUP),
        "w_down": lay(down.transpose(0, 2, 1)).reshape(-1, D),
    }
    nc = bacc.Bacc("TRN2", target_bir_lowering=False, num_devices=1)
    names = {n: nc.dram_tensor(f"in_{n}", v.shape, mybir.dt.from_np(v.dtype), kind="ExternalInput").ap()
             for n, v in arrays.items()}
    names["out"] = nc.dram_tensor("out", (TOK, D), F32, kind="ExternalOutput").ap()
    program(nc, names)
    result = run_bass_kernel_spmd(nc, [{f"in_{n}": v for n, v in arrays.items()}], core_ids=[0])
    return result.results[0]["out"].reshape(BATCH, SEQ, D)
```
